# Optimizing a Trainium2 kernel written in Bass

```python
import numpy as np
import jax
import jax.numpy as jnp

def _softmax(x, axis=-1):
    return jax.nn.softmax(x, axis=axis)

def _gelu(x):
    return jax.nn.gelu(x, approximate=True)

def _silu(x):
    return jax.nn.silu(x)

def _sigmoid(x):
    return jax.nn.sigmoid(x)

def _layernorm(x, axis=-1, eps=1e-05):
    m = jnp.mean(x, axis=axis, keepdims=True)
    v = jnp.var(x, axis=axis, keepdims=True)
    return (x - m) / jnp.sqrt(v + eps)

def _scatter_add(tgt, idx, src, axis=0):
    return tgt.at[idx].add(src)

def _segment_sum(src, seg, n):
    return jax.ops.segment_sum(src, seg, n)
kernel_name = 'mk_macaron_d4_jaxref_r8_8a83c4'

def setup_inputs(seed: int=0):
    np.random.seed(seed)
    _w = jnp.asarray

    def _L0_attn_setup():
        import math
        import jax, jax.numpy as jnp
        import numpy as np
        HEADS = 16
        REL_WINDOW = 128
        key = jax.random.key(seed)
        k1, k2, k3, k4, k5 = jax.random.split(key, 5)
        b, s, d = (2, 256, 128)
        hd = d // HEADS
        R = 2 * REL_WINDOW + 1
        return {'x': jax.random.normal(k1, (b, s, d), dtype=jnp.float32), 'Wqkv': jax.random.normal(k2, (3 * d, d), dtype=jnp.float32) * (1.0 / math.sqrt(d)), 'bqkv': jax.random.normal(k3, (3 * d,), dtype=jnp.float32) * 0.02, 'Wr': jax.random.normal(k4, (R, hd), dtype=jnp.float32) * (1.0 / math.sqrt(hd)), 'br': jax.random.normal(k5, (R,), dtype=jnp.float32) * 0.02}
    _L0_attn_in = _L0_attn_setup()

    def _L0_ffn_setup():
        import jax, jax.numpy as jnp
        import numpy as np
        HIDDEN_SIZE = 128
        NUM_EXPERTS = 8
        MOE_INTERMEDIATE_SIZE = 176
        NUM_EXPERTS_PER_TOK = 2
        SHARED_EXPERT_INTERMEDIATE_SIZE = 352
        B, T = (2, 128)
        W_SCALE = 0.02
        key = jax.random.key(seed)
        ks = jax.random.split(key, 8)
        H, E, I, SI = (HIDDEN_SIZE, NUM_EXPERTS, MOE_INTERMEDIATE_SIZE, SHARED_EXPERT_INTERMEDIATE_SIZE)
        return {'x': jax.random.normal(ks[0], (B, T, H), jnp.float32), 'gate_w': jax.random.normal(ks[1], (E, H), jnp.float32) * W_SCALE, 'experts_gate_up': jax.random.normal(ks[2], (E, 2 * I, H), jnp.float32) * W_SCALE, 'experts_down': jax.random.normal(ks[3], (E, H, I), jnp.float32) * W_SCALE, 'shared_gate_w': jax.random.normal(ks[4], (SI, H), jnp.float32) * W_SCALE, 'shared_up_w': jax.random.normal(ks[5], (SI, H), jnp.float32) * W_SCALE, 'shared_down_w': jax.random.normal(ks[6], (H, SI), jnp.float32) * W_SCALE, 'shared_expert_gate_w': jax.random.normal(ks[7], (1, H), jnp.float32) * W_SCALE}
    _L0_ffn_in = _L0_ffn_setup()

    def _L1_attn_setup():
        import jax, jax.numpy as jnp
        import numpy as np
        HEADS, D_MODEL, D_V = (16, 128, 64)
        D_K = D_MODEL // HEADS
        key = jax.random.key(seed)
        k1, k2, k3, k4, k5 = jax.random.split(key, 5)
        B, T = (2, 256)
        s = 1.0 / np.sqrt(D_MODEL)
        return {'x': jax.random.normal(k1, (B, T, D_MODEL), dtype=jnp.float32), 'Wq': jax.random.normal(k2, (D_MODEL, HEADS * D_K), dtype=jnp.float32) * s, 'Wk': jax.random.normal(k3, (D_MODEL, HEADS * D_K), dtype=jnp.float32) * s, 'Wv': jax.random.normal(k4, (D_MODEL, HEADS * D_V), dtype=jnp.float32) * s, 'Wo': jax.random.normal(k5, (HEADS * D_V, D_MODEL), dtype=jnp.float32) * (1.0 / np.sqrt(HEADS * D_V))}
    _L1_attn_in = _L1_attn_setup()

    def _L1_ffn_setup():
        import jax, jax.numpy as jnp
        import numpy as np
        H = 16
        E = 8
        EPS = 1e-05

        def _layernorm(x, g, b):
            mu = jnp.mean(x, axis=-1, keepdims=True)
            var = jnp.mean(jnp.square(x - mu), axis=-1, keepdims=True)
            return (x - mu) * jax.lax.rsqrt(var + EPS) * g + b
        key = jax.random.key(seed)
        T, B, C = (128, 8, 128)
        ks = jax.random.split(key, 12)
        s = 0.02
        return {'x': jax.random.normal(ks[0], (T, B, C), jnp.float32), 'in_proj_w': jax.random.normal(ks[1], (3 * C, C), jnp.float32) * s, 'in_proj_b': jnp.zeros((3 * C,), jnp.float32), 'out_w': jax.random.normal(ks[2], (C, C), jnp.float32) * s, 'out_b': jnp.zeros((C,), jnp.float32), 'ln1_g': jnp.ones((C,), jnp.float32), 'ln1_b': jnp.zeros((C,), jnp.float32), 'router_w': jax.random.normal(ks[3], (E, C), jnp.float32) * s, 'router_b': jnp.zeros((E,), jnp.float32), 'w1': jax.random.normal(ks[4], (E, C, C), jnp.float32) * s, 'b1': jnp.zeros((E, C), jnp.float32), 'w2': jax.random.normal(ks[5], (E, C, C), jnp.float32) * s, 'b2': jnp.zeros((E, C), jnp.float32), 'ln2_g': jnp.ones((C,), jnp.float32), 'ln2_b': jnp.zeros((C,), jnp.float32)}
    _L1_ffn_in = _L1_ffn_setup()

    def _L2_attn_setup():
        import jax, jax.numpy as jnp
        import numpy as np
        EPS = 1e-08

        def polar_orth(W):
            u, s, vt = jnp.linalg.svd(W.astype(jnp.float32), full_matrices=False)
            return u @ vt

        def rms(z):
            return z * jax.lax.rsqrt(jnp.mean(z * z, axis=-1, keepdims=True) + EPS)

        def _reference_tuple_inner(x, Wq, Wv, Wc, Wp1, Wp2, identity):
            B, T, D = x.shape
            P1 = polar_orth(Wp1).astype(x.dtype)
            P2 = polar_orth(Wp2).astype(x.dtype)
            q = jnp.einsum('btd,ed->bte', x, Wq)
            v = jnp.einsum('btd,ed->bte', x, Wv)

            def combine(left, right):
                z = left @ P1.T + right @ P2.T
                return rms(z)
            seq = jnp.concatenate([jnp.broadcast_to(identity.astype(x.dtype), (B, 1, D)), q], axis=1)
            h = jax.lax.associative_scan(combine, seq, axis=1)
            qs = h[:, 1:]
            Y = jnp.einsum('btd,ed->bte', qs * v, Wc)
            return (Y, qs)
        key = jax.random.key(seed)
        ks = jax.random.split(key, 7)
        B, T, D = (4, 512, 128)
        scale = 1.0 / np.sqrt(D)
        x = jax.random.normal(ks[0], (B, T, D), jnp.float32)
        Wq = jax.random.normal(ks[1], (D, D), jnp.float32) * scale
        Wv = jax.random.normal(ks[2], (D, D), jnp.float32) * scale
        Wc = jax.random.normal(ks[3], (D, D), jnp.float32) * scale
        Wp1 = jax.random.normal(ks[4], (D, D), jnp.float32) * scale
        Wp2 = jax.random.normal(ks[5], (D, D), jnp.float32) * scale
        identity = jax.random.uniform(ks[6], (D,), jnp.float32)
        return {'x': x, 'Wq': Wq, 'Wv': Wv, 'Wc': Wc, 'Wp1': Wp1, 'Wp2': Wp2, 'identity': identity}
    _L2_attn_in = _L2_attn_setup()

    def _L2_ffn_setup():
        import jax, jax.numpy as jnp
        import numpy as np
        B, T, D, E = (4, 128, 128, 8)
        HD = 4 * D
        key = jax.random.key(seed)
        k1, k2, k3, k4 = jax.random.split(key, 4)
        std = 0.5 * D ** (-0.5)
        bound = 3.0 ** 0.5 * std
        x = jax.random.normal(k1, (B, T, D), dtype=jnp.float32)
        router_w = jax.random.normal(k2, (E, D), dtype=jnp.float32) * 0.02
        expert_fc = jax.random.uniform(k3, (E, D, HD), dtype=jnp.float32, minval=-bound, maxval=bound)
        expert_proj = jax.random.normal(k4, (E, D, HD), dtype=jnp.float32) * 0.02
        return {'x': x, 'router_w': router_w, 'expert_fc': expert_fc, 'expert_proj': expert_proj}
    _L2_ffn_in = _L2_ffn_setup()

    def _L3_attn_setup():
        import jax, jax.numpy as jnp
        import numpy as np
        E = 128
        H = 16
        D = E // H

        def _mha(x, Wq, bq, Wk, bk, Wv, bv, Wo, bo):
            q = jnp.einsum('bse,hde->bhsd', x, Wq) + bq[None, :, None, :]
            k = jnp.einsum('bse,hde->bhsd', x, Wk) + bk[None, :, None, :]
            v = jnp.einsum('bse,hde->bhsd', x, Wv) + bv[None, :, None, :]
            scores = jnp.einsum('bhsd,bhtd->bhst', q, k) / jnp.sqrt(jnp.asarray(D, x.dtype))
            w = jax.nn.softmax(scores, axis=-1)
            o = jnp.einsum('bhst,bhtd->bhsd', w, v)
            B, _, S, _ = o.shape
            o = jnp.transpose(o, (0, 2, 1, 3)).reshape(B, S, H * D)
            return o @ Wo.T + bo
        key = jax.random.key(seed)
        ks = jax.random.split(key, 9)
        s = 0.02
        return {'hidden_state': jax.random.normal(ks[0], (4, 128, E), jnp.float32), 'Wq': jax.random.normal(ks[1], (H, D, E), jnp.float32) * s, 'bq': jax.random.normal(ks[2], (H, D), jnp.float32) * s, 'Wk': jax.random.normal(ks[3], (H, D, E), jnp.float32) * s, 'bk': jax.random.normal(ks[4], (H, D), jnp.float32) * s, 'Wv': jax.random.normal(ks[5], (H, D, E), jnp.float32) * s, 'bv': jax.random.normal(ks[6], (H, D), jnp.float32) * s, 'Wo': jax.random.normal(ks[7], (E, E), jnp.float32) * s, 'bo': jax.random.normal(ks[8], (E,), jnp.float32) * s}
    _L3_attn_in = _L3_attn_setup()

    def _L3_ffn_setup():
        import jax, jax.numpy as jnp
        import numpy as np
        B, S, D = (1, 256, 128)
        E, K, F = (64, 8, 96)
        SF = 96
        C = 64
        ROUTED_SCALE = 1.0

        def _moe_forward(x, router_w, w_gate, w_up, w_down, ws_gate_up, ws_down):
            T = x.shape[0]
            logits = x.astype(jnp.float32) @ router_w.T
            probs = jax.nn.softmax(logits, axis=-1)
            topk_w, topk_ids = jax.lax.top_k(probs, K)
            topk_w = topk_w / jnp.sum(topk_w, axis=-1, keepdims=True)
            topk_w = topk_w.astype(x.dtype)
            N = T * K
            flat_e = topk_ids.reshape(-1)
            flat_w = topk_w.reshape(-1)
            tok = jnp.arange(N) // K
            onehot = flat_e[:, None] == jnp.arange(E)[None, :]
            pos = jnp.cumsum(onehot, axis=0)[jnp.arange(N), flat_e] - 1
            valid = pos < C
            idx = jnp.where(valid, flat_e * C + pos, E * C)
            x_buf = jnp.zeros((E * C + 1, x.shape[1]), x.dtype).at[idx].set(x[tok])
            xb = x_buf[:E * C].reshape(E, C, -1)
            g = jnp.einsum('ecd,edf->ecf', xb, w_gate)
            u = jnp.einsum('ecd,edf->ecf', xb, w_up)
            h = jax.nn.silu(g) * u
            y = jnp.einsum('ecf,efd->ecd', h, w_down).reshape(E * C, -1)
            safe = jnp.where(valid, idx, 0)
            contrib = y[safe] * (flat_w * valid.astype(flat_w.dtype))[:, None]
            routed = jax.ops.segment_sum(contrib, tok, num_segments=T)
            routed = routed * ROUTED_SCALE
            gu = x @ ws_gate_up
            sg, su = (gu[:, :SF], gu[:, SF:])
            shared = jax.nn.silu(sg) * su @ ws_down
            return routed + shared
        key = jax.random.key(seed)
        ks = jax.random.split(key, 7)
        w = 0.02
        return {'hidden_states': jax.random.normal(ks[0], (B, S, D), jnp.float32), 'router_w': jax.random.normal(ks[1], (E, D), jnp.float32) * w, 'w_gate': jax.random.normal(ks[2], (E, D, F), jnp.float32) * w, 'w_up': jax.random.normal(ks[3], (E, D, F), jnp.float32) * w, 'w_down': jax.random.normal(ks[4], (E, F, D), jnp.float32) * w, 'ws_gate_up': jax.random.normal(ks[5], (D, 2 * SF), jnp.float32) * w, 'ws_down': jax.random.normal(ks[6], (SF, D), jnp.float32) * w}
    _L3_ffn_in = _L3_ffn_setup()
    _d = {'L0_attn_x': _L0_attn_in['x'], 'L0_attn_Wqkv': _L0_attn_in['Wqkv'], 'L0_attn_bqkv': _L0_attn_in['bqkv'], 'L0_attn_Wr': _L0_attn_in['Wr'], 'L0_attn_br': _L0_attn_in['br'], 'L0_ffn_gate_w': _L0_ffn_in['gate_w'], 'L0_ffn_experts_gate_up': _L0_ffn_in['experts_gate_up'], 'L0_ffn_experts_down': _L0_ffn_in['experts_down'], 'L0_ffn_shared_gate_w': _L0_ffn_in['shared_gate_w'], 'L0_ffn_shared_up_w': _L0_ffn_in['shared_up_w'], 'L0_ffn_shared_down_w': _L0_ffn_in['shared_down_w'], 'L0_ffn_shared_expert_gate_w': _L0_ffn_in['shared_expert_gate_w'], 'L1_attn_Wq': _L1_attn_in['Wq'], 'L1_attn_Wk': _L1_attn_in['Wk'], 'L1_attn_Wv': _L1_attn_in['Wv'], 'L1_attn_Wo': _L1_attn_in['Wo'], 'L1_ffn_in_proj_w': _L1_ffn_in['in_proj_w'], 'L1_ffn_in_proj_b': _L1_ffn_in['in_proj_b'], 'L1_ffn_out_w': _L1_ffn_in['out_w'], 'L1_ffn_out_b': _L1_ffn_in['out_b'], 'L1_ffn_ln1_g': _L1_ffn_in['ln1_g'], 'L1_ffn_ln1_b': _L1_ffn_in['ln1_b'], 'L1_ffn_router_w': _L1_ffn_in['router_w'], 'L1_ffn_router_b': _L1_ffn_in['router_b'], 'L1_ffn_w1': _L1_ffn_in['w1'], 'L1_ffn_b1': _L1_ffn_in['b1'], 'L1_ffn_w2': _L1_ffn_in['w2'], 'L1_ffn_b2': _L1_ffn_in['b2'], 'L1_ffn_ln2_g': _L1_ffn_in['ln2_g'], 'L1_ffn_ln2_b': _L1_ffn_in['ln2_b'], 'L2_attn_Wq': _L2_attn_in['Wq'], 'L2_attn_Wv': _L2_attn_in['Wv'], 'L2_attn_Wc': _L2_attn_in['Wc'], 'L2_attn_Wp1': _L2_attn_in['Wp1'], 'L2_attn_Wp2': _L2_attn_in['Wp2'], 'L2_attn_identity': _L2_attn_in['identity'], 'L2_ffn_router_w': _L2_ffn_in['router_w'], 'L2_ffn_expert_fc': _L2_ffn_in['expert_fc'], 'L2_ffn_expert_proj': _L2_ffn_in['expert_proj'], 'L3_attn_Wq': _L3_attn_in['Wq'], 'L3_attn_bq': _L3_attn_in['bq'], 'L3_attn_Wk': _L3_attn_in['Wk'], 'L3_attn_bk': _L3_attn_in['bk'], 'L3_attn_Wv': _L3_attn_in['Wv'], 'L3_attn_bv': _L3_attn_in['bv'], 'L3_attn_Wo': _L3_attn_in['Wo'], 'L3_attn_bo': _L3_attn_in['bo'], 'L3_ffn_router_w': _L3_ffn_in['router_w'], 'L3_ffn_w_gate': _L3_ffn_in['w_gate'], 'L3_ffn_w_up': _L3_ffn_in['w_up'], 'L3_ffn_w_down': _L3_ffn_in['w_down'], 'L3_ffn_ws_gate_up': _L3_ffn_in['ws_gate_up'], 'L3_ffn_ws_down': _L3_ffn_in['ws_down']}
    _x0 = _d['L0_attn_x']
    _d['L0_attn_x'] = jax.random.normal(jax.random.fold_in(jax.random.key(seed), 1), (8, 512, 128), dtype=_x0.dtype)
    del _x0
    return _d

def reference(L0_attn_x, L0_attn_Wqkv, L0_attn_bqkv, L0_attn_Wr, L0_attn_br, L0_ffn_gate_w, L0_ffn_experts_gate_up, L0_ffn_experts_down, L0_ffn_shared_gate_w, L0_ffn_shared_up_w, L0_ffn_shared_down_w, L0_ffn_shared_expert_gate_w, L1_attn_Wq, L1_attn_Wk, L1_attn_Wv, L1_attn_Wo, L1_ffn_in_proj_w, L1_ffn_in_proj_b, L1_ffn_out_w, L1_ffn_out_b, L1_ffn_ln1_g, L1_ffn_ln1_b, L1_ffn_router_w, L1_ffn_router_b, L1_ffn_w1, L1_ffn_b1, L1_ffn_w2, L1_ffn_b2, L1_ffn_ln2_g, L1_ffn_ln2_b, L2_attn_Wq, L2_attn_Wv, L2_attn_Wc, L2_attn_Wp1, L2_attn_Wp2, L2_attn_identity, L2_ffn_router_w, L2_ffn_expert_fc, L2_ffn_expert_proj, L3_attn_Wq, L3_attn_bq, L3_attn_Wk, L3_attn_bk, L3_attn_Wv, L3_attn_bv, L3_attn_Wo, L3_attn_bo, L3_ffn_router_w, L3_ffn_w_gate, L3_ffn_w_up, L3_ffn_w_down, L3_ffn_ws_gate_up, L3_ffn_ws_down):

    def _L0_attn_ref(x, Wqkv, bqkv, Wr, br):
        import math
        import jax, jax.numpy as jnp
        import numpy as np
        HEADS = 16
        REL_WINDOW = 128
        b, s, d = x.shape
        h = HEADS
        hd = d // h
        w = REL_WINDOW
        scale = math.sqrt(d / h)
        qkv = (x @ Wqkv.T + bqkv).reshape(b, s, h, 3 * hd)
        q, k, v = jnp.split(qkv, 3, axis=-1)
        q = q.transpose(0, 2, 1, 3)
        k = k.transpose(0, 2, 1, 3)
        v = v.transpose(0, 2, 1, 3)
        content = jnp.einsum('bhik,bhjk->bhij', q, k) / scale
        idx = jnp.arange(s)
        offsets = jnp.clip(idx[None, :] - idx[:, None], -w, w) + w
        rp = jnp.einsum('bhik,rk->bhir', q, Wr) + br
        pos = jnp.take_along_axis(rp, jnp.broadcast_to(offsets, (b, h, s, s)), axis=-1)
        attn = jax.nn.softmax(content + pos, axis=-1)
        out = jnp.einsum('bhij,bhjk->bhik', attn, v)
        return out.transpose(0, 2, 1, 3).reshape(b, s, d)

    def _L0_ffn_ref(x, gate_w, experts_gate_up, experts_down, shared_gate_w, shared_up_w, shared_down_w, shared_expert_gate_w):
        import jax, jax.numpy as jnp
        import numpy as np
        HIDDEN_SIZE = 128
        NUM_EXPERTS = 8
        MOE_INTERMEDIATE_SIZE = 176
        NUM_EXPERTS_PER_TOK = 2
        SHARED_EXPERT_INTERMEDIATE_SIZE = 352
        B, T = (2, 128)
        W_SCALE = 0.02
        Bx, Tx, H = x.shape
        E = gate_w.shape[0]
        I = experts_down.shape[2]
        x_flat = x.reshape(Bx * Tx, H)
        logits = x_flat @ gate_w.T
        scores = jax.nn.softmax(logits, axis=-1)
        _, topk_ids = jax.lax.top_k(scores, NUM_EXPERTS_PER_TOK)
        in_topk = jax.nn.one_hot(topk_ids, E, dtype=x.dtype).sum(axis=1)
        w = scores * in_topk
        gu = jnp.einsum('nh,eih->nei', x_flat, experts_gate_up)
        g, u = (gu[..., :I], gu[..., I:])
        h = jax.nn.silu(g) * u
        expert_out = jnp.einsum('nei,ehi->neh', h, experts_down)
        out = jnp.einsum('neh,ne->nh', expert_out, w)
        shared = jax.nn.silu(x_flat @ shared_gate_w.T) * (x_flat @ shared_up_w.T) @ shared_down_w.T
        shared_weight = jax.nn.sigmoid(x_flat @ shared_expert_gate_w.T)
        out = out + shared_weight * shared
        return out.reshape(Bx, Tx, H)

    def _L1_attn_ref(x, Wq, Wk, Wv, Wo):
        import jax, jax.numpy as jnp
        import numpy as np
        HEADS, D_MODEL, D_V = (16, 128, 64)
        D_K = D_MODEL // HEADS
        B, T, _ = x.shape
        scale = jnp.asarray(np.sqrt(D_K), x.dtype)
        q = (x @ Wq).reshape(B, T, HEADS, D_K).transpose(0, 2, 1, 3)
        k = (x @ Wk).reshape(B, T, HEADS, D_K).transpose(0, 2, 1, 3)
        v = (x @ Wv).reshape(B, T, HEADS, D_V).transpose(0, 2, 1, 3)
        scores = jnp.einsum('bhqd,bhkd->bhqk', q, k) / scale
        causal = jnp.triu(jnp.ones((T, T), dtype=bool), k=1)
        scores = jnp.where(causal, jnp.asarray(-jnp.inf, scores.dtype), scores)
        attn = jax.nn.softmax(scores, axis=-1)
        ctx = jnp.einsum('bhqk,bhkd->bhqd', attn, v)
        out = ctx.transpose(0, 2, 1, 3).reshape(B, T, HEADS * D_V)
        return out @ Wo

    def _L1_ffn_ref(x, in_proj_w, in_proj_b, out_w, out_b, ln1_g, ln1_b, router_w, router_b, w1, b1, w2, b2, ln2_g, ln2_b):
        import jax, jax.numpy as jnp
        import numpy as np
        H = 16
        E = 8
        EPS = 1e-05

        def _layernorm(x, g, b):
            mu = jnp.mean(x, axis=-1, keepdims=True)
            var = jnp.mean(jnp.square(x - mu), axis=-1, keepdims=True)
            return (x - mu) * jax.lax.rsqrt(var + EPS) * g + b
        T, B, C = x.shape
        D = C // H
        qkv = x @ in_proj_w.T + in_proj_b
        q, k, v = jnp.split(qkv, 3, axis=-1)
        q = q.reshape(T, B, H, D)
        k = k.reshape(T, B, H, D)
        v = v.reshape(T, B, H, D)
        scale = 1.0 / np.sqrt(D).astype(np.float32)
        scores = jnp.einsum('tbhd,sbhd->bhts', q, k) * scale
        attn = jax.nn.softmax(scores, axis=-1)
        ctx = jnp.einsum('bhts,sbhd->tbhd', attn, v).reshape(T, B, C)
        attn_out = ctx @ out_w.T + out_b
        h = _layernorm(x + attn_out, ln1_g, ln1_b)
        flat = h.reshape(-1, C)
        logits = flat @ router_w.T + router_b
        probs = jax.nn.softmax(logits, axis=-1)
        _, top_i = jax.lax.top_k(probs, 2)
        assign = jnp.max(top_i, axis=-1)
        out = jnp.zeros_like(flat)
        for e in range(E):
            he = jax.nn.gelu(flat @ w1[e].T + b1[e], approximate=False)
            oe = he @ w2[e].T + b2[e]
            out = jnp.where((assign == e)[:, None], oe, out)
        moe_out = out.reshape(T, B, C)
        return _layernorm(h + moe_out, ln2_g, ln2_b)

    def _L2_attn_ref(x, Wq, Wv, Wc, Wp1, Wp2, identity):
        import jax, jax.numpy as jnp
        import numpy as np
        EPS = 1e-08

        def polar_orth(W):
            u, s, vt = jnp.linalg.svd(W.astype(jnp.float32), full_matrices=False)
            return u @ vt

        def rms(z):
            return z * jax.lax.rsqrt(jnp.mean(z * z, axis=-1, keepdims=True) + EPS)

        def _reference_tuple_inner(x, Wq, Wv, Wc, Wp1, Wp2, identity):
            B, T, D = x.shape
            P1 = polar_orth(Wp1).astype(x.dtype)
            P2 = polar_orth(Wp2).astype(x.dtype)
            q = jnp.einsum('btd,ed->bte', x, Wq)
            v = jnp.einsum('btd,ed->bte', x, Wv)

            def combine(left, right):
                z = left @ P1.T + right @ P2.T
                return rms(z)
            seq = jnp.concatenate([jnp.broadcast_to(identity.astype(x.dtype), (B, 1, D)), q], axis=1)
            h = jax.lax.associative_scan(combine, seq, axis=1)
            qs = h[:, 1:]
            Y = jnp.einsum('btd,ed->bte', qs * v, Wc)
            return (Y, qs)
        return _reference_tuple_inner(x, Wq, Wv, Wc, Wp1, Wp2, identity)[0]

    def _L2_ffn_ref(x, router_w, expert_fc, expert_proj):
        import jax, jax.numpy as jnp
        import numpy as np
        B, T, D, E = (4, 128, 128, 8)
        HD = 4 * D
        logits = jnp.einsum('btd,ed->bte', x, router_w)
        probs = jax.nn.softmax(logits, axis=-1)
        expert_ids = jnp.argmax(probs, axis=-1)
        mask = jax.nn.one_hot(expert_ids, E, dtype=x.dtype)
        h = jnp.einsum('btd,edh->ebth', x, expert_fc)
        h = jnp.square(jax.nn.relu(h))
        out_e = jnp.einsum('ebth,edh->ebtd', h, expert_proj)
        output = jnp.einsum('ebtd,bte->btd', out_e, mask)
        return output

    def _L3_attn_ref(hidden_state, Wq, bq, Wk, bk, Wv, bv, Wo, bo):
        import jax, jax.numpy as jnp
        import numpy as np
        E = 128
        H = 16
        D = E // H

        def _mha(x, Wq, bq, Wk, bk, Wv, bv, Wo, bo):
            q = jnp.einsum('bse,hde->bhsd', x, Wq) + bq[None, :, None, :]
            k = jnp.einsum('bse,hde->bhsd', x, Wk) + bk[None, :, None, :]
            v = jnp.einsum('bse,hde->bhsd', x, Wv) + bv[None, :, None, :]
            scores = jnp.einsum('bhsd,bhtd->bhst', q, k) / jnp.sqrt(jnp.asarray(D, x.dtype))
            w = jax.nn.softmax(scores, axis=-1)
            o = jnp.einsum('bhst,bhtd->bhsd', w, v)
            B, _, S, _ = o.shape
            o = jnp.transpose(o, (0, 2, 1, 3)).reshape(B, S, H * D)
            return o @ Wo.T + bo
        return _mha(hidden_state, Wq, bq, Wk, bk, Wv, bv, Wo, bo)

    def _L3_ffn_ref(hidden_states, router_w, w_gate, w_up, w_down, ws_gate_up, ws_down):
        import jax, jax.numpy as jnp
        import numpy as np
        B, S, D = (1, 256, 128)
        E, K, F = (64, 8, 96)
        SF = 96
        C = 64
        ROUTED_SCALE = 1.0

        def _moe_forward(x, router_w, w_gate, w_up, w_down, ws_gate_up, ws_down):
            T = x.shape[0]
            logits = x.astype(jnp.float32) @ router_w.T
            probs = jax.nn.softmax(logits, axis=-1)
            topk_w, topk_ids = jax.lax.top_k(probs, K)
            topk_w = topk_w / jnp.sum(topk_w, axis=-1, keepdims=True)
            topk_w = topk_w.astype(x.dtype)
            N = T * K
            flat_e = topk_ids.reshape(-1)
            flat_w = topk_w.reshape(-1)
            tok = jnp.arange(N) // K
            onehot = flat_e[:, None] == jnp.arange(E)[None, :]
            pos = jnp.cumsum(onehot, axis=0)[jnp.arange(N), flat_e] - 1
            valid = pos < C
            idx = jnp.where(valid, flat_e * C + pos, E * C)
            x_buf = jnp.zeros((E * C + 1, x.shape[1]), x.dtype).at[idx].set(x[tok])
            xb = x_buf[:E * C].reshape(E, C, -1)
            g = jnp.einsum('ecd,edf->ecf', xb, w_gate)
            u = jnp.einsum('ecd,edf->ecf', xb, w_up)
            h = jax.nn.silu(g) * u
            y = jnp.einsum('ecf,efd->ecd', h, w_down).reshape(E * C, -1)
            safe = jnp.where(valid, idx, 0)
            contrib = y[safe] * (flat_w * valid.astype(flat_w.dtype))[:, None]
            routed = jax.ops.segment_sum(contrib, tok, num_segments=T)
            routed = routed * ROUTED_SCALE
            gu = x @ ws_gate_up
            sg, su = (gu[:, :SF], gu[:, SF:])
            shared = jax.nn.silu(sg) * su @ ws_down
            return routed + shared
        b, s, d = hidden_states.shape
        x = hidden_states.reshape(-1, d)
        out = _moe_forward(x, router_w, w_gate, w_up, w_down, ws_gate_up, ws_down)
        return out.reshape(b, s, d)
    x = L0_attn_x
    x = x + 0.5 * _L0_ffn_ref(_layernorm(x, axis=-1), L0_ffn_gate_w, L0_ffn_experts_gate_up, L0_ffn_experts_down, L0_ffn_shared_gate_w, L0_ffn_shared_up_w, L0_ffn_shared_down_w, L0_ffn_shared_expert_gate_w)
    x = x + _L0_attn_ref(_layernorm(x, axis=-1), L0_attn_Wqkv, L0_attn_bqkv, L0_attn_Wr, L0_attn_br)
    x = x + 0.5 * _L0_ffn_ref(_layernorm(x, axis=-1), L0_ffn_gate_w, L0_ffn_experts_gate_up, L0_ffn_experts_down, L0_ffn_shared_gate_w, L0_ffn_shared_up_w, L0_ffn_shared_down_w, L0_ffn_shared_expert_gate_w)
    x = x + 0.5 * _L1_ffn_ref(_layernorm(x, axis=-1), L1_ffn_in_proj_w, L1_ffn_in_proj_b, L1_ffn_out_w, L1_ffn_out_b, L1_ffn_ln1_g, L1_ffn_ln1_b, L1_ffn_router_w, L1_ffn_router_b, L1_ffn_w1, L1_ffn_b1, L1_ffn_w2, L1_ffn_b2, L1_ffn_ln2_g, L1_ffn_ln2_b)
    x = x + _L1_attn_ref(_layernorm(x, axis=-1), L1_attn_Wq, L1_attn_Wk, L1_attn_Wv, L1_attn_Wo)
    x = x + 0.5 * _L1_ffn_ref(_layernorm(x, axis=-1), L1_ffn_in_proj_w, L1_ffn_in_proj_b, L1_ffn_out_w, L1_ffn_out_b, L1_ffn_ln1_g, L1_ffn_ln1_b, L1_ffn_router_w, L1_ffn_router_b, L1_ffn_w1, L1_ffn_b1, L1_ffn_w2, L1_ffn_b2, L1_ffn_ln2_g, L1_ffn_ln2_b)
    x = x + 0.5 * _L2_ffn_ref(_layernorm(x, axis=-1), L2_ffn_router_w, L2_ffn_expert_fc, L2_ffn_expert_proj)
    x = x + _L2_attn_ref(_layernorm(x, axis=-1), L2_attn_Wq, L2_attn_Wv, L2_attn_Wc, L2_attn_Wp1, L2_attn_Wp2, L2_attn_identity)
    x = x + 0.5 * _L2_ffn_ref(_layernorm(x, axis=-1), L2_ffn_router_w, L2_ffn_expert_fc, L2_ffn_expert_proj)
    x = x + 0.5 * _L3_ffn_ref(_layernorm(x, axis=-1), L3_ffn_router_w, L3_ffn_w_gate, L3_ffn_w_up, L3_ffn_w_down, L3_ffn_ws_gate_up, L3_ffn_ws_down)
    x = x + _L3_attn_ref(_layernorm(x, axis=-1), L3_attn_Wq, L3_attn_bq, L3_attn_Wk, L3_attn_bk, L3_attn_Wv, L3_attn_bv, L3_attn_Wo, L3_attn_bo)
    x = x + 0.5 * _L3_ffn_ref(_layernorm(x, axis=-1), L3_ffn_router_w, L3_ffn_w_gate, L3_ffn_w_up, L3_ffn_w_down, L3_ffn_ws_gate_up, L3_ffn_ws_down)
    return x

_drawn_inputs = setup_inputs


def setup_inputs(seed=0):
    import zlib

    import numpy as np

    out = dict(_drawn_inputs(seed))
    spreads = {'L1_ffn_in_proj_b': (0.0, 0.342),
     'L1_ffn_out_b': (0.0, 0.1),
     'L1_ffn_ln1_g': (1.0, 0.2),
     'L1_ffn_ln1_b': (0.0, 0.1),
     'L1_ffn_router_b': (0.0, 0.1),
     'L1_ffn_b1': (0.0, 0.8),
     'L1_ffn_b2': (0.0, 0.1),
     'L1_ffn_ln2_g': (1.0, 0.2),
     'L1_ffn_ln2_b': (0.0, 0.1)}
    factors = {'L0_attn_br': 8.0,
     'L0_ffn_gate_w': 8.0,
     'L0_ffn_experts_gate_up': 8.0,
     'L0_ffn_experts_down': 8.0,
     'L0_ffn_shared_gate_w': 7.347,
     'L0_ffn_shared_up_w': 7.817,
     'L0_ffn_shared_down_w': 7.721,
     'L0_ffn_shared_expert_gate_w': 8.0,
     'L1_ffn_in_proj_w': 3.747,
     'L1_ffn_w1': 3.173,
     'L1_ffn_w2': 2.868,
     'L2_attn_identity': 4.761,
     'L3_attn_Wq': 8.0,
     'L3_attn_bq': 8.0,
     'L3_attn_Wk': 8.0,
     'L3_attn_bk': 8.0,
     'L3_attn_Wv': 8.0,
     'L3_attn_bv': 8.0,
     'L3_attn_Wo': 8.0,
     'L3_attn_bo': 6.165,
     'L3_ffn_router_w': 8.0,
     'L3_ffn_w_gate': 8.0,
     'L3_ffn_w_up': 8.0,
     'L3_ffn_w_down': 8.0,
     'L3_ffn_ws_gate_up': 8.0,
     'L3_ffn_ws_down': 8.0}
    for name, (base, spread) in spreads.items():
        noise = np.random.default_rng([zlib.crc32(name.encode()), seed]).standard_normal(out[name].shape)
        drawn = base * np.exp(spread * noise) if base else spread * noise
        out[name] = jnp.asarray(drawn.astype(out[name].dtype))
    for name, factor in factors.items():
        out[name] = (out[name] * factor).astype(out[name].dtype)
    return out
```

```python
import numpy as np
import concourse.bass as bass
from concourse import mybir
from contextlib import ExitStack

F32 = mybir.dt.float32
BF16 = mybir.dt.bfloat16
U32 = mybir.dt.uint32
I32 = mybir.dt.int32
ALU = mybir.AluOpType
ACT = mybir.ActivationFunctionType
AX = mybir.AxisListType

NB, T, D = 8, 512, 128
N = NB * T
TILES = T // 128
HEADS, HD = 16, 8
BIG = 1e30


class PoolDmaCount:
    def __init__(self, sem, base):
        self.sem, self.base = sem, base

    def wait(self, eng, n):
        eng.wait_ge(self.sem, self.base + n)


class Stage:

    count = 0

    def __init__(self, nc, name):
        Stage.count += 1
        self.taken = 0
        self.nc, self.name, self.ctx, self.sems = nc, f"{name}_{Stage.count}", ExitStack(), []

    def __enter__(self):
        self.ctx.__enter__()
        return self

    def sb(self, name, shape, dt=F32):
        return self.ctx.enter_context(self.nc.sbuf_tensor(f"{self.name}_{name}", shape, dt))

    def ps(self, name, shape=(128, 512), dt=F32):
        return self.ctx.enter_context(self.nc.psum_tensor(f"{self.name}_{name}", list(shape), dt))

    def sem(self, name):
        s = self.ctx.enter_context(self.nc.semaphore(f"{self.name}_{name}"))
        self.sems.append(s)
        return s

    def pool_dma_sem(self, total):
        c = PoolDmaCount(Stage.pool_dma[self.taken], Stage.pool_dma_count[self.taken])
        Stage.pool_dma_count[self.taken] += total
        self.taken += 1
        return c

    def __exit__(self, *a):
        if a[0] is not None:
            return self.ctx.__exit__(*a)
        if not self.sems:
            self.nc.all_engine_barrier()
            return self.ctx.__exit__(*a)
        ids = sorted(s.num for s in self.sems)
        cleared = range(ids[0], ids[-1] + 1)
        assert not any(s in cleared for s in self.nc.barrier_sems)
        self.nc.all_engine_barrier(sems_to_clear=cleared)
        return self.ctx.__exit__(*a)


def token_rows(dram, permuted):
    if permuted:
        return dram.rearrange("(t g n) c -> g t n c", t=NB, n=128 // NB)
    return dram.rearrange("(g p) c -> g p c", p=128)


def load_tiles(eng, dst, dram, b, permuted, sem):
    v = token_rows(dram, permuted)
    for k in range(TILES):
        src = v[bass.ds(b * TILES + k, 1)]
        if permuted:
            eng.dma_start(dst[:, k, :], src.rearrange("o t n c -> (o t) n c")).then_inc(sem, 16)
        else:
            eng.dma_start(dst[:, k, :], src.rearrange("o p c -> (o p) c")).then_inc(sem, 16)


def store_tiles(eng, dram, src, b, permuted, sem):
    v = token_rows(dram, permuted)
    for k in range(TILES):
        dst = v[bass.ds(b * TILES + k, 1)]
        if permuted:
            eng.dma_start(dst.rearrange("o t n c -> (o t) n c"), src[:, k, :]).then_inc(sem, 16)
        else:
            eng.dma_start(dst.rearrange("o p c -> (o p) c"), src[:, k, :]).then_inc(sem, 16)


def bc(ap, n):
    return ap.unsqueeze(2).to_broadcast([ap.shape[0], ap.shape[1], n])


def prep(nc, name, W, src, xnt, xn=None, permuted=False, affine=None, route=None, eps=1e-5):
    with Stage(nc, name) as st:
        xt = st.sb("xt", [128, 2, TILES, D])
        stats = st.sb("stats", [128, 2, TILES, 6])
        mv = st.sb("mv", [128, 2, TILES, 2])
        vare = st.sb("vare", [128, 2, TILES])
        rstd = st.sb("rstd", [128, 2, TILES])
        half = st.sb("half", [128, TILES])
        y = st.sb("y", [128, 2, TILES, D])
        yT = st.sb("yT", [128, 2, T])
        ident = st.sb("ident", [128, 128])
        psY = [st.ps(f"psY{i}") for i in range(2)]
        if affine:
            gb = st.sb("gb", [128, 2, D])
            z = st.sb("z", [128, 2, TILES, D])
        kind = route and route["kind"]
        if route:
            E, R, G = route["experts"], route["rows"], route["parts"]
            wr = st.sb("wr", [128, R])
            rb = st.sb("rb", [128, R])
            iota = st.sb("iota", [128, TILES, E])
            psL = [st.ps(f"psL{i}") for i in range(2)]
            psG = [st.ps(f"psG{i}") for i in range(2)]
            lg = st.sb("lg", [128, TILES, R])
            mx = st.sb("mx", [128, TILES])
            ex = st.sb("ex", [128, TILES, E])
            sm = st.sb("sm", [128, TILES])
            ri = st.sb("ri", [128, TILES])
            pr = st.sb("pr", [128, TILES, E])
            v8 = st.sb("v8", [128, TILES, 8])
            i8 = st.sb("i8", [128, TILES, 8], U32)
            fi = st.sb("fi", [128, TILES, 2])
            pick = st.sb("pick", [128, TILES])
            m0 = st.sb("m0", [128, TILES, E])
            m1 = st.sb("m1", [128, TILES, E])
            gt = st.sb("gt", [128, TILES, R])
            sg = st.sb("sg", [128, TILES, 1])
            hi = st.sb("hi", [128, TILES, R], BF16)
            res = st.sb("res", [128, TILES, R])
            parts = st.sb("parts", [128, 2, TILES, G * R])
            gT = st.sb("gT", [G * R, 2, T])
        const_in = st.sem("const_in")
        x_in = [st.sem(f"x_in{s}") for s in range(2)]
        x_free = st.sem("x_free")
        y_done = st.sem("y_done")
        y_stored = [st.pool_dma_sem(64 * (NB // 2) if xn is not None else 0) for s in range(2)]
        yT_ready = st.sem("yT_ready")
        yT_copied = st.sem("yT_copied")
        yT_stored = [st.sem(f"yT_stored{s}") for s in range(2)]
        var_done = st.sem("var_done")
        rstd_done = st.sem("rstd_done")
        dve = st.sem("dve")
        paced = st.sem("paced")
        half_set = st.sem("half_set")
        logits_ready = st.sem("logits_ready")
        logits_free = st.sem("logits_free")
        shifted = st.sem("shifted")
        exps_done = st.sem("exps_done")
        gates_done = st.sem("gates_done")
        gates_turned = st.sem("gates_turned")
        gates_copied = st.sem("gates_copied")
        gates_stored = [st.sem(f"gates_stored{s}") for s in range(2)]
        NCONST = 1 + (2 if affine else 0) + (3 if route else 0)

        with nc.Block() as block:
            @block.sync
            def _(sp):
                sp.dma_start(ident[:], W["ident"]).then_inc(const_in, 16)
                if affine:
                    for j in range(2):
                        sp.dma_start(gb[:, j, :], W[affine[j]].to_broadcast([128, D])).then_inc(const_in, 16)
                if route:
                    sp.dma_start(wr[:], W[route["w"]]).then_inc(const_in, 16)
                    sp.dma_start(rb[:], W[route["b"]].to_broadcast([128, R])).then_inc(const_in, 16)
                    sp.dma_start(iota[:], W["iota8"][:, 0:E].unsqueeze(1).to_broadcast([128, TILES, E])).then_inc(const_in, 16)
                with sp.Fori(0, NB // 2) as i:
                    for s in range(2):
                        b = i * 2 + s
                        sp.wait_ge(x_free, b + 1)
                        load_tiles(sp, xt[:, s], src, b, permuted, x_in[s])

            @block.gpsimd
            def _(pool):
                pool.memset(half[:], -0.5).then_inc(half_set, 1)
                pool.wait_ge(half_set, 1)
                with pool.Fori(0, NB // 2) as i:
                    for s in range(2):
                        b = i * 2 + s
                        pool.wait_ge(var_done, b + 1)
                        pool.tensor_tensor(rstd[:, s], vare[:, s], half[:], ALU.pow).then_inc(rstd_done, 1)
                        if xn is not None:
                            pool.wait_ge(y_done, b + 1)
                            if affine:
                                store_tiles(pool, xn, z[:, s], b, False, y_stored[s].sem)
                            else:
                                store_tiles(pool, xn, y[:, s], b, False, y_stored[s].sem)
                if xn is not None:
                    for s in range(2):
                        y_stored[s].wait(pool, NB // 2 * 64)

            @block.vector
            def _(v):
                v.sem_inc(x_free, 2)
                v.wait_ge(const_in, 16 * NCONST)
                with v.Fori(0, NB // 2) as i:
                    STEPS = [0]
                    PER = 2 * (3 + (2 if affine else 0)) + (2 * route["steps"] if route else 0)

                    def link(ins):
                        STEPS[0] += 1
                        ins.then_inc(dve, 1)
                        v.wait_ge(dve, i * PER + STEPS[0])
                        v.sem_inc(paced, 1)

                    for s in range(2):
                        b = i * 2 + s
                        v.wait_ge(x_in[s], i * 64 + 64)
                        for k in range(TILES):
                            ins = v.bn_stats(stats[:, s, k], xt[:, s, k])
                        link(ins)
                        for k in range(TILES):
                            ins = v.bn_aggr(mv[:, s, k], stats[:, s, k])
                        link(ins)
                        v.tensor_scalar(vare[:, s], mv[:, s, :, 1], eps, None, ALU.add).then_inc(var_done, 1)
                        v.wait_ge(rstd_done, b + 1)
                        if not affine:
                            v.wait_ge(yT_ready, b + 1)
                            if xn is not None:
                                y_stored[s].wait(v, i * 64)
                        for k in range(TILES):
                            ins = v.tensor_scalar(y[:, s, k], xt[:, s, k], mv[:, s, k, 0:1], rstd[:, s, k:k + 1],
                                                  ALU.subtract, ALU.mult)
                        link(ins)
                        v.sem_inc(x_free, 1)
                        if affine:
                            g = gb[:, 0:1, :].to_broadcast([128, TILES, D])
                            o = gb[:, 1:2, :].to_broadcast([128, TILES, D])
                            link(v.tensor_tensor(y[:, s], y[:, s], g, ALU.mult))
                            v.wait_ge(yT_ready, b + 1)
                            if xn is not None:
                                y_stored[s].wait(v, i * 64)
                            link(v.tensor_tensor(z[:, s], y[:, s], o, ALU.add))
                        v.sem_inc(y_done, 1)
                        if not route:
                            continue
                        v.wait_ge(logits_ready, b + 1)
                        L = psL[s][:, 0:TILES * R].rearrange("p (k e) -> p k e", k=TILES)
                        link(v.tensor_tensor(lg[:], L, rb[:].unsqueeze(1).to_broadcast([128, TILES, R]), ALU.add))
                        v.sem_inc(logits_free, 1)
                        link(v.tensor_reduce(mx[:], lg[:, :, 0:E], AX.X, ALU.max))
                        link(v.tensor_tensor(lg[:, :, 0:E], lg[:, :, 0:E], bc(mx[:], E), ALU.subtract))
                        v.sem_inc(shifted, 1)
                        v.wait_ge(exps_done, b + 1)
                        link(v.tensor_reduce(sm[:], ex[:], AX.X, ALU.add))
                        link(v.reciprocal(ri[:], sm[:]))
                        link(v.tensor_tensor(pr[:], ex[:], bc(ri[:], E), ALU.mult))
                        for k in range(TILES):
                            ins = v.max(v8[:, k], pr[:, k])
                        link(ins)
                        for k in range(TILES):
                            ins = v.max_index(i8[:, k], v8[:, k], pr[:, k])
                        link(ins)
                        link(v.tensor_copy(fi[:], i8[:, :, 0:2]))
                        if kind == "top2":
                            v.tensor_tensor(m0[:], iota[:], bc(fi[:, :, 0], E), ALU.is_equal)
                            link(v.tensor_tensor(m1[:], iota[:], bc(fi[:, :, 1], E), ALU.is_equal))
                            link(v.tensor_tensor(m0[:], m0[:], m1[:], ALU.add))
                            v.tensor_tensor(gt[:, :, 0:E], m0[:], pr[:], ALU.mult)
                            link(v.tensor_scalar(sg[:], sg[:], 1.0, None, ALU.add))
                            link(v.reciprocal(gt[:, :, E:R], sg[:]))
                        elif kind == "top1":
                            link(v.tensor_tensor(gt[:], iota[:], bc(fi[:, :, 0], E), ALU.is_equal))
                        else:
                            link(v.tensor_reduce(pick[:], fi[:], AX.X, ALU.max))
                            link(v.tensor_tensor(gt[:], iota[:], bc(pick[:], E), ALU.is_equal))
                        v.wait_ge(gates_turned, b + 1)
                        if G == 1:
                            link(v.tensor_copy(parts[:, s], gt[:]))
                        else:
                            link(v.tensor_copy(hi[:], gt[:]))
                            v.tensor_copy(parts[:, s, :, 0:R], hi[:])
                            link(v.tensor_tensor(res[:], gt[:], hi[:], ALU.subtract))
                            link(v.tensor_copy(hi[:], res[:]))
                            v.tensor_copy(parts[:, s, :, R:2 * R], hi[:])
                            link(v.tensor_tensor(parts[:, s, :, 2 * R:3 * R], res[:], hi[:], ALU.subtract))
                        v.sem_inc(gates_done, 1)
                assert STEPS[0] == PER, (STEPS[0], PER)

            @block.tensor
            def _(pe):
                pe.sem_inc(yT_ready, 2)
                if route:
                    pe.sem_inc(gates_turned, 2)
                pe.wait_ge(const_in, 16 * NCONST)
                with pe.Fori(0, NB // 2) as i:
                    for s in range(2):
                        b = i * 2 + s
                        out = z if affine else y
                        pe.wait_ge(y_done, b + 1)
                        pe.wait_ge(yT_copied, b + 1)
                        for k in range(TILES):
                            ins = pe.transpose(psY[s][:, k * 128:(k + 1) * 128], out[:, s, k], ident[:])
                        ins.then_inc(yT_ready, 1)
                        if route:
                            pe.wait_ge(yT_copied, b + 3)
                            pe.wait_ge(logits_free, b + 1)
                            for k in range(TILES):
                                ins = pe.matmul(psL[s][:, k * R:(k + 1) * R], yT[:, s, k * 128:(k + 1) * 128], wr[:],
                                                start=True, stop=True)
                            ins.then_inc(logits_ready, 1)
                            pe.wait_ge(gates_done, b + 1)
                            pe.wait_ge(gates_copied, b + 1)
                            for k in range(TILES):
                                ins = pe.transpose(psG[s][0:G * R, k * 128:(k + 1) * 128], parts[:, s, k], ident[:])
                            ins.then_inc(gates_turned, 1)

            @block.scalar
            def _(a):
                a.sem_inc(yT_copied, 2)
                for s in range(2):
                    a.sem_inc(yT_stored[s], 16)
                    a.sem_inc(gates_stored[s], 16)
                if route:
                    a.sem_inc(logits_free, 2)
                    a.sem_inc(gates_copied, 2)
                with a.Fori(0, NB // 2) as i:
                    for s in range(2):
                        b = i * 2 + s
                        a.wait_ge(yT_ready, b + 3)
                        a.wait_ge(yT_stored[s], i * 16 + 16)
                        if route:
                            a.wait_ge(logits_free, b + 1)
                        a.copy(yT[:, s], psY[s][:]).then_inc(yT_copied, 1)
                        a.wait_ge(yT_copied, b + 3)
                        a.dma_start(xnt[:, bass.ds(b * T, T)], yT[:, s]).then_inc(yT_stored[s], 16)
                        if route:
                            a.wait_ge(shifted, b + 1)
                            ins = a.activation(ex[:], lg[:, :, 0:E], ACT.Exp)
                            if R > E:
                                ins = a.activation(sg[:], lg[:, :, E:R], ACT.Exp, scale=-1.0)
                            ins.then_inc(exps_done, 1)
                            a.wait_ge(gates_turned, b + 3)
                            a.wait_ge(gates_stored[s], i * 16 + 16)
                            a.copy(gT[:, s], psG[s][0:G * R, :]).then_inc(gates_copied, 1)
                            a.wait_ge(gates_copied, b + 3)
                            a.dma_start(route["table"][0:G * R, bass.ds(b * T, T)], gT[:, s]).then_inc(gates_stored[s], 16)
                for s in range(2):
                    a.wait_ge(yT_stored[s], 16 * (NB // 2) + 16)
                    if route:
                        a.wait_ge(gates_stored[s], 16 * (NB // 2) + 16)


ROUTES = {
    "L0": dict(kind="top2", experts=8, rows=9, parts=3, steps=9 + 4 + 4),
    "L1": dict(kind="top2max", experts=8, rows=8, parts=1, steps=9 + 2 + 1),
    "L2": dict(kind="top1", experts=8, rows=8, parts=1, steps=9 + 1 + 1),
}


def moe(nc, name, W, kind, X, xnt, table, hn=None, permuted=False):
    F = {"L0": 1760, "L1": 1024, "L2": 4096}[kind]
    C = -(-F // 128)
    rows = [min(128, F - 128 * c) for c in range(C)]
    GR = 27 if kind == "L0" else 8
    NS = 8 if kind == "L2" else C
    with Stage(nc, name) as st:
        w1 = st.sb("w1", [128, F])
        w2 = st.sb("w2", [128, C, D])
        sel32 = st.sb("sel32", [GR, NS * 128])
        sel = st.sb("sel", [GR, NS * 128], BF16)
        xT = st.sb("xT", [128, 2, T])
        xt = st.sb("xt", [128, 2, TILES, D])
        xo = st.sb("xo", [128, 2, TILES, D])
        g32 = st.sb("g32", [GR, 2, T])
        g16 = st.sb("g16", [GR, 2, T], BF16)
        a1 = st.sb("a1", [128, 2, T])
        tb = st.sb("tb", [128, 2, T])
        h = st.sb("h", [128, 2, T])
        psG = [st.ps(f"psG{i}") for i in range(2)]
        psW = [st.ps(f"psW{i}") for i in range(2)]
        psO = [st.ps(f"psO{i}") for i in range(2)]
        if kind == "L0":
            wu = st.sb("wu", [128, F])
            psU = [st.ps(f"psU{i}") for i in range(2)]
        if kind == "L1":
            b1 = st.sb("b1", [128, C])
            b2 = st.sb("b2", [8, D])
            hx = st.sb("hx", [128, 2, TILES, D])
            gb = st.sb("gb", [128, 2, D])
            y2 = st.sb("y2", [128, TILES, D])
            stats = st.sb("stats", [128, TILES, 6])
            mv = st.sb("mv", [128, TILES, 2])
            vare = st.sb("vare", [128, TILES])
            rstd = st.sb("rstd", [128, TILES])
            half = st.sb("half", [128, TILES])
        if kind == "L2":
            xm = st.sb("xm", [128, 2, T])
        const_in = st.sem("const_in")
        sel_cast = st.sem("sel_cast")
        x_in = [st.sem(f"x_in{s}") for s in range(2)]
        res_in = [st.sem(f"res_in{s}") for s in range(2)]
        g_cast = st.sem("g_cast")
        in_free = st.sem("in_free")
        up_done = st.sem("up_done")
        act_done = st.sem("act_done")
        mid_done = st.sem("mid_done")
        down_done = st.sem("down_done")
        sum_done = st.sem("sum_done")
        sum_free = st.sem("sum_free")
        out_done = st.sem("out_done")
        stored = [st.pool_dma_sem(64 * (NB // 2)) for s in range(2)]
        dve = st.sem("dve")
        paced = st.sem("paced")
        rep_done = st.sem("rep_done")
        masked = st.sem("masked")
        var_done = st.sem("var_done")
        rstd_done = st.sem("rstd_done")
        half_set = st.sem("half_set")

        with nc.Block() as block:
            @block.sync
            def _(sp):
                sp.dma_start(w1[:], W[name_of(kind, "w1")]).then_inc(const_in, 16)
                sp.dma_start(w2[:], W[name_of(kind, "w2")].rearrange("(c p) d -> p c d", p=128)).then_inc(const_in, 16)
                sp.dma_start(sel32[:], W[name_of(kind, "sel")]).then_inc(const_in, 16)
                if kind == "L0":
                    sp.dma_start(wu[:], W["L0_wu"]).then_inc(const_in, 16)
                if kind == "L1":
                    sp.dma_start(b1[:], W["L1_b1"]).then_inc(const_in, 16)
                    sp.dma_start(b2[:], W["L1_b2"]).then_inc(const_in, 16)
                    sp.dma_start(gb[:, 0, :], W["L1_ln2_g"].to_broadcast([128, D])).then_inc(const_in, 16)
                    sp.dma_start(gb[:, 1, :], W["L1_ln2_b"].to_broadcast([128, D])).then_inc(const_in, 16)
                with sp.Fori(0, NB // 2) as i:
                    for s in range(2):
                        b = i * 2 + s
                        sp.wait_ge(in_free, b + 1)
                        sp.dma_start(xT[:, s], xnt[:, bass.ds(b * T, T)]).then_inc(x_in[s], 16)
                        sp.dma_start(g32[:, s], table[0:GR, bass.ds(b * T, T)]).then_inc(x_in[s], 16)
                        sp.wait_ge(sum_free, b + 1)
                        load_tiles(sp, xt[:, s], X, b, permuted, res_in[s])
                        if kind == "L1":
                            load_tiles(sp, hx[:, s], hn, b, False, res_in[s])

            @block.gpsimd
            def _(pool):
                if kind == "L1":
                    pool.memset(half[:], -0.5).then_inc(half_set, 1)
                    pool.wait_ge(half_set, 1)
                pool.sem_inc(sum_free, 2)
                with pool.Fori(0, NB // 2) as i:
                    for s in range(2):
                        b = i * 2 + s
                        if kind == "L1":
                            pool.wait_ge(var_done, b + 1)
                            pool.tensor_tensor(rstd[:], vare[:], half[:], ALU.pow).then_inc(rstd_done, 1)
                        pool.wait_ge(out_done, b + 1)
                        store_tiles(pool, X, xo[:, s], b, permuted, stored[s].sem)
                for s in range(2):
                    stored[s].wait(pool, 64 * (NB // 2))

            @block.tensor
            def _(pe):
                pe.sem_inc(in_free, 2)
                pe.sem_inc(down_done, 2)
                pe.wait_ge(const_in, 16 * NCON[kind])
                pe.wait_ge(sel_cast, 1)
                with pe.Fori(0, NB // 2) as i:
                    for s in range(2):
                        b = i * 2 + s
                        pe.wait_ge(x_in[s], i * 32 + 32)
                        pe.wait_ge(g_cast, b + 1)

                        def rep(j, m):
                            return pe.matmul(psW[j % 2][0:m, :], sel[:, j * 128:j * 128 + m], g16[:, s],
                                             start=True, stop=True)

                        def up(c):
                            m = rows[c]
                            if kind == "L2":
                                if c % 4 == 0:
                                    e = c // 4
                                    pe.wait_ge(masked, b * 8 + e + 1)
                                    rep(e, 128).then_inc(rep_done, 1)
                                    pe.wait_ge(masked, b * 8 + e + 3)
                                pe.wait_ge(mid_done, b * C + c + 1)
                                pe.matmul(psG[c % 2][:], w1[:, c * 128:(c + 1) * 128], xm[:, c // 4 % 2],
                                          start=True, stop=True).then_inc(up_done, 1)
                                return
                            pe.wait_ge(mid_done, b * C + c + 1)
                            ins = pe.matmul(psG[c % 2][0:m], w1[:, c * 128:c * 128 + m], xT[:, s], start=True, stop=True)
                            if kind == "L0":
                                pe.matmul(psU[c % 2][0:m], wu[:, c * 128:c * 128 + m], xT[:, s], start=True, stop=True)
                            rep(c, m).then_inc(up_done, 1)

                        def down(c):
                            m = rows[c]
                            pe.wait_ge(mid_done, b * C + c + 3)
                            if c == 0:
                                pe.wait_ge(sum_free, b + 1)
                            for k in range(TILES):
                                ins = pe.matmul(psO[s][:, k * D:(k + 1) * D], h[0:m, c % 2, k * 128:(k + 1) * 128],
                                                w2[0:m, c], start=(c == 0 and k == 0),
                                                stop=(c == C - 1 and k == TILES - 1 and kind != "L1"), skip_group_check=True)
                            ins.then_inc(down_done, 1)

                        for c in range(C):
                            up(c)
                            if c:
                                down(c - 1)
                        down(C - 1)
                        if kind == "L1":
                            for k in range(TILES):
                                ins = pe.matmul(psO[s][:, k * D:(k + 1) * D], g32[:, s, k * 128:(k + 1) * 128], b2[:],
                                                start=False, stop=(k == TILES - 1), skip_group_check=True)
                        pe.matmul(psW[0][0:1, 0:1], sel[0:1, 0:1], g16[0:1, s, 0:1], start=True, stop=True).then_inc(sum_done, 1)

            @block.scalar
            def _(a):
                with a.Fori(0, NB // 2) as i:
                    for s in range(2):
                        b = i * 2 + s
                        for c in range(C):
                            m = rows[c]
                            a.wait_ge(up_done, b * C + c + 1)
                            a.wait_ge(mid_done, b * C + c + 1)
                            if kind == "L0":
                                ins = a.activation(a1[0:m, c % 2], psG[c % 2][0:m], ACT.Silu)
                            elif kind == "L1":
                                if b is not None and c == 0:
                                    a.wait_ge(const_in, 16 * NCON[kind])
                                ins = a.activation(a1[0:m, c % 2], psG[c % 2][0:m], ACT.Gelu, bias=b1[:, c:c + 1])
                            else:
                                ins = a.activation(a1[0:m, c % 2], psG[c % 2][0:m], ACT.Relu)
                            ins.then_inc(act_done, 1)

            @block.vector
            def _(v):
                v.wait_ge(const_in, 16 * NCON[kind])
                v.tensor_copy(sel[:], sel32[:]).then_inc(sel_cast, 1)
                v.sem_inc(mid_done, 2)
                if kind == "L2":
                    v.sem_inc(masked, 2)
                with v.Fori(0, NB // 2) as i:
                    STEPS = [0]
                    PER = 2 * {"L0": C, "L1": 6, "L2": 0}[kind]

                    def link(ins):
                        STEPS[0] += 1
                        ins.then_inc(dve, 1)
                        v.wait_ge(dve, i * PER + STEPS[0])
                        v.sem_inc(paced, 1)

                    for s in range(2):
                        b = i * 2 + s
                        v.wait_ge(x_in[s], i * 32 + 32)
                        v.wait_ge(in_free, b + 1)
                        v.tensor_copy(g16[:, s], g32[:, s]).then_inc(g_cast, 1)
                        for c in range(C):
                            m = rows[c]
                            if kind == "L2" and c % 4 == 0:
                                e = c // 4
                                v.wait_ge(rep_done, b * 8 + e + 1)
                                if e >= 2:
                                    v.wait_ge(up_done, b * C + 4 * (e - 1))
                                v.tensor_tensor(xm[:, e % 2], xT[:, s], psW[e % 2][:], ALU.mult).then_inc(masked, 1)
                            v.wait_ge(act_done, b * C + c + 1)
                            if kind == "L0":
                                link(v.tensor_tensor(tb[0:m, c % 2], a1[0:m, c % 2], psU[c % 2][0:m], ALU.mult))
                            v.wait_ge(down_done, b * C + c + 1)
                            if kind == "L0":
                                ins = v.tensor_tensor(h[0:m, c % 2], tb[0:m, c % 2], psW[c % 2][0:m], ALU.mult)
                            elif kind == "L1":
                                ins = v.tensor_tensor(h[0:m, c % 2], a1[0:m, c % 2], psW[c % 2][0:m], ALU.mult)
                            else:
                                ins = v.tensor_tensor(h[0:m, c % 2], a1[0:m, c % 2], a1[0:m, c % 2], ALU.mult)
                            ins.then_inc(mid_done, 1)
                        v.wait_ge(sum_done, b + 1)
                        v.wait_ge(res_in[s], i * (128 if kind == "L1" else 64) + (128 if kind == "L1" else 64))
                        stored[s].wait(v, i * 64)
                        O = psO[s][:].rearrange("p (k d) -> p k d", k=TILES)
                        if kind != "L1":
                            v.scalar_tensor_tensor(out=xo[:, s], in0=O, scalar=0.5, in1=xt[:, s],
                                                   op0=ALU.mult, op1=ALU.add).then_inc(out_done, 1)
                        else:
                            link(v.tensor_tensor(y2[:], O, hx[:, s], ALU.add))
                            for k in range(TILES):
                                ins = v.bn_stats(stats[:, k], y2[:, k])
                            link(ins)
                            for k in range(TILES):
                                ins = v.bn_aggr(mv[:, k], stats[:, k])
                            link(ins)
                            v.tensor_scalar(vare[:], mv[:, :, 1], 1e-5, None, ALU.add).then_inc(var_done, 1)
                            v.wait_ge(rstd_done, b + 1)
                            for k in range(TILES):
                                ins = v.tensor_scalar(y2[:, k], y2[:, k], mv[:, k, 0:1], rstd[:, k:k + 1],
                                                      ALU.subtract, ALU.mult)
                            link(ins)
                            link(v.tensor_tensor(y2[:], y2[:], gb[:, 0:1, :].to_broadcast([128, TILES, D]), ALU.mult))
                            link(v.tensor_tensor(y2[:], y2[:], gb[:, 1:2, :].to_broadcast([128, TILES, D]), ALU.add))
                            v.scalar_tensor_tensor(out=xo[:, s], in0=y2[:], scalar=0.5, in1=xt[:, s],
                                                   op0=ALU.mult, op1=ALU.add).then_inc(out_done, 1)
                        v.wait_ge(out_done, b + 1)
                        v.sem_inc(sum_free, 1)
                        v.sem_inc(in_free, 1)
                assert STEPS[0] == PER, (STEPS[0], PER)


def attention(nc, name, W, kind, xnt, S, X, out):
    key = {"rel": "A0", "block": "A1", "causal": "A2", "plain": "A3"}[kind]
    DV = 64 if kind == "causal" else HD
    VW = HEADS * DV
    NV = TILES * VW // 512 if kind == "causal" else TILES
    QK = 8
    block_kind = kind == "block"
    added = kind != "plain"
    U = TILES * 4 if block_kind else TILES * HEADS
    PERT = U // TILES
    KR = 9 if kind == "rel" else 8
    OB = 2 if kind == "causal" else 1
    OT = VW // 128
    projected = kind != "rel"
    with Stage(nc, name) as st:
        ident = st.sb("ident", [128, 128])
        wq = st.sb("wq", [128, 4, 128])
        wk = st.sb("wk", [128, 4, 128])
        bq = st.sb("bq", [128, 4])
        bk = st.sb("bk", [128, 4])
        wv = st.sb("wv", [128, VW])
        xT = st.sb("xT", [128, 2, T])
        xt = st.sb("xt", [128, 2, TILES, D])
        q = st.sb("q", [128, 4, T])
        k_ = st.sb("k", [128, 4, T])
        va = st.sb("va", [128, TILES, VW])
        p = st.sb("p", [128, 3, T])
        pT = st.sb("pT", [128, 2, T])
        nm = st.sb("nm", [128, 4, 4])
        rs = st.sb("rs", [128, TILES, HEADS])
        ri = st.sb("ri", [128, 2, HEADS])
        o = st.sb("o", [128, 2, VW])
        xo = st.sb("xo", [128, 2, TILES, D])
        psP = [st.ps(f"psP{i}") for i in range(2)]
        psS = [st.ps(f"psS{i}") for i in range(2)]
        psT = [st.ps(f"psT{i}") for i in range(2)]
        psO = st.ps("psO", [128, 512 * OB])
        if added:
            t = st.sb("t", [128, 3, T])
        if kind in ("causal", "block"):
            mask = st.sb("mask", [128, T])
        if kind == "rel":
            far = st.sb("far", [128, 2])
            kl = st.sb("kl", [128, 4, T])
            kr = st.sb("kr", [128, 4, T])
            wrel = st.sb("wrel", [128, 511])
            pos = st.sb("pos", [128, TILES, 2, T])
            rp = st.sb("rp", [128, 3, 511])
        if kind != "causal":
            bv = st.sb("bv", [128, VW])
        if projected:
            wo = st.sb("wo", [128, OT, D])
            oT = st.sb("oT", [128, 2, VW])
            if kind != "causal":
                bo = st.sb("bo", [128, D])
        const_in = st.sem("const_in")
        x_in = [st.sem(f"x_in{s}") for s in range(2)]
        res_in = [st.sem(f"res_in{s}") for s in range(2)]
        in_free = st.sem("in_free")
        res_free = st.sem("res_free")
        proj_done = st.sem("proj_done")
        qk_copied = st.sem("qk_copied")
        v_copied = st.sem("v_copied")
        scores_ready = st.sem("scores_ready")
        added_done = st.sem("added_done")
        max_done = st.sem("max_done")
        probs_done = st.sem("probs_done")
        turned = st.sem("turned")
        turned_copied = st.sem("turned_copied")
        tile_done = st.sem("tile_done")
        tile_scaled = st.sem("tile_scaled")
        o_turned = st.sem("o_turned")
        o_copied = st.sem("o_copied")
        o_projected = st.sem("o_projected")
        out_done = st.sem("out_done")
        stored = [st.pool_dma_sem(64 * (NB // 2)) for s in range(2)]
        dve = st.sem("dve")
        paced = st.sem("paced")
        pos_set = st.sem("pos_set")
        rel_ready = st.sem("rel_ready")
        rel_copied = st.sem("rel_copied")
        rel_stored = [st.sem(f"rel_stored{j}") for j in range(3)]
        pos_in = [st.sem(f"pos_in{j}") for j in range(8)]
        NCN = 6 + (kind in ("causal", "block")) + 2 * (kind == "rel") + (kind != "causal") + projected + (
            projected and kind != "causal")

        def width(it):
            return (it + 1) * 128 if kind == "causal" else T

        def window(it):
            return max(0, it - 1) * 128, min(TILES, it + 2) * 128

        with nc.Block() as block:
            @block.sync
            def _(sp):
                def const(dst, src):
                    sp.dma_start(dst, src).then_inc(const_in, 16)

                const(ident[:], W["ident"])
                const(wq[:].rearrange("p a b -> p (a b)"), W[f"{key}_wq"])
                const(wk[:].rearrange("p a b -> p (a b)"), W[f"{key}_wk"])
                const(bq[:], W[f"{key}_bq"])
                const(bk[:], W[f"{key}_bk"])
                const(wv[:], W[f"{key}_wv"])
                if kind in ("causal", "block"):
                    const(mask[:], W[f"{key}_mask"])
                if kind == "rel":
                    const(far[:], W["A0_far"])
                    const(wrel[:], W["A0_wrel"])
                if kind != "causal":
                    const(bv[:], W[f"{key}_bv"].to_broadcast([128, VW]))
                if projected:
                    const(wo[:], W[f"{key}_wo"].rearrange("(c p) d -> p c d", p=128))
                    if kind != "causal":
                        const(bo[:], W[f"{key}_bo"].to_broadcast([128, D]))
                if kind == "rel":
                    sp.wait_ge(pos_set, 1)
                with sp.Fori(0, NB // 2) as i:
                    for s in range(2):
                        b = i * 2 + s
                        sp.wait_ge(in_free, b + 1)
                        sp.dma_start(xT[:, s], xnt[:, bass.ds(b * T, T)]).then_inc(x_in[s], 16)
                        sp.wait_ge(res_free, b + 1)
                        load_tiles(sp, xt[:, s], X, b, False, res_in[s])
                        if kind == "rel":
                            for u in range(U):
                                it, h = divmod(u, HEADS)
                                lo, hi = window(it)
                                j = u % 2
                                if h >= 2:
                                    sp.wait_ge(added_done, b * U + u - 1)
                                base = (lo - (it - 1) * 128) + 127
                                row = S["PR"][bass.ds(b * U + u, 1)]
                                src = skewed(row, base, hi - lo)
                                sp.dma_start(pos[:, it, j, lo:hi], src).then_inc(pos_in[it * 2 + j], 16)

            @block.gpsimd
            def _(pool):
                if kind == "rel":
                    pool.memset(pos[:].rearrange("p a b c -> p (a b c)"), 0.0).then_inc(pos_set, 1)
                with pool.Fori(0, NB // 2) as i:
                    for s in range(2):
                        b = i * 2 + s
                        pool.wait_ge(out_done, b * TILES + TILES + 1)
                        store_tiles(pool, out, xo[:, s], b, False, stored[s].sem)
                for s in range(2):
                    stored[s].wait(pool, 64 * (NB // 2))

            @block.tensor
            def _(pe):
                pe.sem_inc(in_free, 2)
                pe.wait_ge(const_in, 16 * NCN)
                with pe.Fori(0, NB // 2) as i:
                    for s in range(2):
                        b = i * 2 + s
                        pe.wait_ge(x_in[s], i * 16 + 16)
                        for j in range(QK + NV):
                            if 2 <= j < QK + 2:
                                pe.wait_ge(qk_copied, b * QK + j - 1)
                            elif j >= QK + 2:
                                pe.wait_ge(v_copied, b * NV + j - QK - 1)
                            elif projected:
                                pe.wait_ge(out_done, b * TILES + 1)
                            if j < 4:
                                ins = pe.matmul(psP[j % 2][:], wq[:, j], xT[:, s], start=True, stop=True)
                            elif j < QK:
                                ins = pe.matmul(psP[j % 2][:], wk[:, j - 4], xT[:, s], start=True, stop=True)
                            else:
                                n = j - QK
                                k, c = (n // 2, n % 2) if kind == "causal" else (n, 0)
                                w = min(VW, 512)
                                ins = pe.matmul(psP[j % 2][:, 0:w], xT[:, s, k * 128:(k + 1) * 128],
                                                wv[:, c * 512:c * 512 + w], start=True, stop=True)
                            ins.then_inc(proj_done, 1)
                        pe.wait_ge(qk_copied, b * QK + QK)
                        pe.wait_ge(v_copied, b * NV + NV)
                        pe.sem_inc(in_free, 1)

                        def scores(u):
                            it, h = divmod(u, PERT)
                            if u >= 2:
                                if added:
                                    pe.wait_ge(added_done, b * U + u - 1)
                                else:
                                    pe.wait_ge(probs_done, b * U + u - 1)
                            if block_kind:
                                for m in range(4):
                                    r = slice(32 * h, 32 * h + HD)
                                    ins = pe.matmul(psS[u % 2][:, m * 128:(m + 1) * 128],
                                                    q[r, m, it * 128:(it + 1) * 128], k_[r, m, it * 128:(it + 1) * 128],
                                                    start=True, stop=True)
                                ins.then_inc(scores_ready, 1)
                                return
                            m, g = divmod(h, 4)
                            r = slice(32 * g, 32 * g + KR)
                            lhs = q[r, m, it * 128:(it + 1) * 128]
                            if kind == "rel":
                                lo, hi = window(it)
                                parts = [(kl, 0, lo), (k_, lo, hi), (kr, hi, T)]
                            else:
                                parts = [(k_, 0, width(it))]
                            for ks, lo, hi in parts:
                                if hi > lo:
                                    ins = pe.matmul(psS[u % 2][:, lo:hi], lhs, ks[r, m, lo:hi], start=True, stop=True)
                            ins.then_inc(scores_ready, 1)

                        def turn(u):
                            it, h = divmod(u, PERT)
                            pe.wait_ge(probs_done, b * U + u + 1)
                            if u >= 2:
                                pe.wait_ge(turned_copied, b * U + u - 1)
                            for j in range(width(it) // 128):
                                ins = pe.transpose(psT[u % 2][:, j * 128:(j + 1) * 128],
                                                   p[:, u % 3, j * 128:(j + 1) * 128], ident[:])
                            ins.then_inc(turned, 1)

                        def values(u):
                            it, h = divmod(u, PERT)
                            pe.wait_ge(turned_copied, b * U + u + 1)
                            if h == 0:
                                pe.wait_ge(tile_scaled, b * TILES + it + 1)
                            if block_kind:
                                for g in range(4):
                                    hh = 4 * g + h
                                    ins = pe.matmul(psO[:, hh * DV:(hh + 1) * DV], pT[:, u % 2, g * 128:(g + 1) * 128],
                                                    va[:, it, hh * DV:(hh + 1) * DV], start=True, stop=True)
                            else:
                                J = width(it) // 128
                                for j in range(J):
                                    ins = pe.matmul(psO[:, h * DV:(h + 1) * DV], pT[:, u % 2, j * 128:(j + 1) * 128],
                                                    va[:, j, h * DV:(h + 1) * DV], start=(j == 0), stop=(j == J - 1))
                            if h == PERT - 1:
                                ins.then_inc(tile_done, 1)

                        def turn_output(it):
                            n = b * TILES + it
                            pe.wait_ge(tile_scaled, n + 1 + 1)
                            for c in range(OT):
                                if c % 4 == 0:
                                    if it > 0 and c == 0:
                                        pe.wait_ge(o_copied, n + 1)
                                        pe.wait_ge(out_done, n + 1)
                                ins = pe.transpose(psP[c // 4][:, c % 4 * 128:(c % 4 + 1) * 128],
                                                   o[:, it % 2, c * 128:(c + 1) * 128], ident[:])
                            ins.then_inc(o_turned, 1)

                        def project(it):
                            pe.wait_ge(o_copied, b * TILES + it + 1 + 1)
                            for c in range(OT):
                                ins = pe.matmul(psP[0][:, 0:D], oT[:, it % 2, c * 128:(c + 1) * 128], wo[:, c],
                                                start=(c == 0), stop=(c == OT - 1))
                            ins.then_inc(o_projected, 1)

                        for u in range(U + 8):
                            if u < U:
                                scores(u)
                            if 2 <= u < U + 2:
                                turn(u - 2)
                            if 3 <= u < U + 3:
                                values(u - 3)
                            if projected and u >= 5 and (u - 5) % PERT == PERT - 1 and u - 5 < U:
                                turn_output((u - 5) // PERT)
                            if projected and u >= 7 and (u - 7) % PERT == PERT - 1 and u - 7 < U:
                                project((u - 7) // PERT)

            @block.scalar
            def _(a):
                with a.Fori(0, NB // 2) as i:
                    for s in range(2):
                        b = i * 2 + s
                        for n in range(NV):
                            j = QK + n
                            a.wait_ge(proj_done, b * (QK + NV) + j + 1)
                            k, c = (n // 2, n % 2) if kind == "causal" else (n, 0)
                            w = min(VW, 512)
                            if kind != "causal":
                                continue
                            a.copy(va[:, k, c * 512:c * 512 + w], psP[j % 2][:, 0:w]).then_inc(v_copied, 1)
                        for u in range(U):
                            it, h = divmod(u, PERT)
                            a.wait_ge(max_done, b * U + u + 1)
                            if u >= 3:
                                a.wait_ge(turned, b * U + u - 2)
                            src = t[:, u % 3] if added else psS[u % 2][:]
                            if block_kind:
                                for g in range(4):
                                    ins = a.activation(p[:, u % 3, g * 128:(g + 1) * 128], src[:, g * 128:(g + 1) * 128],
                                                       ACT.Exp, bias=nm[:, u % 4, g:g + 1], scale=-1.0,
                                                       accum_out=rs[:, it, 4 * g + h:4 * g + h + 1])
                            else:
                                L = width(it)
                                ins = a.activation(p[:, u % 3, 0:L], src[:, 0:L], ACT.Exp, bias=nm[:, u % 4, 0:1],
                                                   scale=-1.0, accum_out=rs[:, it, h:h + 1])
                            ins.then_inc(probs_done, 1)

            @block.vector
            def _(v):
                v.sem_inc(res_free, 2)
                v.sem_inc(out_done, 1)
                v.sem_inc(tile_scaled, 1)
                v.sem_inc(o_copied, 1)
                v.wait_ge(const_in, 16 * NCN)
                with v.Fori(0, NB // 2) as i:
                    STEPS = [0]
                    PER = 2 * (TILES * (2 if kind in ("plain", "block") else 1) + (U if block_kind else 0))

                    def link(ins):
                        STEPS[0] += 1
                        ins.then_inc(dve, 1)
                        v.wait_ge(dve, i * PER + STEPS[0])

                    for s in range(2):
                        b = i * 2 + s
                        for j in range(QK):
                            v.wait_ge(proj_done, b * (QK + NV) + j + 1)
                            m = j % 4
                            if j < 4:
                                v.tensor_scalar(q[:, m], psP[j % 2][:], bq[:, m:m + 1], None, ALU.add).then_inc(qk_copied, 1)
                            else:
                                v.tensor_scalar(k_[:, m], psP[j % 2][:], bk[:, m:m + 1], -(HD ** -0.5), ALU.add,
                                                ALU.mult).then_inc(qk_copied, 1)
                        if kind == "rel":
                            v.wait_ge(qk_copied, b * QK + QK)
                            flat = k_[:].rearrange("p a b -> p (a b)")
                            v.tensor_scalar(kl[:].rearrange("p a b -> p (a b)"), flat, far[:, 0:1], None, ALU.subtract)
                            v.tensor_scalar(kr[:].rearrange("p a b -> p (a b)"), flat, far[:, 1:2], None, ALU.subtract)
                        if kind != "causal":
                            for n in range(NV):
                                j = QK + n
                                v.wait_ge(proj_done, b * (QK + NV) + j + 1)
                                v.tensor_tensor(va[:, n], psP[j % 2][:, 0:VW], bv[:], ALU.add).then_inc(v_copied, 1)

                        def lowest(u):
                            it, h = divmod(u, PERT)
                            L = width(it)
                            v.wait_ge(scores_ready, b * U + u + 1)
                            if added and u >= 3:
                                v.wait_ge(probs_done, b * U + u - 2)
                            elif u >= 4:
                                v.wait_ge(probs_done, b * U + u - 3)
                            if kind == "plain":
                                v.tensor_reduce(nm[:, u % 4, 0:1], psS[u % 2][:], AX.X, ALU.min).then_inc(max_done, 1)
                            elif block_kind:
                                link(v.tensor_tensor(t[:, u % 3], psS[u % 2][:], mask[:], ALU.add))
                                v.sem_inc(added_done, 1)
                                v.tensor_reduce(nm[:, u % 4, :], t[:, u % 3].rearrange("p (g k) -> p g k", g=4), AX.X,
                                                ALU.min).then_inc(max_done, 1)
                            else:
                                if kind == "causal":
                                    plus = mask[:, T - L:T]
                                else:
                                    plus = pos[:, it, h % 2]
                                    v.wait_ge(pos_in[it * 2 + h % 2], (b * (HEADS // 2) + h // 2 + 1) * 16)
                                v.sem_inc(paced, 1)
                                v.tensor_tensor_reduce(out=t[:, u % 3, 0:L], in0=psS[u % 2][:, 0:L], in1=plus, scale=1.0,
                                                       scalar=3e38, op0=ALU.add, op1=ALU.min,
                                                       accum_out=nm[:, u % 4, 0:1]).then_inc(max_done, 1)
                                v.wait_ge(max_done, b * U + u + 1)
                                v.sem_inc(added_done, 1)

                        def copy_turned(u):
                            it, h = divmod(u, PERT)
                            v.wait_ge(turned, b * U + u + 1)
                            v.tensor_copy(pT[:, u % 2, 0:width(it)], psT[u % 2][:, 0:width(it)]).then_inc(turned_copied, 1)

                        def scale_tile(it):
                            n = b * TILES + it
                            v.wait_ge(tile_done, n + 1)
                            link(v.reciprocal(ri[:, it % 2], rs[:, it]))
                            O = psO[:, 0:VW].rearrange("p (h d) -> p h d", h=HEADS)
                            dst = o[:, it % 2].rearrange("p (h d) -> p h d", h=HEADS)
                            v.tensor_tensor(dst, O, bc(ri[:, it % 2], DV), ALU.mult).then_inc(tile_scaled, 1)
                            if kind == "rel":
                                v.wait_ge(res_in[s], i * 64 + 64)
                                stored[s].wait(v, i * 64)
                                v.wait_ge(tile_scaled, n + 1 + 1)
                                v.tensor_tensor(xo[:, s, it], o[:, it % 2], xt[:, s, it], ALU.add).then_inc(out_done, 1)

                        def copy_output(it):
                            n = b * TILES + it
                            v.wait_ge(o_turned, n + 1)
                            for c in range(0, OT, 4):
                                w = min(512, VW)
                                ins = v.tensor_copy(oT[:, it % 2, c * 128:c * 128 + w], psP[c // 4][:, 0:w])
                            ins.then_inc(o_copied, 1)

                        def finish_tile(it):
                            n = b * TILES + it
                            v.wait_ge(o_projected, n + 1)
                            v.wait_ge(res_in[s], i * 64 + 64)
                            stored[s].wait(v, i * 64)
                            if kind == "causal":
                                v.tensor_tensor(xo[:, s, it], psP[0][:, 0:D], xt[:, s, it], ALU.add).then_inc(out_done, 1)
                            else:
                                link(v.tensor_tensor(xo[:, s, it], psP[0][:, 0:D], bo[:], ALU.add))
                                v.tensor_tensor(xo[:, s, it], xo[:, s, it], xt[:, s, it], ALU.add).then_inc(out_done, 1)

                        for u in range(U + 8):
                            if u < U:
                                lowest(u)
                            if 2 <= u < U + 2:
                                copy_turned(u - 2)
                            if u >= 4 and (u - 4) % PERT == PERT - 1 and u - 4 < U:
                                scale_tile((u - 4) // PERT)
                            if projected and u >= 6 and (u - 6) % PERT == PERT - 1 and u - 6 < U:
                                copy_output((u - 6) // PERT)
                            if projected and u >= 8 and (u - 8) % PERT == PERT - 1 and u - 8 < U:
                                finish_tile((u - 8) // PERT)
                        v.wait_ge(out_done, b * TILES + TILES + 1)
                        v.sem_inc(res_free, 1)
                assert STEPS[0] == PER, (STEPS[0], PER)


QUINTIC, CUBIC = (3.4445, -4.7750, 2.0315), (1.5, -0.5, 0.0)
GROW, SETTLE = 16, 8


def polar(nc, name, W, PT):
    with Stage(nc, name) as st:
        ident = st.sb("ident", [128, 128])
        ones = st.sb("ones", [128, 128])
        w0 = st.sb("w0", [128, 2, 2, 128])
        x = st.sb("x", [128, 2, 2, 128])
        a = st.sb("a", [128, 2, 128])
        b_ = st.sb("b", [128, 2, 128])
        c_ = st.sb("c", [128, 2, 128])
        aI = st.sb("aI", [128, 2, 128])
        sq = st.sb("sq", [128, 128])
        rows = st.sb("rows", [128, 2])
        tot = st.sb("tot", [128, 2])
        inv = st.sb("inv", [128, 2])
        half = st.sb("half", [128, 2])
        psA = [st.ps(f"psA{m}", [128, 4, 128]) for m in range(2)]
        psX = [st.ps(f"psX{m}", [128, 2, 256]) for m in range(2)]
        const_in = st.sem("const_in")
        ones_set = st.sem("ones_set")
        rows_summed = st.sem("rows_summed")
        total_ready = st.sem("total_ready")
        total_copied = st.sem("total_copied")
        inv_done = st.sem("inv_done")
        x_ready = st.sem("x_ready")
        gram_ready = st.sem("gram_ready")
        gram_copied = st.sem("gram_copied")
        square_ready = st.sem("square_ready")
        poly_ready = st.sem("poly_ready")
        step_ready = st.sem("step_ready")
        dve = st.sem("dve")
        stored = st.sem("stored")
        with nc.Block() as block:
            @block.sync
            def _(sp):
                sp.dma_start(ident[:], W["ident"]).then_inc(const_in, 16)
                for m in range(2):
                    for t in range(2):
                        sp.dma_start(w0[:, m, t], W["P_w"][2 * m + t]).then_inc(const_in, 16)
                sp.wait_ge(x_ready, 2 * (1 + GROW + SETTLE))
                for m in range(2):
                    sp.dma_start(PT[m], x[:, m, 1]).then_inc(stored, 16)
                sp.wait_ge(stored, 32)

            @block.gpsimd
            def _(pool):
                pool.memset(half[:], -0.5)
                pool.memset(ones[:], 1.0).then_inc(ones_set, 1)
                pool.wait_ge(ones_set, 1)
                pool.wait_ge(total_copied, 1)
                pool.tensor_tensor(inv[:], tot[:], half[:], ALU.pow).then_inc(inv_done, 1)

            @block.tensor
            def _(pe):
                pe.wait_ge(const_in, 80)
                pe.wait_ge(ones_set, 1)
                pe.wait_ge(rows_summed, 2)
                pe.matmul(psA[0][:, 0, 0:2], ones[:], rows[:], start=True, stop=True).then_inc(total_ready, 1)

                def step(n, m):
                    pe.wait_ge(x_ready, n + 1 + m)
                    pe.matmul(psA[m][:, 0], x[:, m, 0], x[:, m, 0], start=True, stop=True).then_inc(gram_ready, 1)

                def square(n, m):
                    pe.wait_ge(gram_copied, n + 1 + m)
                    pe.matmul(psA[m][:, 1], a[:, m], a[:, m], start=True, stop=True).then_inc(square_ready, 1)

                def apply(n, m):
                    pe.wait_ge(poly_ready, n + 1 + m)
                    pe.matmul(psX[m][:, 0, 0:128], x[:, m, 1], b_[:, m], start=True, stop=True)
                    pe.matmul(psX[m][:, 1, 0:128], b_[:, m], x[:, m, 1], start=True, stop=True).then_inc(step_ready, 1)

                for first, count in ((0, GROW), (GROW, SETTLE)):
                    with pe.Fori(first, first + count) as i:
                        for f in (step, square, apply):
                            for m in range(2):
                                f(i * 2, m)

            @block.scalar
            def _(s_):
                s_.wait_ge(total_ready, 1)
                s_.copy(tot[:], psA[0][:, 0, 0:2]).then_inc(total_copied, 1)

            @block.vector
            def _(v):
                v.wait_ge(const_in, 80)
                for m in range(2):
                    v.tensor_tensor(sq[:], w0[:, m, 0], w0[:, m, 0], ALU.mult).then_inc(dve, 1)
                    v.wait_ge(dve, 2 * m + 1)
                    v.tensor_reduce(rows[:, m:m + 1], sq[:], AX.X, ALU.add).then_inc(dve, 1)
                    v.wait_ge(dve, 2 * m + 2)
                    v.sem_inc(rows_summed, 1)
                v.wait_ge(inv_done, 1)
                for m in range(2):
                    v.tensor_scalar(x[:, m], w0[:, m], inv[:, m:m + 1], None, ALU.mult).then_inc(x_ready, 1)
                v.tensor_scalar(aI[:, 0], ident[:], QUINTIC[0], None, ALU.mult).then_inc(dve, 1)
                v.tensor_scalar(aI[:, 1], ident[:], CUBIC[0], None, ALU.mult).then_inc(dve, 1)
                v.wait_ge(dve, 6)
                for ph, (first, count, (_, cb, cc)) in enumerate(((0, GROW, QUINTIC), (GROW, SETTLE, CUBIC))):
                    with v.Fori(first, first + count) as i:
                        n = i * 2
                        for m in range(2):
                            v.wait_ge(gram_ready, n + 1 + m)
                            v.tensor_copy(a[:, m], psA[m][:, 0]).then_inc(gram_copied, 1)
                        for m in range(2):
                            v.wait_ge(gram_copied, n + 1 + m)
                            v.scalar_tensor_tensor(out=c_[:, m], in0=a[:, m], scalar=cb, in1=aI[:, ph], op0=ALU.mult,
                                                   op1=ALU.add).then_inc(dve, 1)
                        for m in range(2):
                            v.wait_ge(square_ready, n + 1 + m)
                            v.wait_ge(dve, n + 6 + 1 + m)
                            v.scalar_tensor_tensor(out=b_[:, m], in0=psA[m][:, 1], scalar=cc, in1=c_[:, m], op0=ALU.mult,
                                                   op1=ALU.add).then_inc(poly_ready, 1)
                        for m in range(2):
                            v.wait_ge(step_ready, n + 1 + m)
                            v.tensor_copy(x[:, m], psX[m][:, :, 0:128]).then_inc(x_ready, 1)


def scan_attention(nc, name, W, xnt, X, PT):
    LEVELS = 9
    size = [513] + [256 >> k for k in range(LEVELS)]
    with Stage(nc, name) as st:
        wq = st.sb("wq", [128, 128])
        wv = st.sb("wv", [128, 128])
        wc = st.sb("wc", [128, 128])
        pt = st.sb("pt", [128, 2, 128])
        first = st.sb("first", [128, 1])
        mean = st.sb("mean", [128, 128])
        eps = st.sb("eps", [128, 1])
        xT = st.sb("xT", [128, 2, T])
        seq = st.sb("seq", [128, NB, 513])
        val = st.sb("val", [128, NB, T])
        res = st.sb("res", [128, NB, 513])
        lev = [seq] + [st.sb(f"lev{k}", [128, NB, size[k]]) for k in range(1, LEVELS)]
        sq = st.sb("sq", [128, 2, T])
        root = st.sb("root", [128, 2, T])
        rinv = st.sb("rinv", [128, 2, T])
        g = st.sb("g", [128, 2, T])
        xt = st.sb("xt", [128, 2, TILES, D])
        xo = st.sb("xo", [128, 2, TILES, D])
        psZ = [st.ps(f"psZ{i}") for i in range(2)]
        psM = [st.ps(f"psM{i}") for i in range(2)]
        psP = [st.ps(f"psP{i}") for i in range(2)]
        psY = [st.ps(f"psY{i}") for i in range(2)]

        combines = []

        def add(left, right, out, m, need):
            nb = min(NB, max(1, T // m))
            for b0 in range(0, NB, nb):
                combines.append((left[:, b0:b0 + nb], right[:, b0:b0 + nb], out[:, b0:b0 + nb], nb, m, need))

        for k in range(LEVELS):
            need = len(combines)
            m = size[k + 1]
            out = lev[k + 1][:] if k + 1 < LEVELS else res[:, :, 511:512]
            add(lev[k][:, :, 0:2 * m:2], lev[k][:, :, 1:2 * m:2], out, m, need)
        DOWN = len(combines)
        for k in range(LEVELS - 1, -1, -1):
            need = len(combines)
            m = 256 if k == 0 else size[k] // 2 - 1
            if m == 0:
                continue
            w = 1 << k
            l0, o0 = 2 * w - 1, 3 * w - 1
            add(res[:, :, l0:l0 + 2 * w * (m - 1) + 1:2 * w], lev[k][:, :, 2:2 * m + 1:2],
                res[:, :, o0:o0 + 2 * w * (m - 1) + 1:2 * w], m, need)
        CN = len(combines)

        const_in = st.sem("const_in")
        eps_set = st.sem("eps_set")
        x_in = [st.sem(f"x_in{s}") for s in range(2)]
        in_free = st.sem("in_free")
        q_ready = st.sem("q_ready")
        v_ready = st.sem("v_ready")
        q_copied = st.sem("q_copied")
        v_copied = st.sem("v_copied")
        first_set = st.sem("first_set")
        sums_ready = st.sem("sums_ready")
        squared = st.sem("squared")
        means_ready = st.sem("means_ready")
        rooted = st.sem("rooted")
        inverted = st.sem("inverted")
        combined = st.sem("combined")
        heads_copied = st.sem("heads_copied")
        gated = st.sem("gated")
        y_ready = st.sem("y_ready")
        res_in = [st.sem(f"res_in{s}") for s in range(2)]
        out_done = st.sem("out_done")
        out_free = st.sem("out_free")
        stored = [st.pool_dma_sem(64 * (NB // 2)) for s in range(2)]
        with nc.Block() as block:
            @block.sync
            def _(sp):
                sp.dma_start(wq[:], W["S_wq"]).then_inc(const_in, 16)
                sp.dma_start(wv[:], W["S_wv"]).then_inc(const_in, 16)
                sp.dma_start(wc[:], W["S_wc"]).then_inc(const_in, 16)
                sp.dma_start(first[:], W["S_first"]).then_inc(const_in, 16)
                sp.dma_start(mean[:], W["S_mean"]).then_inc(const_in, 16)
                for m in range(2):
                    sp.dma_start(pt[:, m], PT[m]).then_inc(const_in, 16)
                with sp.Fori(0, NB // 2) as i:
                    for s in range(2):
                        b = i * 2 + s
                        sp.wait_ge(in_free, b + 1)
                        sp.dma_start(xT[:, s], xnt[:, bass.ds(b * T, T)]).then_inc(x_in[s], 16)
                with sp.Fori(0, NB // 2) as i:
                    for s in range(2):
                        b = i * 2 + s
                        sp.wait_ge(out_free, b + 1)
                        load_tiles(sp, xt[:, s], X, b, False, res_in[s])

            @block.gpsimd
            def _(pool):
                pool.memset(eps[:], 1e-8).then_inc(eps_set, 1)
                with pool.Fori(0, NB // 2) as i:
                    for s in range(2):
                        b = i * 2 + s
                        pool.wait_ge(out_done, b + 1)
                        store_tiles(pool, X, xo[:, s], b, False, stored[s].sem)
                for s in range(2):
                    stored[s].wait(pool, 64 * (NB // 2))

            @block.tensor
            def _(pe):
                pe.sem_inc(in_free, 2)
                pe.sem_inc(q_copied, 1)
                pe.sem_inc(v_copied, 1)
                pe.wait_ge(const_in, 112)
                with pe.Fori(0, NB // 2) as i:
                    for s in range(2):
                        b = i * 2 + s
                        pe.wait_ge(x_in[s], i * 16 + 16)
                        pe.wait_ge(q_copied, b + 1)
                        pe.matmul(psP[0][:], wq[:], xT[:, s], start=True, stop=True).then_inc(q_ready, 1)
                        pe.wait_ge(v_copied, b + 1)
                        pe.matmul(psP[1][:], wv[:], xT[:, s], start=True, stop=True).then_inc(v_ready, 1)
                        pe.wait_ge(v_copied, b + 2)
                        pe.sem_inc(in_free, 1)
                pe.wait_ge(q_copied, NB + 1)
                pe.wait_ge(first_set, 1)

                def means(n):
                    _, _, _, nb, m, _ = combines[n]
                    pe.wait_ge(squared, n + 1)
                    if n >= 2:
                        pe.wait_ge(rooted, n - 1)
                    pe.matmul(psM[n % 2][:, 0:nb * m], mean[:], sq[:, n % 2, 0:nb * m], start=True,
                              stop=True).then_inc(means_ready, 1)

                for n, (left, right, _, nb, m, need) in enumerate(combines):
                    late = need > n - 1
                    if n and late:
                        means(n - 1)
                    ahead = max(need, n - 1)
                    if ahead:
                        pe.wait_ge(combined, ahead)
                    if n == DOWN:
                        pe.wait_ge(heads_copied, LEVELS - 1)
                    z = psZ[n % 2][:, 0:nb * m].rearrange("p (b m) -> p b m", b=nb)
                    pe.matmul(z, pt[:, 0], left, start=True, stop=False)
                    pe.matmul(z, pt[:, 1], right, start=False, stop=True).then_inc(sums_ready, 1)
                    if n and not late:
                        means(n - 1)
                means(CN - 1)
                with pe.Fori(0, NB // 2) as i:
                    for s in range(2):
                        b = i * 2 + s
                        pe.wait_ge(gated, b + 1)
                        pe.wait_ge(out_free, b + 1)
                        for k in range(TILES):
                            ins = pe.matmul(psY[s][:, k * D:(k + 1) * D], g[:, s, k * 128:(k + 1) * 128], wc[:],
                                            start=True, stop=True)
                        ins.then_inc(y_ready, 1)

            @block.scalar
            def _(a):
                a.wait_ge(eps_set, 1)
                with a.Fori(0, NB) as b:
                    a.wait_ge(q_ready, b + 1)
                    a.copy(seq[:, bass.ds(b, 1), 1:513], psP[0][:].unsqueeze(1)).then_inc(q_copied, 1)
                for n, (_, _, _, nb, m, _) in enumerate(combines):
                    c = nb * m
                    a.wait_ge(sums_ready, n + 1)
                    if n >= 2:
                        a.wait_ge(means_ready, n - 1)
                    a.activation(sq[:, n % 2, 0:c], psZ[n % 2][:, 0:c], ACT.Square).then_inc(squared, 1)
                    a.wait_ge(means_ready, n + 1)
                    if n >= 2:
                        a.wait_ge(inverted, n - 1)
                    a.activation(root[:, n % 2, 0:c], psM[n % 2][:, 0:c], ACT.Sqrt, bias=eps[:, 0:1]).then_inc(rooted, 1)

            @block.vector
            def _(v):
                v.sem_inc(out_free, 2)
                v.wait_ge(const_in, 112)
                v.tensor_copy(seq[:, :, 0:1], first[:].unsqueeze(1).to_broadcast([128, NB, 1])).then_inc(first_set, 1)
                with v.Fori(0, NB) as b:
                    v.wait_ge(v_ready, b + 1)
                    v.tensor_copy(val[:, bass.ds(b, 1), :], psP[1][:].unsqueeze(1)).then_inc(v_copied, 1)
                for n, (_, _, out, nb, m, _) in enumerate(combines):
                    c = nb * m
                    if n == DOWN:
                        v.wait_ge(combined, DOWN)
                        for k in range(1, LEVELS):
                            w = 1 << k
                            v.tensor_copy(res[:, :, w - 1:w], lev[k][:, :, 0:1]).then_inc(heads_copied, 1)
                    v.wait_ge(rooted, n + 1)
                    if n >= 2:
                        v.wait_ge(combined, n - 1)
                    v.reciprocal(rinv[:, n % 2, 0:c], root[:, n % 2, 0:c]).then_inc(inverted, 1)
                    v.wait_ge(inverted, n + 1)
                    v.tensor_tensor(out, psZ[n % 2][:, 0:c].rearrange("p (b m) -> p b m", b=nb),
                                    rinv[:, n % 2, 0:c].rearrange("p (b m) -> p b m", b=nb), ALU.mult).then_inc(combined, 1)
                v.wait_ge(combined, CN)
                with v.Fori(0, NB // 2) as i:
                    for s in range(2):
                        b = i * 2 + s
                        v.tensor_tensor(g[:, s].unsqueeze(1), res[:, bass.ds(b, 1), 1:513], val[:, bass.ds(b, 1), :],
                                        ALU.mult).then_inc(gated, 1)
                        v.wait_ge(y_ready, b + 1)
                        v.wait_ge(res_in[s], i * 64 + 64)
                        stored[s].wait(v, i * 64)
                        v.tensor_tensor(xo[:, s], psY[s][:].rearrange("p (k d) -> p k d", k=TILES), xt[:, s],
                                        ALU.add).then_inc(out_done, 1)
                        v.wait_ge(out_done, b + 1)
                        v.sem_inc(out_free, 1)


EX, FX, CAP = 64, 96, 64
ROWX = D + EX


def route64(nc, name, W, xnt, XW, X, SLOT):
    with Stage(nc, name) as st:
        ident = st.sb("ident", [128, 128])
        wr = st.sb("wr", [128, EX])
        wsg = st.sb("wsg", [128, 2 * FX])
        wsd = st.sb("wsd", [FX, D])
        ramp = st.sb("ramp", [EX, N])
        slot_no = st.sb("slot_no", [EX, CAP])
        xT = st.sb("xT", [128, 2, T])
        xt = st.sb("xt", [128, 2, TILES, D])
        xo = st.sb("xo", [128, 2, TILES, D])
        lg = st.sb("lg", [128, TILES, EX])
        mx = st.sb("mx", [128, TILES])
        ex = st.sb("ex", [128, TILES, EX])
        sm = st.sb("sm", [128, TILES])
        ri = st.sb("ri", [128, TILES])
        pr = st.sb("pr", [128, TILES, EX])
        left = st.sb("left", [128, TILES, EX])
        v8 = st.sb("v8", [128, TILES, 8])
        mk = st.sb("mk", [128, 2, TILES, EX])
        wt = st.sb("wt", [128, 2, TILES, EX])
        sg = st.sb("sg", [FX, T])
        h = st.sb("h", [FX, T])
        order = [st.sb(f"order{j}", [EX, N]) for j in range(2)]
        top = st.sb("top", [EX, CAP])
        none = st.sb("none", [EX, CAP])
        tok = st.sb("tok", [EX, CAP])
        toki = st.sb("toki", [EX, CAP], I32)
        psL = st.ps("psL")
        psM = st.ps("psM")
        psG = st.ps("psG")
        psU = st.ps("psU")
        psO = st.ps("psO")
        const_in = st.sem("const_in")
        x_in = [st.sem(f"x_in{s}") for s in range(2)]
        res_in = [st.sem(f"res_in{s}") for s in range(2)]
        in_free = st.sem("in_free")
        logits_ready = st.sem("logits_ready")
        shifted = st.sem("shifted")
        exps_done = st.sem("exps_done")
        chosen = st.sem("chosen")
        choice_turned = st.sem("choice_turned")
        choice_kept = st.sem("choice_kept")
        shared_ready = st.sem("shared_ready")
        silu_done = st.sem("silu_done")
        h_done = st.sem("h_done")
        shared_out = st.sem("shared_out")
        out_done = st.sem("out_done")
        stored = [st.pool_dma_sem(64 * (NB // 2)) for s in range(2)]
        w_stored = [st.pool_dma_sem(64 * (NB // 2)) for s in range(2)]
        dve = st.sem("dve")
        paced = st.sem("paced")
        slots_done = st.sem("slots_done")
        slots_stored = st.sem("slots_stored")
        with nc.Block() as block:
            @block.sync
            def _(sp):
                for dst, src in ((ident, "ident"), (wr, "L3_router"), (wsg, "L3_wsg"), (wsd, "L3_wsd"), (ramp, "L3_ramp")):
                    sp.dma_start(dst[:], W[src]).then_inc(const_in, 16)
                sp.dma_start(slot_no[:], W["iota8"][0:EX, 0:CAP]).then_inc(const_in, 16)
                sp.dma_start(X[N:N + CAP], W["zero_rows"][:, 0:D]).then_inc(const_in, 16)
                sp.dma_start(XW[N:N + CAP], W["zero_rows"]).then_inc(const_in, 16)
                with sp.Fori(0, NB // 2) as i:
                    for s in range(2):
                        b = i * 2 + s
                        sp.wait_ge(in_free, b + 1)
                        sp.dma_start(xT[:, s], xnt[:, bass.ds(b * T, T)]).then_inc(x_in[s], 16)
                        load_tiles(sp, xt[:, s], X[0:N], b, False, res_in[s])
                sp.wait_ge(slots_done, 1)
                sp.dma_start(SLOT, toki[:]).then_inc(slots_stored, 16)
                sp.wait_ge(slots_stored, 16)
                sp.wait_ge(const_in, 128)

            @block.gpsimd
            def _(pool):
                wide = XW[0:N, D:ROWX].rearrange("(g p) c -> g p c", p=128)
                with pool.Fori(0, NB // 2) as i:
                    for s in range(2):
                        b = i * 2 + s
                        pool.wait_ge(chosen, b + 1)
                        for k in range(TILES):
                            pool.dma_start(wide[bass.ds(b * TILES + k, 1)].rearrange("o p c -> (o p) c"),
                                           wt[:, s, k]).then_inc(w_stored[s].sem, 16)
                        pool.wait_ge(out_done, b + 1 + 1)
                        store_tiles(pool, X[0:N], xo[:, s], b, False, stored[s].sem)
                for s in range(2):
                    stored[s].wait(pool, 64 * (NB // 2))
                    w_stored[s].wait(pool, 64 * (NB // 2))

            @block.tensor
            def _(pe):
                pe.wait_ge(const_in, 128)
                with pe.Fori(0, NB // 2) as i:
                    for s in range(2):
                        b = i * 2 + s
                        pe.wait_ge(x_in[s], i * 16 + 16)
                        pe.wait_ge(out_done, b + 1)
                        for k in range(TILES):
                            ins = pe.matmul(psL[:, k * EX:(k + 1) * EX], xT[:, s, k * 128:(k + 1) * 128], wr[:], start=True,
                                            stop=True)
                        ins.then_inc(logits_ready, 1)
                        pe.matmul(psG[0:FX], wsg[:, 0:FX], xT[:, s], start=True, stop=True)
                        pe.matmul(psU[0:FX], wsg[:, FX:2 * FX], xT[:, s], start=True, stop=True).then_inc(shared_ready, 1)
                        pe.wait_ge(h_done, b + 1)
                        for k in range(TILES):
                            ins = pe.matmul(psO[:, k * D:(k + 1) * D], h[:, k * 128:(k + 1) * 128], wsd[:], start=True,
                                            stop=True)
                        ins.then_inc(shared_out, 1)
                        pe.wait_ge(chosen, b + 1)
                        pe.sem_inc(paced, 1)
                        for k in range(TILES):
                            ins = pe.transpose(psM[0:EX, k * 128:(k + 1) * 128], mk[:, s, k], ident[:])
                        ins.then_inc(choice_turned, 1)

            @block.scalar
            def _(a):
                with a.Fori(0, NB // 2) as i:
                    for s in range(2):
                        b = i * 2 + s
                        a.wait_ge(shifted, b + 1)
                        a.activation(ex[:], lg[:], ACT.Exp).then_inc(exps_done, 1)
                        a.wait_ge(shared_ready, b + 1)
                        a.activation(sg[:], psG[0:FX], ACT.Silu).then_inc(silu_done, 1)

            @block.vector
            def _(v):
                v.sem_inc(in_free, 2)
                v.sem_inc(out_done, 1)
                v.sem_inc(choice_turned, 1)
                v.wait_ge(const_in, 128)
                with v.Fori(0, NB // 2) as i:
                    STEPS = [0]
                    PER = 2 * 9

                    def link(ins):
                        STEPS[0] += 1
                        ins.then_inc(dve, 1)
                        v.wait_ge(dve, i * PER + STEPS[0])
                        v.sem_inc(paced, 1)

                    for s in range(2):
                        b = i * 2 + s
                        v.wait_ge(logits_ready, b + 1)
                        L = psL[:, 0:TILES * EX].rearrange("p (k e) -> p k e", k=TILES)
                        link(v.tensor_reduce(mx[:], L, AX.X, ALU.max))
                        v.tensor_tensor(lg[:], L, bc(mx[:], EX), ALU.subtract).then_inc(shifted, 1)
                        v.wait_ge(exps_done, b + 1)
                        link(v.tensor_reduce(sm[:], ex[:], AX.X, ALU.add))
                        link(v.reciprocal(ri[:], sm[:]))
                        link(v.tensor_tensor(pr[:], ex[:], bc(ri[:], EX), ALU.mult))
                        for k in range(TILES):
                            ins = v.max(v8[:, k], pr[:, k])
                        link(ins)
                        for k in range(TILES):
                            ins = v.match_replace(left[:, k], v8[:, k], pr[:, k], -1.0)
                        v.tensor_reduce(sm[:], v8[:], AX.X, ALU.add)
                        link(ins)
                        v.wait_ge(choice_turned, b + 1)
                        w_stored[s].wait(v, i * 64)
                        link(v.tensor_scalar(mk[:, s], left[:], 0.0, None, ALU.is_lt))
                        link(v.reciprocal(ri[:], sm[:]))
                        link(v.tensor_tensor(left[:], pr[:], mk[:, s], ALU.mult))
                        v.tensor_tensor(wt[:, s], left[:], bc(ri[:], EX), ALU.mult).then_inc(chosen, 1)
                        v.wait_ge(silu_done, b + 1)
                        v.tensor_tensor(h[:], sg[:], psU[0:FX], ALU.mult).then_inc(h_done, 1)
                        v.wait_ge(choice_turned, b + 1 + 1)
                        v.tensor_tensor(order[0][:, bass.ds(b * T, T)], psM[0:EX], ramp[:, bass.ds(b * T, T)],
                                        ALU.mult).then_inc(choice_kept, 1)
                        v.wait_ge(shared_out, b + 1)
                        v.wait_ge(res_in[s], i * 64 + 64)
                        stored[s].wait(v, i * 64)
                        v.scalar_tensor_tensor(out=xo[:, s], in0=psO[:].rearrange("p (k d) -> p k d", k=TILES), scalar=0.5,
                                               in1=xt[:, s], op0=ALU.mult, op1=ALU.add).then_inc(out_done, 1)
                        v.wait_ge(out_done, b + 1 + 1)
                        v.wait_ge(choice_kept, b + 1)
                        v.sem_inc(in_free, 1)
                assert STEPS[0] == PER, (STEPS[0], PER)
                done = PER * (NB // 2)
                for c in range(CAP // 8):
                    part = top[:, 8 * c:8 * c + 8]
                    v.max(part, order[c % 2][:]).then_inc(dve, 1)
                    v.wait_ge(dve, done + 2 * c + 1)
                    v.match_replace(order[1 - c % 2][:], part, order[c % 2][:], 0.0).then_inc(dve, 1)
                    v.wait_ge(dve, done + 2 * c + 2)
                done += 2 * (CAP // 8)
                v.tensor_scalar(none[:], top[:], 0.0, None, ALU.is_equal).then_inc(dve, 1)
                v.wait_ge(dve, done + 1)
                v.tensor_tensor(none[:], none[:], slot_no[:], ALU.mult).then_inc(dve, 1)
                v.wait_ge(dve, done + 2)
                v.tensor_tensor(tok[:], none[:], top[:], ALU.subtract).then_inc(dve, 1)
                v.wait_ge(dve, done + 3)
                v.tensor_scalar(toki[:], tok[:], float(N), None, ALU.add).then_inc(slots_done, 1)


def experts64(nc, name, W, XW, X, SLOT):
    with Stage(nc, name) as st:
        ident = st.sb("ident", [128, 128])
        idx = st.sb("idx", [CAP, 4, 1], I32)
        xg = st.sb("xg", [CAP, 2, ROWX])
        xgT = st.sb("xgT", [128, 2, CAP])
        wgu = st.sb("wgu", [128, 2, 2, FX])
        wd = st.sb("wd", [FX, 2, D])
        wv = st.sb("wv", [CAP, 2])
        sg = st.sb("sg", [FX, 2, CAP])
        h = st.sb("h", [FX, 2, CAP])
        y = st.sb("y", [CAP, 4, D])
        psT = [st.ps(f"psT{s}") for s in range(2)]
        psH = [st.ps(f"psH{s}") for s in range(2)]
        psY = [st.ps(f"psY{s}") for s in range(2)]
        const_in = st.sem("const_in")
        idx_in = [st.sem(f"idx_in{s}") for s in range(4)]
        w_in = [st.sem(f"w_in{s}") for s in range(2)]
        gathered = [st.pool_dma_sem(16 * EX // 2) for s in range(2)]
        turned = st.sem("turned")
        turned_copied = st.sem("turned_copied")
        up_done = st.sem("up_done")
        silu_done = st.sem("silu_done")
        h_done = st.sem("h_done")
        down_done = st.sem("down_done")
        picked = st.sem("picked")
        y_done = st.sem("y_done")
        added = st.pool_dma_sem(16 * EX)
        paced = st.sem("paced")
        with nc.Block() as block:
            @block.sync
            def _(sp):
                sp.dma_start(ident[:], W["ident"]).then_inc(const_in, 16)
                with sp.Fori(0, EX // 4) as i:
                    for s in range(4):
                        e = i * 4 + s
                        added.wait(sp, i * 64 + 16 * s)
                        sp.dma_start(idx[:, s], SLOT[bass.ds(e, 1)].rearrange("o c -> c o")).then_inc(idx_in[s], 16)
                        if s >= 2:
                            sp.wait_ge(down_done, e - 1 + 1)
                        else:
                            sp.wait_ge(down_done, i * 4 + 1)
                        sp.dma_start(wgu[:, s % 2], W["L3_wgu"][:, bass.ds(e, 1)].rearrange("p o a f -> p (o a) f")).then_inc(w_in[s % 2], 16)
                        sp.dma_start(wd[:, s % 2], W["L3_wd"][bass.ds(e, 1)].rearrange("o f d -> (o f) d")).then_inc(w_in[s % 2], 16)

            @block.gpsimd
            def _(pool):
                with pool.Fori(0, EX // 4) as i:
                    for s in range(4):
                        e = i * 4 + s
                        pool.wait_ge(idx_in[s], i * 16 + 16)
                        if s >= 2:
                            pool.wait_ge(turned, e - 1 + 1)
                            pool.wait_ge(picked, e - 1 + 1)
                        else:
                            pool.wait_ge(turned, i * 4 + 1)
                            pool.wait_ge(picked, i * 4 + 1)
                        pool.sem_inc(paced, 1)
                        pool.indirect_dma_start(out=xg[:, s % 2], out_offset=None, in_=XW,
                                                in_offset=bass.IndirectOffsetOnAxis(ap=idx[:, s], axis=0)
                                                ).then_inc(gathered[s % 2].sem, 16)
                        pool.wait_ge(y_done, e + 1)
                        added.wait(pool, e * 16)
                        pool.sem_inc(paced, 1)
                        pool.indirect_dma_start(out=X, out_offset=bass.IndirectOffsetOnAxis(ap=idx[:, s], axis=0),
                                                in_=y[:, s], in_offset=None, compute_op=ALU.add).then_inc(added.sem, 16)
                added.wait(pool, EX * 16)

            @block.tensor
            def _(pe):
                pe.wait_ge(const_in, 16)
                with pe.Fori(0, EX // 4) as i:
                    for s in range(4):
                        e = i * 4 + s
                        q = s % 2
                        gathered[q].wait(pe, (i * 2 + s // 2) * 16 + 16)
                        pe.sem_inc(paced, 1)
                        pe.transpose(psT[q][:, 0:CAP], xg[:, q, 0:D], ident[0:CAP, 0:CAP]).then_inc(turned, 1)
                        pe.wait_ge(turned_copied, e + 1)
                        pe.wait_ge(w_in[q], (i * 2 + s // 2) * 32 + 32)
                        pe.matmul(psH[q][0:FX, 0:CAP], wgu[:, q, 0], xgT[:, q], start=True, stop=True)
                        pe.matmul(psH[q][0:FX, CAP:2 * CAP], wgu[:, q, 1], xgT[:, q], start=True, stop=True).then_inc(up_done, 1)
                        pe.wait_ge(h_done, e + 1)
                        pe.matmul(psY[q][0:CAP, 0:D], h[:, q], wd[:, q], start=True, stop=True).then_inc(down_done, 1)

            @block.scalar
            def _(a):
                with a.Fori(0, EX // 4) as i:
                    for s in range(4):
                        e = i * 4 + s
                        a.wait_ge(up_done, e + 1)
                        a.activation(sg[:, s % 2], psH[s % 2][0:FX, 0:CAP], ACT.Silu).then_inc(silu_done, 1)

            @block.vector
            def _(v):
                v.sem_inc(down_done, 1)
                v.sem_inc(turned, 1)
                v.sem_inc(picked, 1)
                with v.Fori(0, EX // 4) as i:
                    for s in range(4):
                        e = i * 4 + s
                        q = s % 2
                        v.wait_ge(turned, e + 1 + 1)
                        v.tensor_copy(xgT[:, q], psT[q][:, 0:CAP]).then_inc(turned_copied, 1)
                        v.tensor_copy(wv[:, q:q + 1], xg[:, q, bass.ds(e + D, 1)]).then_inc(picked, 1)
                        v.wait_ge(silu_done, e + 1)
                        v.tensor_tensor(h[:, q], sg[:, q], psH[q][0:FX, CAP:2 * CAP], ALU.mult).then_inc(h_done, 1)
                        v.wait_ge(down_done, e + 1 + 1)
                        v.wait_ge(picked, e + 1 + 1)
                        added.wait(v, i * 64)
                        v.tensor_scalar(y[:, s], psY[q][0:CAP, 0:D], wv[:, q:q + 1], 0.5, ALU.mult,
                                        ALU.mult).then_inc(y_done, 1)


RW = 511


def skewed(row, base, n):
    full = row.rearrange("o n -> (o n)")
    sub = full[base:base + 128 * (RW - 1)].rearrange("(p w) -> p w", w=RW - 1)
    return sub[:, 0:n]


def relative(nc, name, W, xnt, PR):
    U = TILES * HEADS
    with Stage(nc, name) as st:
        wq = st.sb("wq", [128, 4, 128])
        bq = st.sb("bq", [128, 4])
        wrel = st.sb("wrel", [128, RW])
        xT = st.sb("xT", [128, 2, T])
        q = st.sb("q", [128, 4, T])
        rp = st.sb("rp", [128, 4, RW])
        psP = [st.ps(f"psP{i}") for i in range(2)]
        psR = [st.ps(f"psR{i}") for i in range(4)]
        const_in = st.sem("const_in")
        x_in = [st.sem(f"x_in{s}") for s in range(2)]
        in_free = st.sem("in_free")
        proj_done = st.sem("proj_done")
        q_copied = st.sem("q_copied")
        rel_ready = st.sem("rel_ready")
        rel_copied = st.sem("rel_copied")
        rel_stored = [st.sem(f"rel_stored{j}") for j in range(4)]
        with nc.Block() as block:
            @block.sync
            def _(sp):
                sp.dma_start(wq[:].rearrange("p a b -> p (a b)"), W["A0_wq"]).then_inc(const_in, 16)
                sp.dma_start(bq[:], W["A0_bq"]).then_inc(const_in, 16)
                sp.dma_start(wrel[:], W["A0_wrel"]).then_inc(const_in, 16)
                with sp.Fori(0, NB // 2) as i:
                    for s in range(2):
                        b = i * 2 + s
                        sp.wait_ge(in_free, b + 1)
                        sp.dma_start(xT[:, s], xnt[:, bass.ds(b * T, T)]).then_inc(x_in[s], 16)
                        for u in range(U):
                            sp.wait_ge(rel_copied, b * U + u + 1 + 1)
                            dst = PR[bass.ds(b * U + u, 1), 0:128 * RW].rearrange("o (p w) -> (o p) w", w=RW)
                            sp.dma_start(dst, rp[:, u % 4]).then_inc(rel_stored[u % 4], 16)
                for j in range(4):
                    sp.wait_ge(rel_stored[j], NB * U // 4 * 16 + 16)

            @block.tensor
            def _(pe):
                pe.sem_inc(in_free, 2)
                pe.wait_ge(const_in, 48)
                with pe.Fori(0, NB // 2) as i:
                    for s in range(2):
                        b = i * 2 + s
                        pe.wait_ge(x_in[s], i * 16 + 16)
                        for m in range(4):
                            if m >= 2:
                                pe.wait_ge(q_copied, b * 4 + m - 1)
                            ins = pe.matmul(psP[m % 2][:], wq[:, m], xT[:, s], start=True, stop=True)
                            ins.then_inc(proj_done, 1)
                        pe.wait_ge(q_copied, b * 4 + 4)
                        pe.sem_inc(in_free, 1)
                        for u in range(U):
                            it, h = divmod(u, HEADS)
                            m, g = divmod(h, 4)
                            if u >= 4:
                                pe.wait_ge(rel_copied, b * U + u - 3 + 1)
                            else:
                                pe.wait_ge(rel_copied, b * U + 1)
                            r = slice(32 * g, 32 * g + 9)
                            pe.matmul(psR[u % 4][:, 0:RW], q[r, m, it * 128:(it + 1) * 128], wrel[r],
                                      start=True, stop=True).then_inc(rel_ready, 1)

            @block.vector
            def _(v):
                v.wait_ge(const_in, 48)
                with v.Fori(0, NB // 2) as i:
                    for s in range(2):
                        b = i * 2 + s
                        for m in range(4):
                            v.wait_ge(proj_done, b * 4 + m + 1)
                            v.tensor_scalar(q[:, m], psP[m % 2][:], bq[:, m:m + 1], None, ALU.add).then_inc(q_copied, 1)

            @block.scalar
            def _(a):
                a.sem_inc(rel_copied, 1)
                for j in range(4):
                    a.sem_inc(rel_stored[j], 16)
                with a.Fori(0, NB // 2) as i:
                    for s in range(2):
                        b = i * 2 + s
                        for u in range(U):
                            a.wait_ge(rel_ready, b * U + u + 1)
                            if u >= 4:
                                a.wait_ge(rel_stored[u % 4], (b * (U // 4) + u // 4) * 16 + 16)
                            else:
                                a.wait_ge(rel_stored[u % 4], b * (U // 4) * 16 + 16)
                            a.activation(rp[:, u % 4], psR[u % 4][:, 0:RW], ACT.Copy, scale=-1.0).then_inc(rel_copied, 1)


NCON = {"L0": 4, "L1": 7, "L2": 3}


def name_of(kind, what):
    return f"{kind}_{what}"


def stage_L0_ffn(nc, W, X, S):
    prep(nc, "p0", W, X, S["XNT"], route=dict(ROUTES["L0"], w="L0_router", b="L0_router_b", table=S["GT"]))
    moe(nc, "m0", W, "L0", X, S["XNT"], S["GT"])


def stage_L1_ffn(nc, W, X, S):
    prep(nc, "p1", W, X, S["XNT"], xn=S["XN"], permuted=True)
    attention(nc, "a1", W, "block", S["XNT"], S, S["XN"], S["Y"])
    prep(nc, "q1", W, S["Y"], S["XNT"], xn=S["H"], affine=("L1_ln1_g", "L1_ln1_b"),
         route=dict(ROUTES["L1"], w="L1_router", b="L1_router_b", table=S["GT"]))
    moe(nc, "m1", W, "L1", X, S["XNT"], S["GT"], hn=S["H"], permuted=True)


def stage_L2_ffn(nc, W, X, S):
    prep(nc, "p2", W, X, S["XNT"], route=dict(ROUTES["L2"], w="L2_router", b="L2_router_b", table=S["GT"]))
    moe(nc, "m2", W, "L2", X, S["XNT"], S["GT"])


def stage_L0_attn(nc, W, X, S):
    prep(nc, "p4", W, X, S["XNT"])
    relative(nc, "r0", W, S["XNT"], S["PR"])
    attention(nc, "a0", W, "rel", S["XNT"], S, X, X)


def stage_L1_attn(nc, W, X, S):
    prep(nc, "p3", W, X, S["XNT"])
    attention(nc, "a2", W, "causal", S["XNT"], S, X, X)


def stage_L2_attn(nc, W, X, S):
    polar(nc, "po", W, S["PT"])
    prep(nc, "p6", W, X, S["XNT"])
    scan_attention(nc, "sc", W, S["XNT"], X, S["PT"])


def stage_L3_attn(nc, W, X, S):
    prep(nc, "p5", W, X, S["XNT"])
    attention(nc, "a3", W, "plain", S["XNT"], S, X, X)


def stage_L3_ffn(nc, W, X, S):
    prep(nc, "p7", W, X, S["XNT"], xn=S["XW"][0:N, 0:D])
    route64(nc, "r3", W, S["XNT"], S["XW"], S["Xfull"], S["SLOT"])
    experts64(nc, "e3", W, S["XW"], S["Xfull"], S["SLOT"])


STAGES = [stage_L0_ffn, stage_L0_attn, stage_L0_ffn, stage_L1_ffn, stage_L1_attn, stage_L1_ffn,
          stage_L2_ffn, stage_L2_attn, stage_L2_ffn, stage_L3_ffn, stage_L3_attn, stage_L3_ffn]


def copy_dram(nc, name, dst, src, n):
    with Stage(nc, name) as st:
        done = st.sem("done")
        with nc.Block() as block:
            @block.sync
            def _(sp):
                sp.dma_start(dst, src).then_inc(done, 16)
                sp.wait_ge(done, 16)


def copy_in(nc, X, x):
    part = N // 4
    with Stage(nc, "cin") as st:
        with nc.Block() as block:
            @block.gpsimd
            def _(pool):
                for j in range(4):
                    pool.dma_start(X[j * part:(j + 1) * part], x[j * part:(j + 1) * part]).then_inc(Stage.pool_dma[j], 16)
                for j in range(4):
                    pool.wait_ge(Stage.pool_dma[j], 16)


def program(nc, W, out, stages):
    full = nc.dram_tensor("X", [N + CAP, D], F32).ap()
    X = full[0:N]
    S = {
        "Xfull": full,
        "XW": nc.dram_tensor("XW", [N + CAP, ROWX], F32).ap(),
        "SLOT": nc.dram_tensor("SLOT", [EX, CAP], I32).ap(),
        "PT": nc.dram_tensor("PT", [2, 128, 128], F32).ap(),
        "XNT": nc.dram_tensor("XNT", [D, N], F32).ap(),
        "XN": nc.dram_tensor("XN", [N, D], F32).ap(),
        "H": nc.dram_tensor("H", [N, D], F32).ap(),
        "Y": nc.dram_tensor("Y", [N, D], F32).ap(),
        "PR": nc.dram_tensor("PR", [NB * TILES * HEADS, 128 * RW + 128], F32).ap(),
        "GT": nc.dram_tensor("GT", [27, N], F32).ap(),
    }
    with ExitStack() as ctx:
        Stage.count = 0
        Stage.pool_dma_count = [16] * 4
        Stage.pool_dma = [ctx.enter_context(nc.semaphore(f"pool_dma{j}")) for j in range(4)]
        copy_in(nc, X, W["x"])
        for stage in stages:
            stage(nc, W, X, S)
        copy_dram(nc, "cout", out, X, N)


def layout(inputs):
    f = np.float32
    I = {k: np.asarray(v) for k, v in inputs.items()}
    w = {"x": I["L0_attn_x"].reshape(N, D)}
    w["ident"] = np.eye(128, dtype=f)
    w["iota8"] = np.ascontiguousarray(np.broadcast_to(np.arange(64, dtype=f), (128, 64)))
    w["L0_router"] = np.concatenate([I["L0_ffn_gate_w"], I["L0_ffn_shared_expert_gate_w"]]).T
    w["L0_router_b"] = np.zeros((1, 9), f)
    gu = I["L0_ffn_experts_gate_up"]
    w["L0_w1"] = np.concatenate([gu[:, :176].reshape(1408, D), I["L0_ffn_shared_gate_w"]]).T
    w["L0_wu"] = np.concatenate([gu[:, 176:].reshape(1408, D), I["L0_ffn_shared_up_w"]]).T
    w["L0_w2"] = np.concatenate([I["L0_ffn_experts_down"].transpose(0, 2, 1).reshape(1408, D),
                                 I["L0_ffn_shared_down_w"].T, np.zeros((32, D), f)])
    sel = np.zeros((27, 14 * 128), f)
    for r in range(1760):
        e = min(r // 176, 8)
        sel[[e, 9 + e, 18 + e], r] = 1
    w["L0_sel"] = sel
    w["L1_router"] = I["L1_ffn_router_w"].T
    w["L1_router_b"] = I["L1_ffn_router_b"].reshape(1, 8)
    w["L1_w1"] = I["L1_ffn_w1"].transpose(2, 0, 1).reshape(D, 1024)
    w["L1_w2"] = I["L1_ffn_w2"].transpose(0, 2, 1).reshape(1024, D)
    w["L1_b1"] = I["L1_ffn_b1"].T
    w["L1_b2"] = I["L1_ffn_b2"]
    w["L1_sel"] = np.repeat(np.eye(8, dtype=f), 128, 1)
    for k in ("ln1_g", "ln1_b", "ln2_g", "ln2_b"):
        w[f"L1_{k}"] = I[f"L1_ffn_{k}"].reshape(1, D)
    w["L2_router"] = I["L2_ffn_router_w"].T
    w["L2_router_b"] = np.zeros((1, 8), f)
    w["L2_w1"] = I["L2_ffn_expert_fc"].transpose(1, 0, 2).reshape(D, 4096)
    w["L2_w2"] = I["L2_ffn_expert_proj"].transpose(0, 2, 1).reshape(4096, D)
    w["L2_sel"] = w["L1_sel"]
    p1, p2 = I["L2_attn_Wp1"], I["L2_attn_Wp2"]
    w["P_w"] = np.stack([p1, p1.T, p2, p2.T])
    w["S_wq"], w["S_wv"], w["S_wc"] = I["L2_attn_Wq"].T, I["L2_attn_Wv"].T, I["L2_attn_Wc"].T
    w["S_first"] = I["L2_attn_identity"].reshape(D, 1)
    w["S_mean"] = np.full((D, D), 1 / D, f)
    w["L3_router"] = I["L3_ffn_router_w"].T
    w["L3_wsg"], w["L3_wsd"] = I["L3_ffn_ws_gate_up"], I["L3_ffn_ws_down"]
    w["L3_ramp"] = np.broadcast_to(N - np.arange(N, dtype=f), (EX, N))
    w["L3_wgu"] = np.stack([I["L3_ffn_w_gate"], I["L3_ffn_w_up"]], 2).transpose(1, 0, 2, 3)
    w["L3_wd"] = I["L3_ffn_w_down"]
    w["zero_rows"] = np.zeros((CAP, ROWX), f)

    def heads4(rows, cols=None):
        o = np.zeros((D, 4, 128), f)
        for hh in range(HEADS):
            m, g = divmod(hh, 4)
            o[:, m, 32 * g:32 * g + HD] = rows[hh].T
        return o.reshape(D, 512)

    def bias4(rows, one=0.0):
        o = np.zeros((128, 4), f)
        for hh in range(HEADS):
            m, g = divmod(hh, 4)
            o[32 * g:32 * g + HD, m] = rows[hh]
            o[32 * g + HD, m] = one
        return o

    zero = np.zeros((HEADS, HD), f)
    a0 = I["L0_attn_Wqkv"].reshape(HEADS, 3, HD, D)
    b0 = I["L0_attn_bqkv"].reshape(HEADS, 3, HD)
    w["A0_wq"], w["A0_wk"] = heads4(a0[:, 0]), heads4(a0[:, 1])
    w["A0_bq"], w["A0_bk"] = bias4(b0[:, 0], 1.0), bias4(b0[:, 1])
    w["A0_wv"], w["A0_bv"] = a0[:, 2].reshape(128, D).T, b0[:, 2].reshape(1, 128)
    rel = np.concatenate([I["L0_attn_Wr"], I["L0_attn_br"][:, None]], 1)
    far = np.zeros((128, 2), f)
    wrel = np.zeros((128, 511), f)
    span = np.clip(np.arange(-255, 256), -128, 128) + 128
    for g in range(4):
        far[32 * g:32 * g + 9, 0], far[32 * g:32 * g + 9, 1] = rel[0], rel[256]
        wrel[32 * g:32 * g + 9] = rel[span].T
    w["A0_far"], w["A0_wrel"] = far, wrel
    a1 = I["L1_ffn_in_proj_w"].reshape(3, HEADS, HD, D)
    b1 = I["L1_ffn_in_proj_b"].reshape(3, HEADS, HD)
    w["A1_wq"], w["A1_wk"] = heads4(a1[0]), heads4(a1[1])
    w["A1_bq"], w["A1_bk"] = bias4(b1[0]), bias4(b1[1])
    w["A1_wv"], w["A1_bv"] = a1[2].reshape(128, D).T, b1[2].reshape(1, 128)
    w["A1_wo"], w["A1_bo"] = I["L1_ffn_out_w"].T, I["L1_ffn_out_b"].reshape(1, D)
    token = np.arange(128)
    apart = (token[:, None] % 16 != token[None] % 16)
    w["A1_mask"] = np.tile(np.where(apart, f(BIG), f(0)), (1, 4)).astype(f)
    w["A2_wq"] = heads4(I["L1_attn_Wq"].T.reshape(HEADS, HD, D))
    w["A2_wk"] = heads4(I["L1_attn_Wk"].T.reshape(HEADS, HD, D))
    w["A2_bq"] = w["A2_bk"] = bias4(zero)
    w["A2_wv"], w["A2_wo"] = I["L1_attn_Wv"], I["L1_attn_Wo"]
    w["A2_mask"] = np.concatenate([np.zeros((128, 384), f), np.where(token[None] > token[:, None], f(BIG), f(0))], 1)
    w["A3_wq"], w["A3_wk"] = heads4(I["L3_attn_Wq"]), heads4(I["L3_attn_Wk"])
    w["A3_bq"], w["A3_bk"] = bias4(I["L3_attn_bq"]), bias4(I["L3_attn_bk"])
    w["A3_wv"], w["A3_bv"] = I["L3_attn_Wv"].reshape(128, D).T, I["L3_attn_bv"].reshape(1, 128)
    w["A3_wo"], w["A3_bo"] = I["L3_attn_Wo"].T, I["L3_attn_bo"].reshape(1, D)
    return {k: np.ascontiguousarray(v) for k, v in w.items()}


def kernel(**inputs):
    import concourse.bacc as _bacc
    from concourse.bass_utils import run_bass_kernel_spmd as _run

    nc = _bacc.Bacc("TRN2", target_bir_lowering=False, num_devices=1)
    arrays, W = {}, {}
    for name, a in layout(inputs).items():
        arrays[f"in_{name}_dram"] = a
        W[name] = nc.dram_tensor(f"in_{name}_dram", a.shape, mybir.dt.from_np(a.dtype), kind="ExternalInput").ap()
    out = nc.dram_tensor("out_0_dram", [N, D], F32, kind="ExternalOutput").ap()
    program(nc, W, out, STAGES)
    r = _run(nc, [arrays], core_ids=[0])
    return r.results[0]["out_0_dram"].reshape(NB, T, D)
```

```python
import numpy as np
import concourse.bass as bass
from concourse import mybir
from contextlib import ExitStack

F32 = mybir.dt.float32
BF16 = mybir.dt.bfloat16
U32 = mybir.dt.uint32
I32 = mybir.dt.int32
ALU = mybir.AluOpType
ACT = mybir.ActivationFunctionType
AX = mybir.AxisListType

NB, T, D = 8, 512, 128
N = NB * T
TILES = T // 128
HEADS, HD = 16, 8
BIG = 1e30


class PoolDmaCount:
    def __init__(self, sem, base):
        self.sem, self.base = sem, base

    def wait(self, eng, n):
        eng.wait_ge(self.sem, self.base + n)


class Stage:

    count = 0

    def __init__(self, nc, name):
        Stage.count += 1
        self.taken = 0
        self.nc, self.name, self.ctx, self.sems = nc, f"{name}_{Stage.count}", ExitStack(), []

    def __enter__(self):
        self.ctx.__enter__()
        return self

    def sb(self, name, shape, dt=F32):
        return self.ctx.enter_context(self.nc.sbuf_tensor(f"{self.name}_{name}", shape, dt))

    def ps(self, name, shape=(128, 512), dt=F32):
        return self.ctx.enter_context(self.nc.psum_tensor(f"{self.name}_{name}", list(shape), dt))

    def sem(self, name):
        s = self.ctx.enter_context(self.nc.semaphore(f"{self.name}_{name}"))
        self.sems.append(s)
        return s

    def pool_dma_sem(self, total):
        c = PoolDmaCount(Stage.pool_dma[self.taken], Stage.pool_dma_count[self.taken])
        Stage.pool_dma_count[self.taken] += total
        self.taken += 1
        return c

    def __exit__(self, *a):
        if a[0] is not None:
            return self.ctx.__exit__(*a)
        if not self.sems:
            self.nc.all_engine_barrier()
            return self.ctx.__exit__(*a)
        ids = sorted(s.num for s in self.sems)
        cleared = range(ids[0], ids[-1] + 1)
        assert not any(s in cleared for s in self.nc.barrier_sems)
        self.nc.all_engine_barrier(sems_to_clear=cleared)
        return self.ctx.__exit__(*a)


def token_rows(dram, permuted):
    if permuted:
        return dram.rearrange("(t g n) c -> g t n c", t=NB, n=128 // NB)
    return dram.rearrange("(g p) c -> g p c", p=128)


def load_tiles(eng, dst, dram, b, permuted, sem):
    v = token_rows(dram, permuted)
    for k in range(TILES):
        src = v[bass.ds(b * TILES + k, 1)]
        if permuted:
            eng.dma_start(dst[:, k, :], src.rearrange("o t n c -> (o t) n c")).then_inc(sem, 16)
        else:
            eng.dma_start(dst[:, k, :], src.rearrange("o p c -> (o p) c")).then_inc(sem, 16)


def store_tiles(eng, dram, src, b, permuted, sem):
    v = token_rows(dram, permuted)
    for k in range(TILES):
        dst = v[bass.ds(b * TILES + k, 1)]
        if permuted:
            eng.dma_start(dst.rearrange("o t n c -> (o t) n c"), src[:, k, :]).then_inc(sem, 16)
        else:
            eng.dma_start(dst.rearrange("o p c -> (o p) c"), src[:, k, :]).then_inc(sem, 16)


def bc(ap, n):
    return ap.unsqueeze(2).to_broadcast([ap.shape[0], ap.shape[1], n])


def prep(nc, name, W, src, xnt, xn=None, permuted=False, affine=None, route=None, eps=1e-5):
    with Stage(nc, name) as st:
        xt = st.sb("xt", [128, 2, TILES, D])
        stats = st.sb("stats", [128, 2, TILES, 6])
        mv = st.sb("mv", [128, 2, TILES, 2])
        vare = st.sb("vare", [128, 2, TILES])
        rstd = st.sb("rstd", [128, 2, TILES])
        half = st.sb("half", [128, TILES])
        y = st.sb("y", [128, 2, TILES, D])
        yT = st.sb("yT", [128, 2, T])
        ident = st.sb("ident", [128, 128])
        psY = [st.ps(f"psY{i}") for i in range(2)]
        if affine:
            gb = st.sb("gb", [128, 2, D])
            z = st.sb("z", [128, 2, TILES, D])
        kind = route and route["kind"]
        if route:
            E, R, G = route["experts"], route["rows"], route["parts"]
            wr = st.sb("wr", [128, R])
            rb = st.sb("rb", [128, R])
            AT = NB * TILES
            iota = st.sb("iota", [128, AT, E])
            psL = st.ps("psL")
            psG = [st.ps(f"psG{i}") for i in range(4)]
            lg = st.sb("lg", [128, AT, R])
            mx = st.sb("mx", [128, AT])
            ex = st.sb("ex", [128, AT, E])
            sm = st.sb("sm", [128, AT])
            ri = st.sb("ri", [128, AT])
            pr = st.sb("pr", [128, AT, E])
            v8 = st.sb("v8", [128, AT, 8])
            i8 = st.sb("i8", [128, AT, 8], U32)
            fi = st.sb("fi", [128, AT, 2])
            pick = st.sb("pick", [128, AT])
            m0 = st.sb("m0", [128, AT, E])
            m1 = st.sb("m1", [128, AT, E])
            gt = st.sb("gt", [128, AT, R])
            sg = st.sb("sg", [128, AT, 1])
            hi = st.sb("hi", [128, AT, R], BF16)
            res = st.sb("res", [128, AT, R])
            parts = st.sb("parts", [128, AT, G * R])
            gT = st.sb("gT", [G * R, NB, T])
        const_in = st.sem("const_in")
        x_in = [st.sem(f"x_in{s}") for s in range(2)]
        x_free = st.sem("x_free")
        y_done = st.sem("y_done")
        y_stored = [st.pool_dma_sem(64 * (NB // 2) if xn is not None else 0) for s in range(2)]
        yT_ready = st.sem("yT_ready")
        yT_copied = st.sem("yT_copied")
        yT_stored = [st.sem(f"yT_stored{s}") for s in range(2)]
        var_done = st.sem("var_done")
        rstd_done = st.sem("rstd_done")
        dve = st.sem("dve")
        paced = st.sem("paced")
        half_set = st.sem("half_set")
        logits_ready = st.sem("logits_ready")
        shifted = st.sem("shifted")
        exps_done = st.sem("exps_done")
        gates_done = st.sem("gates_done")
        gates_turned = st.sem("gates_turned")
        gates_copied = st.sem("gates_copied")
        gates_stored = st.sem("gates_stored")
        NCONST = 1 + (2 if affine else 0) + (3 if route else 0)

        with nc.Block() as block:
            @block.sync
            def _(sp):
                sp.dma_start(ident[:], W["ident"]).then_inc(const_in, 16)
                if affine:
                    for j in range(2):
                        sp.dma_start(gb[:, j, :], W[affine[j]].to_broadcast([128, D])).then_inc(const_in, 16)
                if route:
                    sp.dma_start(wr[:], W[route["w"]]).then_inc(const_in, 16)
                    sp.dma_start(rb[:], W[route["b"]].to_broadcast([128, R])).then_inc(const_in, 16)
                    sp.dma_start(iota[:], W["iota8"][:, 0:E].unsqueeze(1).to_broadcast([128, AT, E])).then_inc(const_in, 16)
                with sp.Fori(0, NB // 2) as i:
                    for s in range(2):
                        b = i * 2 + s
                        sp.wait_ge(x_free, b + 1)
                        load_tiles(sp, xt[:, s], src, b, permuted, x_in[s])

            @block.gpsimd
            def _(pool):
                pool.memset(half[:], -0.5).then_inc(half_set, 1)
                pool.wait_ge(half_set, 1)
                with pool.Fori(0, NB // 2) as i:
                    for s in range(2):
                        b = i * 2 + s
                        pool.wait_ge(var_done, b + 1)
                        pool.tensor_tensor(rstd[:, s], vare[:, s], half[:], ALU.pow).then_inc(rstd_done, 1)
                        if xn is not None:
                            pool.wait_ge(y_done, b + 1)
                            if affine:
                                store_tiles(pool, xn, z[:, s], b, False, y_stored[s].sem)
                            else:
                                store_tiles(pool, xn, y[:, s], b, False, y_stored[s].sem)
                if xn is not None:
                    for s in range(2):
                        y_stored[s].wait(pool, NB // 2 * 64)

            @block.vector
            def _(v):
                v.sem_inc(x_free, 2)
                v.wait_ge(const_in, 16 * NCONST)
                STEPS = [0]
                PER = 2 * (3 + (2 if affine else 0))

                def link(ins, done=0):
                    STEPS[0] += 1
                    ins.then_inc(dve, 1)
                    v.wait_ge(dve, done + STEPS[0])
                    v.sem_inc(paced, 1)

                with v.Fori(0, NB // 2) as i:
                    for s in range(2):
                        b = i * 2 + s
                        v.wait_ge(x_in[s], i * 64 + 64)
                        for k in range(TILES):
                            ins = v.bn_stats(stats[:, s, k], xt[:, s, k])
                        link(ins, i * PER)
                        for k in range(TILES):
                            ins = v.bn_aggr(mv[:, s, k], stats[:, s, k])
                        link(ins, i * PER)
                        v.tensor_scalar(vare[:, s], mv[:, s, :, 1], eps, None, ALU.add).then_inc(var_done, 1)
                        v.wait_ge(rstd_done, b + 1)
                        if not affine:
                            v.wait_ge(yT_ready, b + 1)
                            if xn is not None:
                                y_stored[s].wait(v, i * 64)
                        for k in range(TILES):
                            ins = v.tensor_scalar(y[:, s, k], xt[:, s, k], mv[:, s, k, 0:1], rstd[:, s, k:k + 1],
                                                  ALU.subtract, ALU.mult)
                        link(ins, i * PER)
                        v.sem_inc(x_free, 1)
                        if affine:
                            g = gb[:, 0:1, :].to_broadcast([128, TILES, D])
                            o = gb[:, 1:2, :].to_broadcast([128, TILES, D])
                            link(v.tensor_tensor(y[:, s], y[:, s], g, ALU.mult), i * PER)
                            v.wait_ge(yT_ready, b + 1)
                            if xn is not None:
                                y_stored[s].wait(v, i * 64)
                            link(v.tensor_tensor(z[:, s], y[:, s], o, ALU.add), i * PER)
                        v.sem_inc(y_done, 1)
                assert STEPS[0] == PER, (STEPS[0], PER)
                if not route:
                    return
                STEPS[0] = NB // 2 * PER
                v.wait_ge(logits_ready, NB + 2)
                L = psL[:, 0:AT * R].rearrange("p (k e) -> p k e", k=AT)
                link(v.tensor_tensor(lg[:], L, rb[:].unsqueeze(1).to_broadcast([128, AT, R]), ALU.add))
                link(v.tensor_reduce(mx[:], lg[:, :, 0:E], AX.X, ALU.max))
                link(v.tensor_tensor(lg[:, :, 0:E], lg[:, :, 0:E], bc(mx[:], E), ALU.subtract))
                v.sem_inc(shifted, 1)
                v.wait_ge(exps_done, 1)
                link(v.tensor_reduce(sm[:], ex[:], AX.X, ALU.add))
                link(v.reciprocal(ri[:], sm[:]))
                link(v.tensor_tensor(pr[:], ex[:], bc(ri[:], E), ALU.mult))
                for k in range(AT):
                    ins = v.max(v8[:, k], pr[:, k])
                link(ins)
                for k in range(AT):
                    ins = v.max_index(i8[:, k], v8[:, k], pr[:, k])
                link(ins)
                link(v.tensor_copy(fi[:], i8[:, :, 0:2]))
                if kind == "top2":
                    v.tensor_tensor(m0[:], iota[:], bc(fi[:, :, 0], E), ALU.is_equal)
                    link(v.tensor_tensor(m1[:], iota[:], bc(fi[:, :, 1], E), ALU.is_equal))
                    link(v.tensor_tensor(m0[:], m0[:], m1[:], ALU.add))
                    v.tensor_tensor(gt[:, :, 0:E], m0[:], pr[:], ALU.mult)
                    link(v.tensor_scalar(sg[:], sg[:], 1.0, None, ALU.add))
                    link(v.reciprocal(gt[:, :, E:R], sg[:]))
                elif kind == "top1":
                    link(v.tensor_tensor(gt[:], iota[:], bc(fi[:, :, 0], E), ALU.is_equal))
                else:
                    link(v.tensor_reduce(pick[:], fi[:], AX.X, ALU.max))
                    link(v.tensor_tensor(gt[:], iota[:], bc(pick[:], E), ALU.is_equal))
                if G == 1:
                    v.tensor_copy(parts[:], gt[:]).then_inc(gates_done, 1)
                else:
                    link(v.tensor_copy(hi[:], gt[:]))
                    v.tensor_copy(parts[:, :, 0:R], hi[:])
                    link(v.tensor_tensor(res[:], gt[:], hi[:], ALU.subtract))
                    link(v.tensor_copy(hi[:], res[:]))
                    v.tensor_copy(parts[:, :, R:2 * R], hi[:])
                    v.tensor_tensor(parts[:, :, 2 * R:3 * R], res[:], hi[:], ALU.subtract).then_inc(gates_done, 1)

            @block.tensor
            def _(pe):
                pe.sem_inc(yT_ready, 2)
                if route:
                    pe.sem_inc(logits_ready, 2)
                pe.wait_ge(const_in, 16 * NCONST)
                with pe.Fori(0, NB // 2) as i:
                    for s in range(2):
                        b = i * 2 + s
                        out = z if affine else y
                        pe.wait_ge(y_done, b + 1)
                        pe.wait_ge(yT_copied, b + 1)
                        for k in range(TILES):
                            ins = pe.transpose(psY[s][:, k * 128:(k + 1) * 128], out[:, s, k], ident[:])
                        ins.then_inc(yT_ready, 1)
                        if route:
                            pe.wait_ge(yT_copied, b + 3)
                            for k in range(TILES):
                                ins = pe.matmul(psL[:, bass.ds((b * TILES + k) * R, R)], yT[:, s, k * 128:(k + 1) * 128],
                                                wr[:], start=True, stop=True)
                            ins.then_inc(logits_ready, 1)
                if route:
                    pe.wait_ge(gates_done, 1)
                    for n in range(NB):
                        if n >= 4:
                            pe.wait_ge(gates_copied, n - 3)
                        for k in range(TILES):
                            ins = pe.transpose(psG[n % 4][0:G * R, k * 128:(k + 1) * 128], parts[:, n * TILES + k], ident[:])
                        ins.then_inc(gates_turned, 1)

            @block.scalar
            def _(a):
                a.sem_inc(yT_copied, 2)
                for s in range(2):
                    a.sem_inc(yT_stored[s], 16)
                with a.Fori(0, NB // 2) as i:
                    for s in range(2):
                        b = i * 2 + s
                        a.wait_ge(yT_ready, b + 3)
                        a.wait_ge(yT_stored[s], i * 16 + 16)
                        if route:
                            a.wait_ge(logits_ready, b + 1)
                        a.copy(yT[:, s], psY[s][:]).then_inc(yT_copied, 1)
                        a.wait_ge(yT_copied, b + 3)
                        a.dma_start(xnt[:, bass.ds(b * T, T)], yT[:, s]).then_inc(yT_stored[s], 16)
                if route:
                    a.wait_ge(shifted, 1)
                    ins = a.activation(ex[:], lg[:, :, 0:E], ACT.Exp)
                    if R > E:
                        ins = a.activation(sg[:], lg[:, :, E:R], ACT.Exp, scale=-1.0)
                    ins.then_inc(exps_done, 1)
                    for n in range(NB):
                        a.wait_ge(gates_turned, n + 1)
                        a.copy(gT[:, n], psG[n % 4][0:G * R, :]).then_inc(gates_copied, 1)
                    a.wait_ge(gates_copied, NB)
                    a.dma_start(route["table"][0:G * R], gT[:].rearrange("p n t -> p (n t)")).then_inc(gates_stored, 16)
                    a.wait_ge(gates_stored, 16)
                for s in range(2):
                    a.wait_ge(yT_stored[s], 16 * (NB // 2) + 16)


ROUTES = {
    "L0": dict(kind="top2", experts=8, rows=9, parts=3),
    "L1": dict(kind="top2max", experts=8, rows=8, parts=1),
    "L2": dict(kind="top1", experts=8, rows=8, parts=1),
}


def moe(nc, name, W, kind, X, xnt, table, hn=None, permuted=False):
    F = {"L0": 1760, "L1": 1024, "L2": 4096}[kind]
    C = -(-F // 128)
    rows = [min(128, F - 128 * c) for c in range(C)]
    GR = 27 if kind == "L0" else 8
    NS = 8 if kind == "L2" else C
    with Stage(nc, name) as st:
        w1 = st.sb("w1", [128, F])
        w2 = st.sb("w2", [128, C, D])
        sel32 = st.sb("sel32", [GR, NS * 128])
        sel = st.sb("sel", [GR, NS * 128], BF16)
        xT = st.sb("xT", [128, 2, T])
        xt = st.sb("xt", [128, 2, TILES, D])
        xo = st.sb("xo", [128, 2, TILES, D])
        g32 = st.sb("g32", [GR, 2, T])
        g16 = st.sb("g16", [GR, 2, T], BF16)
        a1 = st.sb("a1", [128, 2, T])
        tb = st.sb("tb", [128, 2, T])
        h = st.sb("h", [128, 2, T])
        psG = [st.ps(f"psG{i}") for i in range(2)]
        psW = [st.ps(f"psW{i}") for i in range(2)]
        psO = [st.ps(f"psO{i}") for i in range(2)]
        if kind == "L0":
            wu = st.sb("wu", [128, F])
            psU = [st.ps(f"psU{i}") for i in range(2)]
        if kind == "L1":
            b1 = st.sb("b1", [128, C])
            b2 = st.sb("b2", [8, D])
            hx = st.sb("hx", [128, 2, TILES, D])
            gb = st.sb("gb", [128, 2, D])
            y2 = st.sb("y2", [128, TILES, D])
            stats = st.sb("stats", [128, TILES, 6])
            mv = st.sb("mv", [128, TILES, 2])
            vare = st.sb("vare", [128, TILES])
            rstd = st.sb("rstd", [128, TILES])
            half = st.sb("half", [128, TILES])
        if kind == "L2":
            xm = st.sb("xm", [128, 2, T])
        const_in = st.sem("const_in")
        sel_cast = st.sem("sel_cast")
        x_in = [st.sem(f"x_in{s}") for s in range(2)]
        res_in = [st.sem(f"res_in{s}") for s in range(2)]
        g_cast = st.sem("g_cast")
        in_free = st.sem("in_free")
        up_done = st.sem("up_done")
        act_done = st.sem("act_done")
        mid_done = st.sem("mid_done")
        down_done = st.sem("down_done")
        sum_done = st.sem("sum_done")
        sum_free = st.sem("sum_free")
        out_done = st.sem("out_done")
        stored = [st.pool_dma_sem(64 * (NB // 2)) for s in range(2)]
        dve = st.sem("dve")
        paced = st.sem("paced")
        rep_done = st.sem("rep_done")
        masked = st.sem("masked")
        var_done = st.sem("var_done")
        rstd_done = st.sem("rstd_done")
        half_set = st.sem("half_set")

        with nc.Block() as block:
            @block.sync
            def _(sp):
                sp.dma_start(w1[:], W[name_of(kind, "w1")]).then_inc(const_in, 16)
                sp.dma_start(w2[:], W[name_of(kind, "w2")].rearrange("(c p) d -> p c d", p=128)).then_inc(const_in, 16)
                sp.dma_start(sel32[:], W[name_of(kind, "sel")]).then_inc(const_in, 16)
                if kind == "L0":
                    sp.dma_start(wu[:], W["L0_wu"]).then_inc(const_in, 16)
                if kind == "L1":
                    sp.dma_start(b1[:], W["L1_b1"]).then_inc(const_in, 16)
                    sp.dma_start(b2[:], W["L1_b2"]).then_inc(const_in, 16)
                    sp.dma_start(gb[:, 0, :], W["L1_ln2_g"].to_broadcast([128, D])).then_inc(const_in, 16)
                    sp.dma_start(gb[:, 1, :], W["L1_ln2_b"].to_broadcast([128, D])).then_inc(const_in, 16)
                with sp.Fori(0, NB // 2) as i:
                    for s in range(2):
                        b = i * 2 + s
                        sp.wait_ge(in_free, b + 1)
                        sp.dma_start(xT[:, s], xnt[:, bass.ds(b * T, T)]).then_inc(x_in[s], 16)
                        sp.dma_start(g32[:, s], table[0:GR, bass.ds(b * T, T)]).then_inc(x_in[s], 16)
                        sp.wait_ge(sum_free, b + 1)
                        load_tiles(sp, xt[:, s], X, b, permuted, res_in[s])
                        if kind == "L1":
                            load_tiles(sp, hx[:, s], hn, b, False, res_in[s])

            @block.gpsimd
            def _(pool):
                if kind == "L1":
                    pool.memset(half[:], -0.5).then_inc(half_set, 1)
                    pool.wait_ge(half_set, 1)
                pool.sem_inc(sum_free, 2)
                with pool.Fori(0, NB // 2) as i:
                    for s in range(2):
                        b = i * 2 + s
                        if kind == "L1":
                            pool.wait_ge(var_done, b + 1)
                            pool.tensor_tensor(rstd[:], vare[:], half[:], ALU.pow).then_inc(rstd_done, 1)
                        pool.wait_ge(out_done, b + 1)
                        store_tiles(pool, X, xo[:, s], b, permuted, stored[s].sem)
                for s in range(2):
                    stored[s].wait(pool, 64 * (NB // 2))

            @block.tensor
            def _(pe):
                pe.sem_inc(in_free, 2)
                pe.sem_inc(down_done, 2)
                pe.wait_ge(const_in, 16 * NCON[kind])
                pe.wait_ge(sel_cast, 1)

                def rep(b, s, j, m):
                    return pe.matmul(psW[j % 2][0:m, :], sel[:, j * 128:j * 128 + m], g16[:, s],
                                     start=True, stop=True)

                def begin(b, s, n):
                    pe.wait_ge(x_in[s], n * 32 + 32)
                    pe.wait_ge(g_cast, b + 1)

                def replicate(b, s, e):
                    pe.wait_ge(masked, b * 8 + e + 1)
                    rep(b, s, e, 128).then_inc(rep_done, 1)

                def up(b, s, c):
                    m = rows[c]
                    pe.wait_ge(mid_done, b * C + c + 1)
                    if kind == "L2":
                        if c % 4 == 0:
                            pe.wait_ge(masked, b * 8 + c // 4 + 3)
                        pe.matmul(psG[c % 2][:], w1[:, c * 128:(c + 1) * 128], xm[:, c // 4 % 2],
                                  start=True, stop=True).then_inc(up_done, 1)
                        return
                    pe.matmul(psG[c % 2][0:m], w1[:, c * 128:c * 128 + m], xT[:, s], start=True, stop=True)
                    if kind == "L0":
                        pe.matmul(psU[c % 2][0:m], wu[:, c * 128:c * 128 + m], xT[:, s], start=True, stop=True)
                    rep(b, s, c, m).then_inc(up_done, 1)

                def down(b, s, c):
                    m = rows[c]
                    pe.wait_ge(mid_done, b * C + c + 3)
                    if c == 0:
                        pe.wait_ge(sum_free, b + 1)
                    for k in range(TILES):
                        ins = pe.matmul(psO[s][:, k * D:(k + 1) * D], h[0:m, c % 2, k * 128:(k + 1) * 128],
                                        w2[0:m, c], start=(c == 0 and k == 0),
                                        stop=(c == C - 1 and k == TILES - 1 and kind != "L1"), skip_group_check=True)
                    ins.then_inc(down_done, 1)
                    if kind == "L1" and c == C - 1:
                        for k in range(TILES):
                            ins = pe.matmul(psO[s][:, k * D:(k + 1) * D], g32[:, s, k * 128:(k + 1) * 128], b2[:],
                                            start=False, stop=(k == TILES - 1), skip_group_check=True)
                        ins.then_inc(sum_done, 1)

                def pair(i, last):
                    for s in range(2):
                        b = i * 2 + s
                        more = not (last and s == 1)
                        after = (b + 1, 1 - s, i + s)
                        for c in range(C):
                            if c == C - 2 and more:
                                begin(*after)
                            if c < C - 1:
                                up(b, s, c + 1)
                            elif more:
                                up(after[0], after[1], 0)
                            if kind == "L2" and c % 4 == 2:
                                if c < C - 2:
                                    replicate(b, s, c // 4 + 1)
                                elif more:
                                    replicate(after[0], after[1], 0)
                            down(b, s, c)

                begin(0, 0, 0)
                if kind == "L2":
                    replicate(0, 0, 0)
                up(0, 0, 0)
                with pe.Fori(0, NB // 2 - 1) as i:
                    pair(i, False)
                pair(NB // 2 - 1, True)

            @block.scalar
            def _(a):
                if kind == "L1":
                    a.wait_ge(const_in, 16 * NCON[kind])
                with a.Fori(0, NB // 2) as i:
                    for s in range(2):
                        b = i * 2 + s
                        for c in range(C):
                            m = rows[c]
                            a.wait_ge(up_done, b * C + c + 1)
                            a.wait_ge(mid_done, b * C + c + 1)
                            if kind == "L0":
                                ins = a.activation(a1[0:m, c % 2], psG[c % 2][0:m], ACT.Silu)
                            elif kind == "L1":
                                ins = a.activation(a1[0:m, c % 2], psG[c % 2][0:m], ACT.Gelu, bias=b1[:, c:c + 1])
                            else:
                                ins = a.activation(a1[0:m, c % 2], psG[c % 2][0:m], ACT.Relu)
                            ins.then_inc(act_done, 1)

            @block.vector
            def _(v):
                v.wait_ge(const_in, 16 * NCON[kind])
                v.tensor_copy(sel[:], sel32[:]).then_inc(sel_cast, 1)
                v.sem_inc(mid_done, 2)
                if kind == "L2":
                    v.sem_inc(masked, 2)
                PER = 2 * {"L0": C, "L1": 6, "L2": 0}[kind]

                def cast_gates(b, s, n):
                    v.wait_ge(x_in[s], n * 32 + 32)
                    v.wait_ge(in_free, b + 1)
                    v.tensor_copy(g16[:, s], g32[:, s]).then_inc(g_cast, 1)

                def mask(b, s, e):
                    v.wait_ge(rep_done, b * 8 + e + 1)
                    v.tensor_tensor(xm[:, e % 2], xT[:, s], psW[e % 2][:], ALU.mult).then_inc(masked, 1)

                def pair(i, last):
                    STEPS = [0]

                    def link(ins):
                        STEPS[0] += 1
                        ins.then_inc(dve, 1)
                        v.wait_ge(dve, i * PER + STEPS[0])
                        v.sem_inc(paced, 1)

                    for s in range(2):
                        b = i * 2 + s
                        more = not (last and s == 1)
                        after = (b + 1, 1 - s, i + s)
                        for c in range(C):
                            m = rows[c]
                            if c == C - 3 and more:
                                cast_gates(*after)
                            if kind == "L2" and c % 4 == 3:
                                if c < C - 1:
                                    mask(b, s, c // 4 + 1)
                                elif more:
                                    mask(after[0], after[1], 0)
                            v.wait_ge(act_done, b * C + c + 1)
                            if kind == "L0":
                                link(v.tensor_tensor(tb[0:m, c % 2], a1[0:m, c % 2], psU[c % 2][0:m], ALU.mult))
                            v.wait_ge(down_done, b * C + c + 1)
                            if kind == "L0":
                                ins = v.tensor_tensor(h[0:m, c % 2], tb[0:m, c % 2], psW[c % 2][0:m], ALU.mult)
                            elif kind == "L1":
                                ins = v.tensor_tensor(h[0:m, c % 2], a1[0:m, c % 2], psW[c % 2][0:m], ALU.mult)
                            else:
                                ins = v.tensor_tensor(h[0:m, c % 2], a1[0:m, c % 2], a1[0:m, c % 2], ALU.mult)
                            ins.then_inc(mid_done, 1)
                        if kind == "L1":
                            v.wait_ge(sum_done, b + 1)
                        else:
                            v.wait_ge(down_done, b * C + C + 2)
                        v.wait_ge(res_in[s], i * (128 if kind == "L1" else 64) + (128 if kind == "L1" else 64))
                        stored[s].wait(v, i * 64)
                        O = psO[s][:].rearrange("p (k d) -> p k d", k=TILES)
                        if kind != "L1":
                            v.scalar_tensor_tensor(out=xo[:, s], in0=O, scalar=0.5, in1=xt[:, s],
                                                   op0=ALU.mult, op1=ALU.add).then_inc(out_done, 1)
                        else:
                            link(v.tensor_tensor(y2[:], O, hx[:, s], ALU.add))
                            for k in range(TILES):
                                ins = v.bn_stats(stats[:, k], y2[:, k])
                            link(ins)
                            for k in range(TILES):
                                ins = v.bn_aggr(mv[:, k], stats[:, k])
                            link(ins)
                            v.tensor_scalar(vare[:], mv[:, :, 1], 1e-5, None, ALU.add).then_inc(var_done, 1)
                            v.wait_ge(rstd_done, b + 1)
                            for k in range(TILES):
                                ins = v.tensor_scalar(y2[:, k], y2[:, k], mv[:, k, 0:1], rstd[:, k:k + 1],
                                                      ALU.subtract, ALU.mult)
                            link(ins)
                            link(v.tensor_tensor(y2[:], y2[:], gb[:, 0:1, :].to_broadcast([128, TILES, D]), ALU.mult))
                            link(v.tensor_tensor(y2[:], y2[:], gb[:, 1:2, :].to_broadcast([128, TILES, D]), ALU.add))
                            v.scalar_tensor_tensor(out=xo[:, s], in0=y2[:], scalar=0.5, in1=xt[:, s],
                                                   op0=ALU.mult, op1=ALU.add).then_inc(out_done, 1)
                        v.wait_ge(out_done, b + 1)
                        v.sem_inc(sum_free, 1)
                        v.sem_inc(in_free, 1)
                    assert STEPS[0] == PER, (STEPS[0], PER)

                cast_gates(0, 0, 0)
                if kind == "L2":
                    mask(0, 0, 0)
                with v.Fori(0, NB // 2 - 1) as i:
                    pair(i, False)
                pair(NB // 2 - 1, True)


def attention(nc, name, W, kind, xnt, S, X, out):
    key = {"rel": "A0", "block": "A1", "causal": "A2", "plain": "A3"}[kind]
    DV = 64 if kind == "causal" else HD
    VW = HEADS * DV
    NV = TILES * VW // 512 if kind == "causal" else TILES
    QK = 8
    block_kind = kind == "block"
    added = kind in ("rel", "causal")
    U = TILES * 4 if block_kind else TILES * HEADS
    PERT = U // TILES
    OB = 2 if kind == "causal" else 1
    OT = VW // 128
    projected = kind != "rel"
    TURN, VALUES = 3, 5
    late = VALUES - 3 + (0 if kind == "causal" else 2)
    ahead = not block_kind
    split = kind in ("plain", "causal")
    BUF = 2 if ahead else 1
    between = [u for u in range(12, U) if (u - 12) % 16 < 9][:QK + NV] if ahead else []
    with Stage(nc, name) as st:
        ident = st.sb("ident", [128, 128])
        wq = st.sb("wq", [128, 4, 128])
        wk = st.sb("wk", [128, 4, 128])
        bq = st.sb("bq", [128, 4])
        bk = st.sb("bk", [128, 4])
        wv = st.sb("wv", [128, VW])
        xT = st.sb("xT", [128, 2, T])
        xt = st.sb("xt", [128, 2, TILES, D])
        q = st.sb("q", [128, BUF, 4, 4, T], BF16 if split else F32)
        if split:
            kA = st.sb("kA", [128, BUF, 4, T], BF16)
            kB = st.sb("kB", [128, BUF, 4, T], BF16)
            staged = st.sb("staged", [128, 8, T])
            whole = st.sb("whole", [128, 4, T], BF16)
            taken = st.sb("taken", [128, 8, T], BF16)
            bias_n = st.sb("bias_n", [128, 8])
            scale_n = st.sb("scale_n", [128, 1])
            rest = st.sb("rest", [128, 2, T])
            second = st.sb("second", [128, 2, T], BF16)
            keys_split = st.sem("keys_split")
            dve_step = st.sem("dve_step")
            slots = st.sb("slots", [128, 5])
            staged_done = st.sem("staged_done")
            split_done = st.sem("split_done")
            pool_step = st.sem("pool_step")
            bias_scaled = st.sem("bias_scaled")
        else:
            k_ = st.sb("k", [128, BUF, 4, T])
        wide = kind == "causal"
        if wide:
            va = st.sb("va", [128, BUF, TILES, VW])
        else:
            va = st.sb("va", [128, BUF, TILES, HEADS, 32])
            oU = st.sb("oU", [128, 2, T])
        p = st.sb("p", [128, 4, T])
        pT = st.sb("pT", [128, 3, T])
        nm = st.sb("nm", [128, 4, 4])
        rs = st.sb("rs", [128, TILES, HEADS])
        ri = st.sb("ri", [128, 2, HEADS])
        o = st.sb("o", [128, 2, VW])
        xo = st.sb("xo", [128, 2, TILES, D])
        psP = [st.ps(f"psP{i}") for i in range(2)]
        psS = [st.ps(f"psS{i}") for i in range(2)]
        psT = [st.ps(f"psT{i}") for i in range(2)]
        psO = [st.ps("psO", [128, 512 * OB])] if wide else [st.ps(f"psO{i}") for i in range(2)]
        if added:
            t = st.sb("t", [128, 4, T])
        if kind in ("causal", "block"):
            mask = st.sb("mask", [128, T])
        if block_kind:
            ident16 = st.sb("ident16", [128, 128], BF16)
            mask16 = st.sb("mask16", [128, T], BF16)
            mask_cast = st.sem("mask_cast")
        if kind == "rel":
            far = st.sb("far", [128, 2])
            kl = st.sb("kl", [128, BUF, 4, T // 2])
            kr = st.sb("kr", [128, BUF, 4, T // 2])
            pos = st.sb("pos", [128, TILES, 2, T])
        if kind != "causal":
            bv = st.sb("bv", [128, VW])
        if projected:
            wo = st.sb("wo", [128, OT, D])
            oT = st.sb("oT", [128, 2, VW])
            if kind != "causal":
                bo = st.sb("bo", [128, D])
        const_in = st.sem("const_in")
        x_in = [st.sem(f"x_in{s}") for s in range(2)]
        res_in = [st.sem(f"res_in{s}") for s in range(2)]
        in_free = st.sem("in_free")
        res_free = st.sem("res_free")
        proj_done = st.sem("proj_done")
        q_copied = st.sem("q_copied")
        qk_copied = st.sem("qk_copied")
        v_copied = st.sem("v_copied")
        scores_ready = st.sem("scores_ready")
        added_done = st.sem("added_done")
        max_done = st.sem("max_done")
        probs_done = st.sem("probs_done")
        turned = st.sem("turned")
        turned_copied = st.sem("turned_copied")
        tile_done = st.sem("tile_done")
        tile_gathered = st.sem("tile_gathered")
        tile_turned = st.sem("tile_turned")
        values_zero = st.sem("values_zero")
        queries_zero = st.sem("queries_zero")
        tile_scaled = st.sem("tile_scaled")
        o_turned = st.sem("o_turned")
        o_copied = st.sem("o_copied")
        o_projected = st.sem("o_projected")
        out_done = st.sem("out_done")
        stored = [st.pool_dma_sem(64 * (NB // 2)) for s in range(2)]
        dve = st.sem("dve")
        paced = st.sem("paced")
        pos_set = st.sem("pos_set")
        pos_in = [st.sem(f"pos_in{j}") for j in range(8)]
        NCN = 6 + (kind in ("causal", "block")) + (kind == "rel") + (kind != "causal") + split + projected + (
            projected and kind != "causal")

        def width(it):
            return (it + 1) * 128 if kind == "causal" else T

        def window(it):
            return max(0, it - 1) * 128, min(TILES, it + 2) * 128

        def split_block(eng, w, step, done, b, s, j, STEPS):
            def link(ins):
                STEPS[0] += 1
                ins.then_inc(step, 1)
                eng.wait_ge(step, STEPS[1] + STEPS[0])
                eng.sem_inc(paced, 1)

            m = j % 4
            y, off, rem, two = staged[:, j], taken[:, j], rest[:, w], second[:, w]
            eng.wait_ge(staged_done, b * 8 + j + 1)
            eng.sem_inc(paced, 1)
            if j < 4:
                link(eng.tensor_tensor(rem, y, off, ALU.add))
                link(eng.tensor_scalar(two, rem, slots[:, 1:2], None, ALU.mult))
                for g in range(4):
                    r = slice(32 * g, 32 * g + 32)
                    ins = eng.tensor_tensor(q[r, s, m, g], rest[r, w], second[r, w], ALU.add)
            else:
                eng.tensor_tensor(kA[:, s, m], y, off, ALU.add)
                link(eng.tensor_tensor(rem, y, whole[:, m], ALU.subtract))
                link(eng.tensor_scalar(two, rem, slots[:, 3:4], None, ALU.mult))
                link(eng.tensor_scalar(rem, rem, slots[:, 4:5], None, ALU.mult))
                ins = eng.tensor_tensor(kB[:, s, m], rem, two, ALU.add)
            link(ins)
            eng.sem_inc(done, 1)

        with nc.Block() as block:
            @block.sync
            def _(sp):
                def const(dst, src):
                    sp.dma_start(dst, src).then_inc(const_in, 16)

                const(ident[:], W["ident"])
                const(wq[:].rearrange("p a b -> p (a b)"), W[f"{key}_wq"])
                const(wk[:].rearrange("p a b -> p (a b)"), W[f"{key}_wk"])
                const(bq[:], W[f"{key}_bq"])
                const(bk[:], W[f"{key}_bk"])
                const(wv[:], W[f"{key}_wv"])
                if split:
                    const(slots[:], W["slots"])
                if kind in ("causal", "block"):
                    const(mask[:], W[f"{key}_mask"])
                if kind == "rel":
                    const(far[:], W["A0_far"])
                if kind != "causal":
                    const(bv[:], W[f"{key}_bv"].to_broadcast([128, VW]))
                if projected:
                    const(wo[:], W[f"{key}_wo"].rearrange("(c p) d -> p c d", p=128))
                    if kind != "causal":
                        const(bo[:], W[f"{key}_bo"].to_broadcast([128, D]))
                if kind == "rel":
                    sp.wait_ge(pos_set, 1)

                def load_x(b, s):
                    sp.wait_ge(in_free, b + 1)
                    sp.dma_start(xT[:, s], xnt[:, bass.ds(b * T, T)]).then_inc(x_in[s], 16)

                def pair(i, last):
                    for s in range(2):
                        b = i * 2 + s
                        if not (last and s == 1):
                            load_x(b + 1, 1 - s)
                        sp.wait_ge(res_free, b + 1)
                        load_tiles(sp, xt[:, s], X, b, False, res_in[s])
                        if kind == "rel":
                            for u in range(U):
                                it, h = divmod(u, HEADS)
                                lo, hi = window(it)
                                j = u % 2
                                if h >= 2:
                                    sp.wait_ge(added_done, b * U + u - 1)
                                base = (lo - (it - 1) * 128) + 127
                                row = S["PR"][bass.ds(b * U + u, 1)]
                                src = skewed(row, base, hi - lo)
                                sp.dma_start(pos[:, it, j, lo:hi], src).then_inc(pos_in[it * 2 + j], 16)

                load_x(0, 0)
                with sp.Fori(0, NB // 2 - 1) as i:
                    pair(i, False)
                pair(NB // 2 - 1, True)

            @block.gpsimd
            def _(pool):
                pool.memset(q[:].rearrange("p s m g t -> p (s m g t)"), 0.0).then_inc(queries_zero, 1)
                if not wide:
                    pool.memset(va[:].rearrange("p s a b c -> p (s a b c)"), 0.0).then_inc(values_zero, 1)
                if kind == "rel":
                    pool.memset(pos[:].rearrange("p a b c -> p (a b c)"), 0.0).then_inc(pos_set, 1)
                PER = 2 * (4 * 3 + 4 * 4)

                def split_next(b, s, j, STEPS):
                    split_block(pool, 0, pool_step, split_done, b, s, j, STEPS)

                def pair(i, last):
                    STEPS = [0, i * PER + 4 * 3]
                    for s in range(2):
                        b = i * 2 + s
                        if split and not (last and s == 1):
                            for j in range(8):
                                split_next(b + 1, 1 - s, j, STEPS)
                        pool.wait_ge(out_done, b * TILES + TILES + 1)
                        store_tiles(pool, out, xo[:, s], b, False, stored[s].sem)
                    assert not split or last or STEPS[0] == PER

                if split:
                    pool.wait_ge(const_in, 16 * NCN)
                    pool.sem_inc(split_done, 8)
                    STEPS = [0, 0]
                    for j in range(4):
                        split_next(0, 0, j, STEPS)
                    assert STEPS[0] == 4 * 3
                    pool.wait_ge(keys_split, 4)
                    pool.sem_inc(split_done, 4)
                with pool.Fori(0, NB // 2 - 1) as i:
                    pair(i, False)
                pair(NB // 2 - 1, True)
                for s in range(2):
                    stored[s].wait(pool, 64 * (NB // 2))

            @block.tensor
            def _(pe):
                pe.sem_inc(in_free, 2)
                pe.wait_ge(const_in, 16 * NCN)
                if block_kind:
                    pe.wait_ge(mask_cast, 2)

                def wait_copied(b, j):
                    if split and j < QK:
                        pe.wait_ge(staged_done, b * 8 + j + 1)
                    elif j in (0, 2):
                        pe.wait_ge(q_copied, b * 2 + j // 2 + 1)
                    elif j < QK:
                        pe.wait_ge(qk_copied, b * 6 + ((j + 1) // 2 if j < 4 else j - 1))
                    else:
                        pe.wait_ge(v_copied, b * NV + j - QK + 1)

                def product(b, s, n, j, tiles):
                    if j == 0:
                        pe.wait_ge(x_in[s], n * 16 + 16)
                    pe.wait_ge(out_done, tiles + 1)
                    if j >= 2:
                        wait_copied(b, j - 2)
                    if j < 4:
                        ins = pe.matmul(psP[j % 2][:], wq[:, j], xT[:, s], start=True, stop=True)
                    elif j < QK:
                        ins = pe.matmul(psP[j % 2][:], wk[:, j - 4], xT[:, s], start=True, stop=True)
                    else:
                        k, c = ((j - QK) // 2, (j - QK) % 2) if kind == "causal" else (j - QK, 0)
                        w = min(VW, 512)
                        ins = pe.matmul(psP[j % 2][:, 0:w], xT[:, s, k * 128:(k + 1) * 128],
                                        wv[:, c * 512:c * 512 + w], start=True, stop=True)
                    ins.then_inc(proj_done, 1)

                def pair(i, last):
                    for s in range(2):
                        b = i * 2 + s
                        qs = s if ahead else 0
                        more = ahead and not (last and s == 1)
                        if not ahead:
                            for j in range(QK + NV):
                                product(b, s, i, j, b * TILES)
                        if split:
                            pe.wait_ge(split_done, b * 8 + 16)
                        else:
                            pe.wait_ge(q_copied, b * 2 + 2)
                            pe.wait_ge(qk_copied, b * 6 + 6)
                        pe.wait_ge(v_copied, b * NV + NV)
                        pe.sem_inc(in_free, 1)

                        def projected_before(u):
                            done = len([x for x in between if x < u])
                            if more:
                                for j in range(max(0, done - 2), done):
                                    wait_copied(b + 1, j)

                        def scores(u):
                            it, h = divmod(u, PERT)
                            if u >= 2:
                                if added:
                                    pe.wait_ge(added_done, b * U + u - 1)
                                else:
                                    pe.wait_ge(probs_done, b * U + u - 1)
                            if block_kind:
                                pe.matmul(psS[u % 2][:], ident16[:], mask16[:], start=True, stop=False,
                                          skip_group_check=True)
                                for m in range(4):
                                    ins = pe.matmul(psS[u % 2][:, m * 128:(m + 1) * 128],
                                                    q[:, qs, m, h, it * 128:(it + 1) * 128], k_[:, qs, m, it * 128:(it + 1) * 128],
                                                    start=False, stop=(m == 3), skip_group_check=True)
                                ins.then_inc(scores_ready, 1)
                                return
                            m, g = divmod(h, 4)
                            lhs = q[:, qs, m, g, it * 128:(it + 1) * 128]
                            if split:
                                L = width(it)
                                pe.matmul(psS[u % 2][:, 0:L], lhs, kA[:, qs, m, 0:L], start=True, stop=False)
                                pe.matmul(psS[u % 2][:, 0:L], lhs, kB[:, qs, m, 0:L], start=False,
                                          stop=True).then_inc(scores_ready, 1)
                                return
                            if kind == "rel":
                                lo, hi = window(it)
                                parts = [(kl, 0, lo, 0), (k_, lo, hi, 0), (kr, hi, T, T // 2)]
                            else:
                                parts = [(k_, 0, width(it), 0)]
                            for ks, lo, hi, first in parts:
                                if hi > lo:
                                    ins = pe.matmul(psS[u % 2][:, lo:hi], lhs, ks[:, qs, m, lo - first:hi - first],
                                                    start=True, stop=True)
                            ins.then_inc(scores_ready, 1)

                        def turn(u):
                            it, h = divmod(u, PERT)
                            pe.wait_ge(probs_done, b * U + u + 1)
                            if u >= 2:
                                pe.wait_ge(turned_copied, b * U + u - 1)
                            for j in range(width(it) // 128):
                                ins = pe.transpose(psT[u % 2][:, j * 128:(j + 1) * 128],
                                                   p[:, u % 4, j * 128:(j + 1) * 128], ident[:])
                            ins.then_inc(turned, 1)

                        def values(u):
                            it, h = divmod(u, PERT)
                            pe.wait_ge(turned_copied, b * U + u + 1)
                            if h == 0 and wide:
                                pe.wait_ge(tile_scaled, b * TILES + it + 1)
                            elif h == 0:
                                pe.wait_ge(tile_gathered, b * TILES + it + 1)
                            if block_kind:
                                for m in range(4):
                                    ins = pe.matmul(psO[it % 2][32 * h:32 * h + 32, m * 128:(m + 1) * 128],
                                                    va[:, qs, it, 4 * m + h], pT[:, u % 3, m * 128:(m + 1) * 128],
                                                    start=True, stop=True)
                            elif not wide:
                                m, g = divmod(h, 4)
                                for j in range(TILES):
                                    ins = pe.matmul(psO[it % 2][32 * g:32 * g + 32, m * 128:(m + 1) * 128],
                                                    va[:, qs, j, h], pT[:, u % 3, j * 128:(j + 1) * 128],
                                                    start=(j == 0), stop=(j == TILES - 1))
                            else:
                                J = width(it) // 128
                                for j in range(J):
                                    ins = pe.matmul(psO[0][:, h * DV:(h + 1) * DV], pT[:, u % 3, j * 128:(j + 1) * 128],
                                                    va[:, qs, j, h * DV:(h + 1) * DV], start=(j == 0), stop=(j == J - 1))
                            if h == PERT - 1:
                                ins.then_inc(tile_done, 1)

                        def turn_values(it):
                            n = b * TILES + it
                            pe.wait_ge(tile_gathered, n + 1 + 2)
                            pe.wait_ge(tile_scaled, n + 1)
                            projected_before(it * PERT + PERT - 1 + 3 + late)
                            for m in range(4):
                                ins = pe.transpose(psP[1][:, m * 128:(m + 1) * 128], oU[:, it % 2, m * 128:(m + 1) * 128],
                                                   ident[:])
                            ins.then_inc(tile_turned, 1)

                        def turn_output(it):
                            n = b * TILES + it
                            pe.wait_ge(tile_scaled, n + 1 + 1)
                            projected_before(it * PERT + PERT - 1 + 5 + late)
                            for c in range(OT):
                                if c % 4 == 0:
                                    if it > 0 and c == 0:
                                        pe.wait_ge(o_copied, n + 1)
                                        pe.wait_ge(out_done, n + 1)
                                ins = pe.transpose(psP[c // 4][:, c % 4 * 128:(c % 4 + 1) * 128],
                                                   o[:, it % 2, c * 128:(c + 1) * 128], ident[:])
                            ins.then_inc(o_turned, 1)

                        def project(it):
                            pe.wait_ge(o_copied, b * TILES + it + 1 + 1)
                            for c in range(OT):
                                ins = pe.matmul(psP[0][:, 0:D], oT[:, it % 2, c * 128:(c + 1) * 128], wo[:, c],
                                                start=(c == 0), stop=(c == OT - 1))
                            ins.then_inc(o_projected, 1)

                        for u in range(U + 8 + late):
                            if u < U:
                                scores(u)
                            if TURN <= u < U + TURN:
                                turn(u - TURN)
                            if VALUES <= u < U + VALUES:
                                values(u - VALUES)
                            if not wide and u >= 3 + late and (u - 3 - late) % PERT == PERT - 1 and u - 3 - late < U:
                                turn_values((u - 3 - late) // PERT)
                            if projected and u >= 5 + late and (u - 5 - late) % PERT == PERT - 1:
                                turn_output((u - 5 - late) // PERT)
                            if projected and u >= 7 + late and (u - 7 - late) % PERT == PERT - 1:
                                project((u - 7 - late) // PERT)
                            if more and u in between:
                                product(b + 1, 1 - s, i + s, between.index(u), b * TILES + (u - 12) // 16)

                if ahead:
                    for j in range(QK + NV):
                        product(0, 0, 0, j, 0)
                with pe.Fori(0, NB // 2 - 1) as i:
                    pair(i, False)
                pair(NB // 2 - 1, True)

            @block.scalar
            def _(a):
                a.wait_ge(const_in, 16 * NCN)
                if split:
                    a.wait_ge(bias_scaled, 2)
                a.wait_ge(queries_zero, 1)

                def take(b, s, j):
                    if j not in (0, 2) and not (kind == "causal" and j >= QK) and not (split and j < QK):
                        return
                    a.wait_ge(proj_done, b * (QK + NV) + j + 1)
                    if split and j < QK:
                        a.wait_ge(split_done, b * 8 + j + 1)
                        bias, scale = (bq, 1.0) if j < 4 else (bk, -(HD ** -0.5))
                        m = j % 4
                        a.activation(staged[:, j], psP[j % 2][:], ACT.Identity, bias=bias[:, m:m + 1], scale=scale)
                        if j >= 4:
                            a.activation(whole[:, m], psP[j % 2][:], ACT.Identity, bias=bias[:, m:m + 1], scale=scale)
                        a.activation(taken[:, j], psP[j % 2][:], ACT.Identity, bias=bias_n[:, j:j + 1],
                                     scale=slots[:, 0:1] if j < 4 else scale_n[:, 0:1]).then_inc(staged_done, 1)
                    elif j < QK:
                        for g in range(4):
                            r = slice(32 * g, 32 * g + 32)
                            ins = a.activation(q[r, s, j, g], psP[0][r], ACT.Identity, bias=bq[r, j:j + 1])
                        ins.then_inc(q_copied, 1)
                    else:
                        k, c = divmod(j - QK, 2)
                        a.copy(va[:, s, k, c * 512:c * 512 + 512], psP[j % 2][:]).then_inc(v_copied, 1)

                def pair(i, last):
                    for s in range(2):
                        b = i * 2 + s
                        more = ahead and not (last and s == 1)
                        if not ahead:
                            for j in range(QK + NV):
                                take(b, 0, j)
                        for u in range(U):
                            it, h = divmod(u, PERT)
                            a.wait_ge(max_done, b * U + u + 1)
                            if u >= 4:
                                a.wait_ge(turned, b * U + u - 3)
                            src = t[:, u % 4] if added else psS[u % 2][:]
                            if block_kind:
                                for g in range(4):
                                    ins = a.activation(p[:, u % 4, g * 128:(g + 1) * 128], src[:, g * 128:(g + 1) * 128],
                                                       ACT.Exp, bias=nm[:, u % 4, g:g + 1], scale=-1.0,
                                                       accum_out=rs[:, it, 4 * g + h:4 * g + h + 1])
                            else:
                                L = width(it)
                                ins = a.activation(p[:, u % 4, 0:L], src[:, 0:L], ACT.Exp, bias=nm[:, u % 4, 0:1],
                                                   scale=-1.0, accum_out=rs[:, it, h:h + 1])
                            ins.then_inc(probs_done, 1)
                            if more and u in between:
                                take(b + 1, 1 - s, between.index(u))

                if ahead:
                    for j in range(QK + NV):
                        take(0, 0, j)
                with a.Fori(0, NB // 2 - 1) as i:
                    pair(i, False)
                pair(NB // 2 - 1, True)

            @block.vector
            def _(v):
                v.sem_inc(res_free, 2)
                v.sem_inc(out_done, 1)
                v.sem_inc(tile_scaled, 1)
                v.sem_inc(tile_gathered, 2)
                v.sem_inc(o_copied, 1)
                v.wait_ge(const_in, 16 * NCN)
                if block_kind:
                    v.tensor_copy(ident16[:], ident[:]).then_inc(mask_cast, 1)
                    v.tensor_copy(mask16[:], mask[:]).then_inc(mask_cast, 1)
                if split:
                    v.tensor_scalar(bk[:], bk[:], -(HD ** -0.5), None, ALU.mult).then_inc(bias_scaled, 1)
                    v.wait_ge(bias_scaled, 1)
                    v.tensor_scalar(bias_n[:, 4:8], bk[:], slots[:, 2:3], None, ALU.mult)
                    v.tensor_scalar(scale_n[:], slots[:, 2:3], -(HD ** -0.5), None, ALU.mult)
                    v.tensor_scalar(bias_n[:, 0:4], bq[:], slots[:, 0:1], None, ALU.mult).then_inc(bias_scaled, 1)
                v.wait_ge(queries_zero, 1)
                if not wide:
                    v.wait_ge(values_zero, 1)
                PER = 2 * (TILES * (2 if kind in ("plain", "block") else 1))

                def take(b, s, j):
                    if j in (0, 2) or (kind == "causal" and j >= QK) or (split and j < QK):
                        return
                    v.wait_ge(proj_done, b * (QK + NV) + j + 1)
                    m = j % 4
                    if j < 4:
                        for g in range(4):
                            r = slice(32 * g, 32 * g + 32)
                            ins = v.tensor_scalar(q[r, s, m, g], psP[1][r], bq[r, m:m + 1], None, ALU.add)
                        ins.then_inc(qk_copied, 1)
                    elif j < QK:
                        v.tensor_scalar(k_[:, s, m], psP[j % 2][:], bk[:, m:m + 1], -(HD ** -0.5), ALU.add,
                                        ALU.mult).then_inc(qk_copied, 1)
                    else:
                        v.tensor_tensor(va[:, s, j - QK, :, 0:HD], psP[j % 2][:, 0:VW].rearrange("p (h d) -> p h d", h=HEADS),
                                        bv[:].rearrange("p (h d) -> p h d", h=HEADS), ALU.add).then_inc(v_copied, 1)
                    if kind == "rel" and j == QK - 1:
                        v.wait_ge(qk_copied, b * 6 + 6)
                        v.tensor_scalar(kl[:, s], k_[:, s, :, 0:T // 2], far[:, 0:1], None, ALU.subtract)
                        v.tensor_scalar(kr[:, s], k_[:, s, :, T // 2:T], far[:, 1:2], None, ALU.subtract)

                def pair(i, last):
                    STEPS = [0]

                    def link(ins):
                        STEPS[0] += 1
                        ins.then_inc(dve, 1)
                        v.wait_ge(dve, i * PER + STEPS[0])

                    for s in range(2):
                        b = i * 2 + s
                        more = ahead and not (last and s == 1)
                        if not ahead:
                            for j in range(QK + NV):
                                take(b, 0, j)

                        def lowest(u):
                            it, h = divmod(u, PERT)
                            L = width(it)
                            v.wait_ge(scores_ready, b * U + u + 1)
                            if u >= 4:
                                v.wait_ge(probs_done, b * U + u - 3)
                            if kind == "plain":
                                v.tensor_reduce(nm[:, u % 4, 0:1], psS[u % 2][:], AX.X, ALU.min).then_inc(max_done, 1)
                            elif block_kind:
                                v.tensor_reduce(nm[:, u % 4, :], psS[u % 2][:].rearrange("p (g k) -> p g k", g=4), AX.X,
                                                ALU.min).then_inc(max_done, 1)
                            else:
                                if kind == "causal":
                                    plus = mask[:, T - L:T]
                                else:
                                    plus = pos[:, it, h % 2]
                                    v.wait_ge(pos_in[it * 2 + h % 2], (b * (HEADS // 2) + h // 2 + 1) * 16)
                                v.sem_inc(paced, 1)
                                v.tensor_tensor_reduce(out=t[:, u % 4, 0:L], in0=psS[u % 2][:, 0:L], in1=plus, scale=1.0,
                                                       scalar=3e38, op0=ALU.add, op1=ALU.min,
                                                       accum_out=nm[:, u % 4, 0:1]).then_inc(max_done, 1)
                                v.wait_ge(max_done, b * U + u + 1)
                                v.sem_inc(added_done, 1)

                        def copy_turned(u):
                            it, h = divmod(u, PERT)
                            v.wait_ge(turned, b * U + u + 1)
                            v.tensor_copy(pT[:, u % 3, 0:width(it)], psT[u % 2][:, 0:width(it)]).then_inc(turned_copied, 1)

                        def gather_tile(it):
                            n = b * TILES + it
                            v.wait_ge(tile_done, n + 1)
                            v.tensor_copy(oU[:, it % 2], psO[it % 2][:]).then_inc(tile_gathered, 1)

                        def scale_tile(it):
                            n = b * TILES + it
                            if wide:
                                v.wait_ge(tile_done, n + 1)
                                O = psO[0][:, 0:VW].rearrange("p (h d) -> p h d", h=HEADS)
                            else:
                                v.wait_ge(tile_turned, n + 1)
                                O = psP[1][:].rearrange("p (h d) -> p h d", h=HEADS)[:, :, 0:HD]
                            link(v.reciprocal(ri[:, it % 2], rs[:, it]))
                            dst = o[:, it % 2].rearrange("p (h d) -> p h d", h=HEADS)
                            v.tensor_tensor(dst, O, bc(ri[:, it % 2], DV), ALU.mult).then_inc(tile_scaled, 1)
                            if kind == "rel":
                                v.wait_ge(res_in[s], i * 64 + 64)
                                stored[s].wait(v, i * 64)
                                v.wait_ge(tile_scaled, n + 1 + 1)
                                v.tensor_tensor(xo[:, s, it], o[:, it % 2], xt[:, s, it], ALU.add).then_inc(out_done, 1)

                        def copy_output(it):
                            n = b * TILES + it
                            v.wait_ge(o_turned, n + 1)
                            for c in range(0, OT, 4):
                                w = min(512, VW)
                                ins = v.tensor_copy(oT[:, it % 2, c * 128:c * 128 + w], psP[c // 4][:, 0:w])
                            ins.then_inc(o_copied, 1)

                        def finish_tile(it):
                            n = b * TILES + it
                            v.wait_ge(o_projected, n + 1)
                            v.wait_ge(res_in[s], i * 64 + 64)
                            stored[s].wait(v, i * 64)
                            if kind == "causal":
                                v.tensor_tensor(xo[:, s, it], psP[0][:, 0:D], xt[:, s, it], ALU.add).then_inc(out_done, 1)
                            else:
                                link(v.tensor_tensor(xo[:, s, it], psP[0][:, 0:D], bo[:], ALU.add))
                                v.tensor_tensor(xo[:, s, it], xo[:, s, it], xt[:, s, it], ALU.add).then_inc(out_done, 1)

                        for u in range(U + 9 + late):
                            if u < U:
                                lowest(u)
                            if TURN <= u < U + TURN:
                                copy_turned(u - TURN)
                            if not wide and u >= 2 + late and (u - 2 - late) % PERT == PERT - 1 and u - 2 - late < U:
                                gather_tile((u - 2 - late) // PERT)
                            if u >= 4 + late and (u - 4 - late) % PERT == PERT - 1 and u - 4 - late < U:
                                scale_tile((u - 4 - late) // PERT)
                            if projected and u >= 6 + late and (u - 6 - late) % PERT == PERT - 1 and u - 6 - late < U:
                                copy_output((u - 6 - late) // PERT)
                            if projected and u >= 8 + late and (u - 8 - late) % PERT == PERT - 1 and u - 8 - late < U:
                                finish_tile((u - 8 - late) // PERT)
                            if more and u in between:
                                take(b + 1, 1 - s, between.index(u))
                        v.wait_ge(out_done, b * TILES + TILES + 1)
                        v.sem_inc(res_free, 1)
                    assert STEPS[0] == PER, (STEPS[0], PER)

                if ahead:
                    for j in range(QK + NV):
                        take(0, 0, j)
                if split:
                    STEPS = [0, 0]
                    for j in range(4, 8):
                        split_block(v, 1, dve_step, keys_split, 0, 0, j, STEPS)
                with v.Fori(0, NB // 2 - 1) as i:
                    pair(i, False)
                pair(NB // 2 - 1, True)


QUINTIC, CUBIC = (3.4445, -4.7750, 2.0315), (1.5, -0.5, 0.0)
GROW, SETTLE = 16, 8


def polar(nc, name, W, PT):
    with Stage(nc, name) as st:
        ident = st.sb("ident", [128, 128])
        ones = st.sb("ones", [128, 128])
        w0 = st.sb("w0", [128, 2, 2, 128])
        x = st.sb("x", [128, 2, 2, 128])
        a = st.sb("a", [128, 2, 128])
        b_ = st.sb("b", [128, 2, 128])
        c_ = st.sb("c", [128, 2, 128])
        aI = st.sb("aI", [128, 2, 128])
        sq = st.sb("sq", [128, 128])
        rows = st.sb("rows", [128, 2])
        tot = st.sb("tot", [128, 2])
        inv = st.sb("inv", [128, 2])
        half = st.sb("half", [128, 2])
        psA = [st.ps(f"psA{m}", [128, 4, 128]) for m in range(2)]
        psX = [st.ps(f"psX{m}", [128, 2, 256]) for m in range(2)]
        const_in = st.sem("const_in")
        ones_set = st.sem("ones_set")
        rows_summed = st.sem("rows_summed")
        total_ready = st.sem("total_ready")
        total_copied = st.sem("total_copied")
        inv_done = st.sem("inv_done")
        x_ready = st.sem("x_ready")
        gram_ready = st.sem("gram_ready")
        gram_copied = st.sem("gram_copied")
        square_ready = st.sem("square_ready")
        poly_ready = st.sem("poly_ready")
        step_ready = st.sem("step_ready")
        dve = st.sem("dve")
        stored = st.sem("stored")
        with nc.Block() as block:
            @block.sync
            def _(sp):
                sp.dma_start(ident[:], W["ident"]).then_inc(const_in, 16)
                for m in range(2):
                    for t in range(2):
                        sp.dma_start(w0[:, m, t], W["P_w"][2 * m + t]).then_inc(const_in, 16)
                sp.wait_ge(x_ready, 2 * (1 + GROW + SETTLE))
                for m in range(2):
                    sp.dma_start(PT[m], x[:, m, 1]).then_inc(stored, 16)
                sp.wait_ge(stored, 32)

            @block.gpsimd
            def _(pool):
                pool.memset(half[:], -0.5)
                pool.memset(ones[:], 1.0).then_inc(ones_set, 1)
                pool.wait_ge(ones_set, 1)
                pool.wait_ge(total_copied, 1)
                pool.tensor_tensor(inv[:], tot[:], half[:], ALU.pow).then_inc(inv_done, 1)

            @block.tensor
            def _(pe):
                pe.wait_ge(const_in, 80)
                pe.wait_ge(ones_set, 1)
                pe.wait_ge(rows_summed, 2)
                pe.matmul(psA[0][:, 0, 0:2], ones[:], rows[:], start=True, stop=True).then_inc(total_ready, 1)

                def step(n, m):
                    pe.wait_ge(x_ready, n + 1 + m)
                    pe.matmul(psA[m][:, 0], x[:, m, 0], x[:, m, 0], start=True, stop=True).then_inc(gram_ready, 1)

                def square(n, m):
                    pe.wait_ge(gram_copied, n + 1 + m)
                    pe.matmul(psA[m][:, 1], a[:, m], a[:, m], start=True, stop=True).then_inc(square_ready, 1)

                def apply(n, m):
                    pe.wait_ge(poly_ready, n + 1 + m)
                    pe.matmul(psX[m][:, 0, 0:128], x[:, m, 1], b_[:, m], start=True, stop=True)
                    pe.matmul(psX[m][:, 1, 0:128], b_[:, m], x[:, m, 1], start=True, stop=True).then_inc(step_ready, 1)

                for first, count in ((0, GROW), (GROW, SETTLE)):
                    with pe.Fori(first, first + count) as i:
                        for f in (step, square, apply):
                            for m in range(2):
                                f(i * 2, m)

            @block.scalar
            def _(s_):
                s_.wait_ge(total_ready, 1)
                s_.copy(tot[:], psA[0][:, 0, 0:2]).then_inc(total_copied, 1)

            @block.vector
            def _(v):
                v.wait_ge(const_in, 80)
                for m in range(2):
                    v.tensor_tensor(sq[:], w0[:, m, 0], w0[:, m, 0], ALU.mult).then_inc(dve, 1)
                    v.wait_ge(dve, 2 * m + 1)
                    v.tensor_reduce(rows[:, m:m + 1], sq[:], AX.X, ALU.add).then_inc(dve, 1)
                    v.wait_ge(dve, 2 * m + 2)
                    v.sem_inc(rows_summed, 1)
                v.wait_ge(inv_done, 1)
                for m in range(2):
                    v.tensor_scalar(x[:, m], w0[:, m], inv[:, m:m + 1], None, ALU.mult).then_inc(x_ready, 1)
                v.tensor_scalar(aI[:, 0], ident[:], QUINTIC[0], None, ALU.mult).then_inc(dve, 1)
                v.tensor_scalar(aI[:, 1], ident[:], CUBIC[0], None, ALU.mult).then_inc(dve, 1)
                v.wait_ge(dve, 6)
                for ph, (first, count, (_, cb, cc)) in enumerate(((0, GROW, QUINTIC), (GROW, SETTLE, CUBIC))):
                    with v.Fori(first, first + count) as i:
                        n = i * 2
                        for m in range(2):
                            v.wait_ge(gram_ready, n + 1 + m)
                            v.tensor_copy(a[:, m], psA[m][:, 0]).then_inc(gram_copied, 1)
                        for m in range(2):
                            v.wait_ge(gram_copied, n + 1 + m)
                            v.scalar_tensor_tensor(out=c_[:, m], in0=a[:, m], scalar=cb, in1=aI[:, ph], op0=ALU.mult,
                                                   op1=ALU.add).then_inc(dve, 1)
                        for m in range(2):
                            v.wait_ge(square_ready, n + 1 + m)
                            v.wait_ge(dve, n + 6 + 1 + m)
                            v.scalar_tensor_tensor(out=b_[:, m], in0=psA[m][:, 1], scalar=cc, in1=c_[:, m], op0=ALU.mult,
                                                   op1=ALU.add).then_inc(poly_ready, 1)
                        for m in range(2):
                            v.wait_ge(step_ready, n + 1 + m)
                            v.tensor_copy(x[:, m], psX[m][:, :, 0:128]).then_inc(x_ready, 1)


def scan_attention(nc, name, W, xnt, X, PT):
    LEVELS = 9
    size = [513] + [256 >> k for k in range(LEVELS)]
    with Stage(nc, name) as st:
        wq = st.sb("wq", [128, 128])
        wv = st.sb("wv", [128, 128])
        wc = st.sb("wc", [128, 128])
        pt = st.sb("pt", [128, 2, 128])
        first = st.sb("first", [128, 1])
        mean = st.sb("mean", [128, 128])
        eps = st.sb("eps", [128, 1])
        xT = st.sb("xT", [128, 2, T])
        seq = st.sb("seq", [128, NB, 513])
        val = st.sb("val", [128, NB, T])
        res = st.sb("res", [128, NB, 513])
        lev = [seq] + [st.sb(f"lev{k}", [128, NB, size[k]]) for k in range(1, LEVELS)]
        sq = st.sb("sq", [128, 2, T])
        root = st.sb("root", [128, 2, T])
        rinv = st.sb("rinv", [128, 2, T])
        g = st.sb("g", [128, 2, T])
        xt = st.sb("xt", [128, 2, TILES, D])
        xo = st.sb("xo", [128, 2, TILES, D])
        psZ = [st.ps(f"psZ{i}") for i in range(2)]
        psM = [st.ps(f"psM{i}") for i in range(2)]
        psP = [st.ps(f"psP{i}") for i in range(2)]
        psY = [st.ps(f"psY{i}") for i in range(2)]

        combines = []

        def add(left, right, out, m, need):
            nb = min(NB, max(1, T // m))
            for b0 in range(0, NB, nb):
                combines.append((left[:, b0:b0 + nb], right[:, b0:b0 + nb], out[:, b0:b0 + nb], nb, m, need))

        for k in range(LEVELS):
            need = len(combines)
            m = size[k + 1]
            out = lev[k + 1][:] if k + 1 < LEVELS else res[:, :, 511:512]
            add(lev[k][:, :, 0:2 * m:2], lev[k][:, :, 1:2 * m:2], out, m, need)
        DOWN = len(combines)
        for k in range(LEVELS - 1, -1, -1):
            need = len(combines)
            m = 256 if k == 0 else size[k] // 2 - 1
            if m == 0:
                continue
            w = 1 << k
            l0, o0 = 2 * w - 1, 3 * w - 1
            add(res[:, :, l0:l0 + 2 * w * (m - 1) + 1:2 * w], lev[k][:, :, 2:2 * m + 1:2],
                res[:, :, o0:o0 + 2 * w * (m - 1) + 1:2 * w], m, need)
        CN = len(combines)

        const_in = st.sem("const_in")
        eps_set = st.sem("eps_set")
        x_in = [st.sem(f"x_in{s}") for s in range(2)]
        in_free = st.sem("in_free")
        q_ready = st.sem("q_ready")
        v_ready = st.sem("v_ready")
        q_copied = st.sem("q_copied")
        v_copied = st.sem("v_copied")
        first_set = st.sem("first_set")
        sums_ready = st.sem("sums_ready")
        squared = st.sem("squared")
        means_ready = st.sem("means_ready")
        rooted = st.sem("rooted")
        inverted = st.sem("inverted")
        combined = st.sem("combined")
        heads_copied = st.sem("heads_copied")
        gated = st.sem("gated")
        y_ready = st.sem("y_ready")
        res_in = [st.sem(f"res_in{s}") for s in range(2)]
        out_done = st.sem("out_done")
        out_free = st.sem("out_free")
        stored = [st.pool_dma_sem(64 * (NB // 2)) for s in range(2)]
        with nc.Block() as block:
            @block.sync
            def _(sp):
                sp.dma_start(wq[:], W["S_wq"]).then_inc(const_in, 16)
                sp.dma_start(wv[:], W["S_wv"]).then_inc(const_in, 16)
                sp.dma_start(wc[:], W["S_wc"]).then_inc(const_in, 16)
                sp.dma_start(first[:], W["S_first"]).then_inc(const_in, 16)
                sp.dma_start(mean[:], W["S_mean"]).then_inc(const_in, 16)
                for m in range(2):
                    sp.dma_start(pt[:, m], PT[m]).then_inc(const_in, 16)
                with sp.Fori(0, NB // 2) as i:
                    for s in range(2):
                        b = i * 2 + s
                        sp.wait_ge(in_free, b + 1)
                        sp.dma_start(xT[:, s], xnt[:, bass.ds(b * T, T)]).then_inc(x_in[s], 16)
                with sp.Fori(0, NB // 2) as i:
                    for s in range(2):
                        b = i * 2 + s
                        sp.wait_ge(out_free, b + 1)
                        load_tiles(sp, xt[:, s], X, b, False, res_in[s])

            @block.gpsimd
            def _(pool):
                pool.memset(eps[:], 1e-8).then_inc(eps_set, 1)
                with pool.Fori(0, NB // 2) as i:
                    for s in range(2):
                        b = i * 2 + s
                        pool.wait_ge(out_done, b + 1)
                        store_tiles(pool, X, xo[:, s], b, False, stored[s].sem)
                for s in range(2):
                    stored[s].wait(pool, 64 * (NB // 2))

            @block.tensor
            def _(pe):
                pe.sem_inc(in_free, 2)
                pe.sem_inc(q_copied, 1)
                pe.sem_inc(v_copied, 1)
                pe.wait_ge(const_in, 112)
                with pe.Fori(0, NB // 2) as i:
                    for s in range(2):
                        b = i * 2 + s
                        pe.wait_ge(x_in[s], i * 16 + 16)
                        pe.wait_ge(q_copied, b + 1)
                        pe.matmul(psP[0][:], wq[:], xT[:, s], start=True, stop=True).then_inc(q_ready, 1)
                        pe.wait_ge(v_copied, b + 1)
                        pe.matmul(psP[1][:], wv[:], xT[:, s], start=True, stop=True).then_inc(v_ready, 1)
                        pe.wait_ge(v_copied, b + 2)
                        pe.sem_inc(in_free, 1)
                pe.wait_ge(q_copied, NB + 1)
                pe.wait_ge(first_set, 1)

                def means(n):
                    _, _, _, nb, m, _ = combines[n]
                    pe.wait_ge(squared, n + 1)
                    if n >= 2:
                        pe.wait_ge(rooted, n - 1)
                    pe.matmul(psM[n % 2][:, 0:nb * m], mean[:], sq[:, n % 2, 0:nb * m], start=True,
                              stop=True).then_inc(means_ready, 1)

                for n, (left, right, _, nb, m, need) in enumerate(combines):
                    late = need > n - 1
                    if n and late:
                        means(n - 1)
                    ahead = max(need, n - 1)
                    if ahead:
                        pe.wait_ge(combined, ahead)
                    if n == DOWN:
                        pe.wait_ge(heads_copied, LEVELS - 1)
                    z = psZ[n % 2][:, 0:nb * m].rearrange("p (b m) -> p b m", b=nb)
                    pe.matmul(z, pt[:, 0], left, start=True, stop=False)
                    pe.matmul(z, pt[:, 1], right, start=False, stop=True).then_inc(sums_ready, 1)
                    if n and not late:
                        means(n - 1)
                means(CN - 1)
                with pe.Fori(0, NB // 2) as i:
                    for s in range(2):
                        b = i * 2 + s
                        pe.wait_ge(gated, b + 1)
                        pe.wait_ge(out_free, b + 1)
                        for k in range(TILES):
                            ins = pe.matmul(psY[s][:, k * D:(k + 1) * D], g[:, s, k * 128:(k + 1) * 128], wc[:],
                                            start=True, stop=True)
                        ins.then_inc(y_ready, 1)

            @block.scalar
            def _(a):
                a.wait_ge(eps_set, 1)
                with a.Fori(0, NB) as b:
                    a.wait_ge(q_ready, b + 1)
                    a.copy(seq[:, bass.ds(b, 1), 1:513], psP[0][:].unsqueeze(1)).then_inc(q_copied, 1)
                for n, (_, _, _, nb, m, _) in enumerate(combines):
                    c = nb * m
                    a.wait_ge(sums_ready, n + 1)
                    if n >= 2:
                        a.wait_ge(means_ready, n - 1)
                    a.activation(sq[:, n % 2, 0:c], psZ[n % 2][:, 0:c], ACT.Square).then_inc(squared, 1)
                    a.wait_ge(means_ready, n + 1)
                    if n >= 2:
                        a.wait_ge(inverted, n - 1)
                    a.activation(root[:, n % 2, 0:c], psM[n % 2][:, 0:c], ACT.Sqrt, bias=eps[:, 0:1]).then_inc(rooted, 1)

            @block.vector
            def _(v):
                v.sem_inc(out_free, 2)
                v.wait_ge(const_in, 112)
                v.tensor_copy(seq[:, :, 0:1], first[:].unsqueeze(1).to_broadcast([128, NB, 1])).then_inc(first_set, 1)
                with v.Fori(0, NB) as b:
                    v.wait_ge(v_ready, b + 1)
                    v.tensor_copy(val[:, bass.ds(b, 1), :], psP[1][:].unsqueeze(1)).then_inc(v_copied, 1)
                for n, (_, _, out, nb, m, _) in enumerate(combines):
                    c = nb * m
                    if n == DOWN:
                        v.wait_ge(combined, DOWN)
                        for k in range(1, LEVELS):
                            w = 1 << k
                            v.tensor_copy(res[:, :, w - 1:w], lev[k][:, :, 0:1]).then_inc(heads_copied, 1)
                    v.wait_ge(rooted, n + 1)
                    if n >= 2:
                        v.wait_ge(combined, n - 1)
                    v.reciprocal(rinv[:, n % 2, 0:c], root[:, n % 2, 0:c]).then_inc(inverted, 1)
                    v.wait_ge(inverted, n + 1)
                    v.tensor_tensor(out, psZ[n % 2][:, 0:c].rearrange("p (b m) -> p b m", b=nb),
                                    rinv[:, n % 2, 0:c].rearrange("p (b m) -> p b m", b=nb), ALU.mult).then_inc(combined, 1)
                v.wait_ge(combined, CN)
                with v.Fori(0, NB // 2) as i:
                    for s in range(2):
                        b = i * 2 + s
                        v.tensor_tensor(g[:, s].unsqueeze(1), res[:, bass.ds(b, 1), 1:513], val[:, bass.ds(b, 1), :],
                                        ALU.mult).then_inc(gated, 1)
                        v.wait_ge(y_ready, b + 1)
                        v.wait_ge(res_in[s], i * 64 + 64)
                        stored[s].wait(v, i * 64)
                        v.tensor_tensor(xo[:, s], psY[s][:].rearrange("p (k d) -> p k d", k=TILES), xt[:, s],
                                        ALU.add).then_inc(out_done, 1)
                        v.wait_ge(out_done, b + 1)
                        v.sem_inc(out_free, 1)


EX, FX, CAP = 64, 96, 64
ROWX = D + EX


def route64(nc, name, W, xnt, XW, X, SLOT):
    with Stage(nc, name) as st:
        ident = st.sb("ident", [128, 128])
        wr = st.sb("wr", [128, EX])
        wsg = st.sb("wsg", [128, 2 * FX])
        wsd = st.sb("wsd", [FX, D])
        ramp = st.sb("ramp", [EX, N])
        slot_no = st.sb("slot_no", [EX, CAP])
        xT = st.sb("xT", [128, 2, T])
        xt = st.sb("xt", [128, 2, TILES, D])
        xo = st.sb("xo", [128, 2, TILES, D])
        lg = st.sb("lg", [128, TILES, EX])
        mx = st.sb("mx", [128, TILES])
        ex = st.sb("ex", [128, TILES, EX])
        sm = st.sb("sm", [128, TILES])
        ri = st.sb("ri", [128, TILES])
        pr = st.sb("pr", [128, TILES, EX])
        left = st.sb("left", [128, TILES, EX])
        v8 = st.sb("v8", [128, TILES, 8])
        mk = st.sb("mk", [128, 2, TILES, EX])
        wt = st.sb("wt", [128, 2, TILES, EX])
        sg = st.sb("sg", [FX, T])
        h = st.sb("h", [FX, T])
        order = [st.sb(f"order{j}", [EX, N]) for j in range(2)]
        top = st.sb("top", [EX, CAP])
        none = st.sb("none", [EX, CAP])
        tok = st.sb("tok", [EX, CAP])
        toki = st.sb("toki", [EX, CAP], I32)
        psL = st.ps("psL")
        psM = st.ps("psM")
        psG = st.ps("psG")
        psU = st.ps("psU")
        psO = st.ps("psO")
        const_in = st.sem("const_in")
        x_in = [st.sem(f"x_in{s}") for s in range(2)]
        res_in = [st.sem(f"res_in{s}") for s in range(2)]
        in_free = st.sem("in_free")
        logits_ready = st.sem("logits_ready")
        shifted = st.sem("shifted")
        exps_done = st.sem("exps_done")
        chosen = st.sem("chosen")
        choice_turned = st.sem("choice_turned")
        choice_kept = st.sem("choice_kept")
        shared_ready = st.sem("shared_ready")
        silu_done = st.sem("silu_done")
        h_done = st.sem("h_done")
        shared_out = st.sem("shared_out")
        out_done = st.sem("out_done")
        stored = [st.pool_dma_sem(64 * (NB // 2)) for s in range(2)]
        w_stored = [st.pool_dma_sem(64 * (NB // 2)) for s in range(2)]
        dve = st.sem("dve")
        paced = st.sem("paced")
        slots_done = st.sem("slots_done")
        slots_stored = st.sem("slots_stored")
        with nc.Block() as block:
            @block.sync
            def _(sp):
                for dst, src in ((ident, "ident"), (wr, "L3_router"), (wsg, "L3_wsg"), (wsd, "L3_wsd"), (ramp, "L3_ramp")):
                    sp.dma_start(dst[:], W[src]).then_inc(const_in, 16)
                sp.dma_start(slot_no[:], W["iota8"][0:EX, 0:CAP]).then_inc(const_in, 16)
                sp.dma_start(X[N:N + CAP], W["zero_rows"][:, 0:D]).then_inc(const_in, 16)
                sp.dma_start(XW[N:N + CAP], W["zero_rows"]).then_inc(const_in, 16)
                with sp.Fori(0, NB // 2) as i:
                    for s in range(2):
                        b = i * 2 + s
                        sp.wait_ge(in_free, b + 1)
                        sp.dma_start(xT[:, s], xnt[:, bass.ds(b * T, T)]).then_inc(x_in[s], 16)
                        load_tiles(sp, xt[:, s], X[0:N], b, False, res_in[s])
                sp.wait_ge(slots_done, 1)
                sp.dma_start(SLOT, toki[:]).then_inc(slots_stored, 16)
                sp.wait_ge(slots_stored, 16)
                sp.wait_ge(const_in, 128)

            @block.gpsimd
            def _(pool):
                wide = XW[0:N, D:ROWX].rearrange("(g p) c -> g p c", p=128)
                with pool.Fori(0, NB // 2) as i:
                    for s in range(2):
                        b = i * 2 + s
                        pool.wait_ge(chosen, b + 1)
                        for k in range(TILES):
                            pool.dma_start(wide[bass.ds(b * TILES + k, 1)].rearrange("o p c -> (o p) c"),
                                           wt[:, s, k]).then_inc(w_stored[s].sem, 16)
                        pool.wait_ge(out_done, b + 1 + 1)
                        store_tiles(pool, X[0:N], xo[:, s], b, False, stored[s].sem)
                for s in range(2):
                    stored[s].wait(pool, 64 * (NB // 2))
                    w_stored[s].wait(pool, 64 * (NB // 2))

            @block.tensor
            def _(pe):
                pe.wait_ge(const_in, 128)
                with pe.Fori(0, NB // 2) as i:
                    for s in range(2):
                        b = i * 2 + s
                        pe.wait_ge(x_in[s], i * 16 + 16)
                        pe.wait_ge(out_done, b + 1)
                        for k in range(TILES):
                            ins = pe.matmul(psL[:, k * EX:(k + 1) * EX], xT[:, s, k * 128:(k + 1) * 128], wr[:], start=True,
                                            stop=True)
                        ins.then_inc(logits_ready, 1)
                        pe.matmul(psG[0:FX], wsg[:, 0:FX], xT[:, s], start=True, stop=True)
                        pe.matmul(psU[0:FX], wsg[:, FX:2 * FX], xT[:, s], start=True, stop=True).then_inc(shared_ready, 1)
                        pe.wait_ge(h_done, b + 1)
                        for k in range(TILES):
                            ins = pe.matmul(psO[:, k * D:(k + 1) * D], h[:, k * 128:(k + 1) * 128], wsd[:], start=True,
                                            stop=True)
                        ins.then_inc(shared_out, 1)
                        pe.wait_ge(chosen, b + 1)
                        pe.sem_inc(paced, 1)
                        for k in range(TILES):
                            ins = pe.transpose(psM[0:EX, k * 128:(k + 1) * 128], mk[:, s, k], ident[:])
                        ins.then_inc(choice_turned, 1)

            @block.scalar
            def _(a):
                with a.Fori(0, NB // 2) as i:
                    for s in range(2):
                        b = i * 2 + s
                        a.wait_ge(shifted, b + 1)
                        a.activation(ex[:], lg[:], ACT.Exp).then_inc(exps_done, 1)
                        a.wait_ge(shared_ready, b + 1)
                        a.activation(sg[:], psG[0:FX], ACT.Silu).then_inc(silu_done, 1)

            @block.vector
            def _(v):
                v.sem_inc(in_free, 2)
                v.sem_inc(out_done, 1)
                v.sem_inc(choice_turned, 1)
                v.wait_ge(const_in, 128)
                with v.Fori(0, NB // 2) as i:
                    STEPS = [0]
                    PER = 2 * 9

                    def link(ins):
                        STEPS[0] += 1
                        ins.then_inc(dve, 1)
                        v.wait_ge(dve, i * PER + STEPS[0])
                        v.sem_inc(paced, 1)

                    for s in range(2):
                        b = i * 2 + s
                        v.wait_ge(logits_ready, b + 1)
                        L = psL[:, 0:TILES * EX].rearrange("p (k e) -> p k e", k=TILES)
                        link(v.tensor_reduce(mx[:], L, AX.X, ALU.max))
                        v.tensor_tensor(lg[:], L, bc(mx[:], EX), ALU.subtract).then_inc(shifted, 1)
                        v.wait_ge(exps_done, b + 1)
                        link(v.tensor_reduce(sm[:], ex[:], AX.X, ALU.add))
                        link(v.reciprocal(ri[:], sm[:]))
                        link(v.tensor_tensor(pr[:], ex[:], bc(ri[:], EX), ALU.mult))
                        for k in range(TILES):
                            ins = v.max(v8[:, k], pr[:, k])
                        link(ins)
                        for k in range(TILES):
                            ins = v.match_replace(left[:, k], v8[:, k], pr[:, k], -1.0)
                        v.tensor_reduce(sm[:], v8[:], AX.X, ALU.add)
                        link(ins)
                        v.wait_ge(choice_turned, b + 1)
                        w_stored[s].wait(v, i * 64)
                        link(v.tensor_scalar(mk[:, s], left[:], 0.0, None, ALU.is_lt))
                        link(v.reciprocal(ri[:], sm[:]))
                        link(v.tensor_tensor(left[:], pr[:], mk[:, s], ALU.mult))
                        v.tensor_tensor(wt[:, s], left[:], bc(ri[:], EX), ALU.mult).then_inc(chosen, 1)
                        v.wait_ge(silu_done, b + 1)
                        v.tensor_tensor(h[:], sg[:], psU[0:FX], ALU.mult).then_inc(h_done, 1)
                        v.wait_ge(choice_turned, b + 1 + 1)
                        v.tensor_tensor(order[0][:, bass.ds(b * T, T)], psM[0:EX], ramp[:, bass.ds(b * T, T)],
                                        ALU.mult).then_inc(choice_kept, 1)
                        v.wait_ge(shared_out, b + 1)
                        v.wait_ge(res_in[s], i * 64 + 64)
                        stored[s].wait(v, i * 64)
                        v.scalar_tensor_tensor(out=xo[:, s], in0=psO[:].rearrange("p (k d) -> p k d", k=TILES), scalar=0.5,
                                               in1=xt[:, s], op0=ALU.mult, op1=ALU.add).then_inc(out_done, 1)
                        v.wait_ge(out_done, b + 1 + 1)
                        v.wait_ge(choice_kept, b + 1)
                        v.sem_inc(in_free, 1)
                assert STEPS[0] == PER, (STEPS[0], PER)
                done = PER * (NB // 2)
                for c in range(CAP // 8):
                    part = top[:, 8 * c:8 * c + 8]
                    v.max(part, order[c % 2][:]).then_inc(dve, 1)
                    v.wait_ge(dve, done + 2 * c + 1)
                    v.match_replace(order[1 - c % 2][:], part, order[c % 2][:], 0.0).then_inc(dve, 1)
                    v.wait_ge(dve, done + 2 * c + 2)
                done += 2 * (CAP // 8)
                v.tensor_scalar(none[:], top[:], 0.0, None, ALU.is_equal).then_inc(dve, 1)
                v.wait_ge(dve, done + 1)
                v.tensor_tensor(none[:], none[:], slot_no[:], ALU.mult).then_inc(dve, 1)
                v.wait_ge(dve, done + 2)
                v.tensor_tensor(tok[:], none[:], top[:], ALU.subtract).then_inc(dve, 1)
                v.wait_ge(dve, done + 3)
                v.tensor_scalar(toki[:], tok[:], float(N), None, ALU.add).then_inc(slots_done, 1)


def experts64(nc, name, W, XW, X, SLOT):
    with Stage(nc, name) as st:
        ident = st.sb("ident", [128, 128])
        idx = st.sb("idx", [CAP, 4, 1], I32)
        xg = st.sb("xg", [CAP, 4, ROWX])
        xgT = st.sb("xgT", [128, 2, CAP])
        wgu = st.sb("wgu", [128, 4, 2, FX])
        wd = st.sb("wd", [FX, 4, D])
        wv = st.sb("wv", [CAP, 2])
        sg = st.sb("sg", [FX, 2, CAP])
        h = st.sb("h", [FX, 2, CAP])
        y = st.sb("y", [CAP, 4, D])
        psT = [st.ps(f"psT{s}") for s in range(2)]
        psH = [st.ps(f"psH{s}") for s in range(2)]
        psY = [st.ps(f"psY{s}") for s in range(2)]
        const_in = st.sem("const_in")
        idx_in = [st.sem(f"idx_in{s}") for s in range(4)]
        w_in = [st.sem(f"w_in{s}") for s in range(4)]
        gathered = [st.pool_dma_sem(16 * EX // 2) for s in range(2)]
        turned = st.sem("turned")
        turned_copied = st.sem("turned_copied")
        up_done = st.sem("up_done")
        silu_done = st.sem("silu_done")
        h_done = st.sem("h_done")
        down_done = st.sem("down_done")
        picked = st.sem("picked")
        y_done = st.sem("y_done")
        added = st.pool_dma_sem(16 * EX)
        earlier_added = st.sem("earlier_added")
        paced = st.sem("paced")
        with nc.Block() as block:
            @block.sync
            def _(sp):
                sp.dma_start(ident[:], W["ident"]).then_inc(const_in, 16)
                with sp.Fori(0, EX // 4) as i:
                    for s in range(4):
                        e = i * 4 + s
                        sp.wait_ge(earlier_added, e + 1)
                        sp.dma_start(idx[:, s], SLOT[bass.ds(e, 1)].rearrange("o c -> c o")).then_inc(idx_in[s], 16)
                        sp.wait_ge(down_done, e + 1)
                        sp.dma_start(wgu[:, s], W["L3_wgu"][:, bass.ds(e, 1)].rearrange("p o a f -> p (o a) f")).then_inc(w_in[s], 16)
                        sp.dma_start(wd[:, s], W["L3_wd"][bass.ds(e, 1)].rearrange("o f d -> (o f) d")).then_inc(w_in[s], 16)

            @block.gpsimd
            def _(pool):
                def gather(k, n):
                    pool.wait_ge(idx_in[k], n * 16 + 16)
                    pool.wait_ge(turned, n * 4 + k + 3)
                    pool.wait_ge(picked, n * 4 + k + 1)
                    pool.sem_inc(paced, 1)
                    pool.indirect_dma_start(out=xg[:, k], out_offset=None, in_=XW,
                                            in_offset=bass.IndirectOffsetOnAxis(ap=idx[:, k], axis=0)
                                            ).then_inc(gathered[k % 2].sem, 16)

                def add(k, e):
                    pool.wait_ge(y_done, e + 1)
                    added.wait(pool, e * 16)
                    pool.sem_inc(earlier_added, 1)
                    pool.indirect_dma_start(out=X, out_offset=bass.IndirectOffsetOnAxis(ap=idx[:, k], axis=0),
                                            in_=y[:, k], in_offset=None, compute_op=ALU.add).then_inc(added.sem, 16)

                pool.sem_inc(earlier_added, 3)
                gather(0, 0)
                gather(1, 0)
                with pool.Fori(0, EX // 4 - 1) as i:
                    for s in range(4):
                        gather((s + 2) % 4, i + (s + 2) // 4)
                        add(s, i * 4 + s)
                for s in range(4):
                    if s < 2:
                        gather(s + 2, EX // 4 - 1)
                    add(s, EX - 4 + s)
                added.wait(pool, EX * 16)

            @block.tensor
            def _(pe):
                pe.wait_ge(const_in, 16)
                with pe.Fori(0, EX // 4) as i:
                    for s in range(4):
                        e = i * 4 + s
                        q = s % 2
                        gathered[q].wait(pe, (i * 2 + s // 2) * 16 + 16)
                        pe.sem_inc(paced, 1)
                        pe.transpose(psT[q][:, 0:CAP], xg[:, s, 0:D], ident[0:CAP, 0:CAP]).then_inc(turned, 1)
                        pe.wait_ge(turned_copied, e + 1)
                        pe.wait_ge(w_in[s], i * 32 + 32)
                        pe.matmul(psH[q][0:FX, 0:CAP], wgu[:, s, 0], xgT[:, q], start=True, stop=True)
                        pe.matmul(psH[q][0:FX, CAP:2 * CAP], wgu[:, s, 1], xgT[:, q], start=True, stop=True).then_inc(up_done, 1)
                        pe.wait_ge(h_done, e + 1)
                        pe.matmul(psY[q][0:CAP, 0:D], h[:, q], wd[:, s], start=True, stop=True).then_inc(down_done, 1)

            @block.scalar
            def _(a):
                with a.Fori(0, EX // 4) as i:
                    for s in range(4):
                        e = i * 4 + s
                        a.wait_ge(up_done, e + 1)
                        a.activation(sg[:, s % 2], psH[s % 2][0:FX, 0:CAP], ACT.Silu).then_inc(silu_done, 1)

            @block.vector
            def _(v):
                v.sem_inc(down_done, 4)
                v.sem_inc(turned, 4)
                v.sem_inc(picked, 4)
                with v.Fori(0, EX // 4) as i:
                    for s in range(4):
                        e = i * 4 + s
                        q = s % 2
                        v.wait_ge(turned, e + 1 + 4)
                        v.tensor_copy(xgT[:, q], psT[q][:, 0:CAP]).then_inc(turned_copied, 1)
                        v.tensor_copy(wv[:, q:q + 1], xg[:, s, bass.ds(e + D, 1)]).then_inc(picked, 1)
                        v.wait_ge(silu_done, e + 1)
                        v.tensor_tensor(h[:, q], sg[:, q], psH[q][0:FX, CAP:2 * CAP], ALU.mult).then_inc(h_done, 1)
                        v.wait_ge(down_done, e + 1 + 4)
                        v.wait_ge(picked, e + 1 + 4)
                        v.wait_ge(earlier_added, e + 1)
                        v.tensor_scalar(y[:, s], psY[q][0:CAP, 0:D], wv[:, q:q + 1], 0.5, ALU.mult,
                                        ALU.mult).then_inc(y_done, 1)


RW = 511


def skewed(row, base, n):
    full = row.rearrange("o n -> (o n)")
    sub = full[base:base + 128 * (RW - 1)].rearrange("(p w) -> p w", w=RW - 1)
    return sub[:, 0:n]


def relative(nc, name, W, xnt, PR):
    U = TILES * HEADS

    def offsets(it):
        return {0: (127, 384), TILES - 1: (0, 384)}.get(it, (0, RW + 1))

    with Stage(nc, name) as st:
        wq = st.sb("wq", [128, 4, 128])
        bq = st.sb("bq", [128, 4])
        wrel = st.sb("wrel", [128, 4, RW + 1])
        xT = st.sb("xT", [128, 2, T])
        q = st.sb("q", [128, 4, T])
        rp = st.sb("rp", [128, 4, RW])
        psP = [st.ps(f"psP{i}") for i in range(2)]
        psR = [st.ps(f"psR{i}") for i in range(4)]
        const_in = st.sem("const_in")
        x_in = [st.sem(f"x_in{s}") for s in range(2)]
        in_free = st.sem("in_free")
        proj_done = st.sem("proj_done")
        q_copied = st.sem("q_copied")
        rel_ready = st.sem("rel_ready")
        rel_copied = st.sem("rel_copied")
        rel_stored = [st.sem(f"rel_stored{j}") for j in range(4)]
        with nc.Block() as block:
            @block.sync
            def _(sp):
                sp.dma_start(wq[:].rearrange("p a b -> p (a b)"), W["A0_wq"]).then_inc(const_in, 16)
                sp.dma_start(bq[:], W["A0_bq"]).then_inc(const_in, 16)
                sp.dma_start(wrel[:], W["A0_wrel"].rearrange("p (g w) -> p g w", g=4)).then_inc(const_in, 16)
                with sp.Fori(0, NB // 2) as i:
                    for s in range(2):
                        b = i * 2 + s
                        sp.wait_ge(in_free, b + 1)
                        sp.dma_start(xT[:, s], xnt[:, bass.ds(b * T, T)]).then_inc(x_in[s], 16)
                        for u in range(U):
                            sp.wait_ge(rel_copied, b * U + u + 1 + 1)
                            dst = PR[bass.ds(b * U + u, 1), 0:128 * RW].rearrange("o (p w) -> (o p) w", w=RW)
                            lo, n = offsets(u // HEADS)
                            n = min(n, RW)
                            sp.dma_start(dst[:, lo:lo + n], rp[:, u % 4, 0:n]).then_inc(rel_stored[u % 4], 16)
                for j in range(4):
                    sp.wait_ge(rel_stored[j], NB * U // 4 * 16 + 16)

            @block.tensor
            def _(pe):
                pe.sem_inc(in_free, 2)
                pe.wait_ge(const_in, 48)
                with pe.Fori(0, NB // 2) as i:
                    for s in range(2):
                        b = i * 2 + s
                        pe.wait_ge(x_in[s], i * 16 + 16)
                        for m in range(4):
                            if m >= 2:
                                pe.wait_ge(q_copied, b * 4 + m - 1)
                            ins = pe.matmul(psP[m % 2][:], wq[:, m], xT[:, s], start=True, stop=True)
                            ins.then_inc(proj_done, 1)
                        pe.wait_ge(q_copied, b * 4 + 4)
                        pe.sem_inc(in_free, 1)
                        for u in range(U):
                            it, h = divmod(u, HEADS)
                            m, g = divmod(h, 4)
                            if u >= 4:
                                pe.wait_ge(rel_copied, b * U + u - 3 + 1)
                            else:
                                pe.wait_ge(rel_copied, b * U + 1)
                            lo, n = offsets(it)
                            pe.matmul(psR[u % 4][:, 0:n], q[:, m, it * 128:(it + 1) * 128], wrel[:, g, lo:lo + n],
                                      start=True, stop=True).then_inc(rel_ready, 1)

            @block.vector
            def _(v):
                v.wait_ge(const_in, 48)
                with v.Fori(0, NB // 2) as i:
                    for s in range(2):
                        b = i * 2 + s
                        for m in range(4):
                            v.wait_ge(proj_done, b * 4 + m + 1)
                            v.tensor_scalar(q[:, m], psP[m % 2][:], bq[:, m:m + 1], None, ALU.add).then_inc(q_copied, 1)

            @block.scalar
            def _(a):
                a.sem_inc(rel_copied, 1)
                for j in range(4):
                    a.sem_inc(rel_stored[j], 16)
                with a.Fori(0, NB // 2) as i:
                    for s in range(2):
                        b = i * 2 + s
                        for u in range(U):
                            a.wait_ge(rel_ready, b * U + u + 1)
                            if u >= 4:
                                a.wait_ge(rel_stored[u % 4], (b * (U // 4) + u // 4) * 16 + 16)
                            else:
                                a.wait_ge(rel_stored[u % 4], b * (U // 4) * 16 + 16)
                            n = min(offsets(u // HEADS)[1], RW)
                            a.activation(rp[:, u % 4, 0:n], psR[u % 4][:, 0:n], ACT.Copy, scale=-1.0).then_inc(rel_copied, 1)


NCON = {"L0": 4, "L1": 7, "L2": 3}


def name_of(kind, what):
    return f"{kind}_{what}"


def stage_L0_ffn(nc, W, X, S):
    prep(nc, "p0", W, X, S["XNT"], route=dict(ROUTES["L0"], w="L0_router", b="L0_router_b", table=S["GT"]))
    moe(nc, "m0", W, "L0", X, S["XNT"], S["GT"])


def stage_L1_ffn(nc, W, X, S):
    prep(nc, "p1", W, X, S["XNT"], xn=S["XN"], permuted=True)
    attention(nc, "a1", W, "block", S["XNT"], S, S["XN"], S["Y"])
    prep(nc, "q1", W, S["Y"], S["XNT"], xn=S["H"], affine=("L1_ln1_g", "L1_ln1_b"),
         route=dict(ROUTES["L1"], w="L1_router", b="L1_router_b", table=S["GT"]))
    moe(nc, "m1", W, "L1", X, S["XNT"], S["GT"], hn=S["H"], permuted=True)


def stage_L2_ffn(nc, W, X, S):
    prep(nc, "p2", W, X, S["XNT"], route=dict(ROUTES["L2"], w="L2_router", b="L2_router_b", table=S["GT"]))
    moe(nc, "m2", W, "L2", X, S["XNT"], S["GT"])


def stage_L0_attn(nc, W, X, S):
    prep(nc, "p4", W, X, S["XNT"])
    relative(nc, "r0", W, S["XNT"], S["PR"])
    attention(nc, "a0", W, "rel", S["XNT"], S, X, X)


def stage_L1_attn(nc, W, X, S):
    prep(nc, "p3", W, X, S["XNT"])
    attention(nc, "a2", W, "causal", S["XNT"], S, X, X)


def stage_L2_attn(nc, W, X, S):
    polar(nc, "po", W, S["PT"])
    prep(nc, "p6", W, X, S["XNT"])
    scan_attention(nc, "sc", W, S["XNT"], X, S["PT"])


def stage_L3_attn(nc, W, X, S):
    prep(nc, "p5", W, X, S["XNT"])
    attention(nc, "a3", W, "plain", S["XNT"], S, X, X)


def stage_L3_ffn(nc, W, X, S):
    prep(nc, "p7", W, X, S["XNT"], xn=S["XW"][0:N, 0:D])
    route64(nc, "r3", W, S["XNT"], S["XW"], S["Xfull"], S["SLOT"])
    experts64(nc, "e3", W, S["XW"], S["Xfull"], S["SLOT"])


STAGES = [stage_L0_ffn, stage_L0_attn, stage_L0_ffn, stage_L1_ffn, stage_L1_attn, stage_L1_ffn,
          stage_L2_ffn, stage_L2_attn, stage_L2_ffn, stage_L3_ffn, stage_L3_attn, stage_L3_ffn]


def copy_dram(nc, name, dst, src, n):
    with Stage(nc, name) as st:
        done = st.sem("done")
        with nc.Block() as block:
            @block.sync
            def _(sp):
                sp.dma_start(dst, src).then_inc(done, 16)
                sp.wait_ge(done, 16)


def copy_in(nc, X, x):
    part = N // 4
    with Stage(nc, "cin") as st:
        with nc.Block() as block:
            @block.gpsimd
            def _(pool):
                for j in range(4):
                    pool.dma_start(X[j * part:(j + 1) * part], x[j * part:(j + 1) * part]).then_inc(Stage.pool_dma[j], 16)
                for j in range(4):
                    pool.wait_ge(Stage.pool_dma[j], 16)


def program(nc, W, out, stages):
    full = nc.dram_tensor("X", [N + CAP, D], F32).ap()
    X = full[0:N]
    S = {
        "Xfull": full,
        "XW": nc.dram_tensor("XW", [N + CAP, ROWX], F32).ap(),
        "SLOT": nc.dram_tensor("SLOT", [EX, CAP], I32).ap(),
        "PT": nc.dram_tensor("PT", [2, 128, 128], F32).ap(),
        "XNT": nc.dram_tensor("XNT", [D, N], F32).ap(),
        "XN": nc.dram_tensor("XN", [N, D], F32).ap(),
        "H": nc.dram_tensor("H", [N, D], F32).ap(),
        "Y": nc.dram_tensor("Y", [N, D], F32).ap(),
        "PR": nc.dram_tensor("PR", [NB * TILES * HEADS, 128 * RW + 128], F32).ap(),
        "GT": nc.dram_tensor("GT", [27, N], F32).ap(),
    }
    with ExitStack() as ctx:
        Stage.count = 0
        Stage.pool_dma_count = [16] * 4
        Stage.pool_dma = [ctx.enter_context(nc.semaphore(f"pool_dma{j}")) for j in range(4)]
        copy_in(nc, X, W["x"])
        for stage in stages:
            stage(nc, W, X, S)
        copy_dram(nc, "cout", out, X, N)


def layout(inputs):
    f = np.float32
    I = {k: np.asarray(v) for k, v in inputs.items()}
    w = {"x": I["L0_attn_x"].reshape(N, D)}
    w["ident"] = np.eye(128, dtype=f)
    w["iota8"] = np.ascontiguousarray(np.broadcast_to(np.arange(64, dtype=f), (128, 64)))
    w["L0_router"] = np.concatenate([I["L0_ffn_gate_w"], I["L0_ffn_shared_expert_gate_w"]]).T
    w["L0_router_b"] = np.zeros((1, 9), f)
    gu = I["L0_ffn_experts_gate_up"]
    w["L0_w1"] = np.concatenate([gu[:, :176].reshape(1408, D), I["L0_ffn_shared_gate_w"]]).T
    w["L0_wu"] = np.concatenate([gu[:, 176:].reshape(1408, D), I["L0_ffn_shared_up_w"]]).T
    w["L0_w2"] = np.concatenate([I["L0_ffn_experts_down"].transpose(0, 2, 1).reshape(1408, D),
                                 I["L0_ffn_shared_down_w"].T, np.zeros((32, D), f)])
    sel = np.zeros((27, 14 * 128), f)
    for r in range(1760):
        e = min(r // 176, 8)
        sel[[e, 9 + e, 18 + e], r] = 1
    w["L0_sel"] = sel
    w["L1_router"] = I["L1_ffn_router_w"].T
    w["L1_router_b"] = I["L1_ffn_router_b"].reshape(1, 8)
    w["L1_w1"] = I["L1_ffn_w1"].transpose(2, 0, 1).reshape(D, 1024)
    w["L1_w2"] = I["L1_ffn_w2"].transpose(0, 2, 1).reshape(1024, D)
    w["L1_b1"] = I["L1_ffn_b1"].T
    w["L1_b2"] = I["L1_ffn_b2"]
    w["L1_sel"] = np.repeat(np.eye(8, dtype=f), 128, 1)
    for k in ("ln1_g", "ln1_b", "ln2_g", "ln2_b"):
        w[f"L1_{k}"] = I[f"L1_ffn_{k}"].reshape(1, D)
    w["L2_router"] = I["L2_ffn_router_w"].T
    w["L2_router_b"] = np.zeros((1, 8), f)
    w["L2_w1"] = I["L2_ffn_expert_fc"].transpose(1, 0, 2).reshape(D, 4096)
    w["L2_w2"] = I["L2_ffn_expert_proj"].transpose(0, 2, 1).reshape(4096, D)
    w["L2_sel"] = w["L1_sel"]
    p1, p2 = I["L2_attn_Wp1"], I["L2_attn_Wp2"]
    w["P_w"] = np.stack([p1, p1.T, p2, p2.T])
    w["S_wq"], w["S_wv"], w["S_wc"] = I["L2_attn_Wq"].T, I["L2_attn_Wv"].T, I["L2_attn_Wc"].T
    w["S_first"] = I["L2_attn_identity"].reshape(D, 1)
    w["S_mean"] = np.full((D, D), 1 / D, f)
    w["L3_router"] = I["L3_ffn_router_w"].T
    w["L3_wsg"], w["L3_wsd"] = I["L3_ffn_ws_gate_up"], I["L3_ffn_ws_down"]
    w["L3_ramp"] = np.broadcast_to(N - np.arange(N, dtype=f), (EX, N))
    w["L3_wgu"] = np.stack([I["L3_ffn_w_gate"], I["L3_ffn_w_up"]], 2).transpose(1, 0, 2, 3)
    w["L3_wd"] = I["L3_ffn_w_down"]
    w["zero_rows"] = np.zeros((CAP, ROWX), f)

    def heads4(rows, cols=None):
        o = np.zeros((D, 4, 128), f)
        for hh in range(HEADS):
            m, g = divmod(hh, 4)
            o[:, m, 32 * g:32 * g + HD] = rows[hh].T
        return o.reshape(D, 512)

    def bias4(rows, one=0.0):
        o = np.zeros((128, 4), f)
        for hh in range(HEADS):
            m, g = divmod(hh, 4)
            o[32 * g:32 * g + HD, m] = rows[hh]
            o[32 * g + HD, m] = one
        return o

    def slots4(w4):
        o = w4.copy()
        for slot in range(1, 4):
            o += np.roll(w4, HD * slot, axis=-1 if w4.shape[1] == 512 else 0)
        return o

    slots = np.zeros((128, 5), f)
    for g in range(4):
        for c, row in enumerate(((0, -1, -1, 0), (0, 0, -1, 0), (0, 0, 0, -1), (-1, 1, 0, 0), (1, 0, 0, 0))):
            for slot in range(4):
                slots[32 * g + HD * slot:32 * g + HD * slot + HD, c] = row[slot]
    w["slots"] = slots
    zero = np.zeros((HEADS, HD), f)
    a0 = I["L0_attn_Wqkv"].reshape(HEADS, 3, HD, D)
    b0 = I["L0_attn_bqkv"].reshape(HEADS, 3, HD)
    w["A0_wq"], w["A0_wk"] = heads4(a0[:, 0]), heads4(a0[:, 1])
    w["A0_bq"], w["A0_bk"] = bias4(b0[:, 0], 1.0), bias4(b0[:, 1])
    w["A0_wv"], w["A0_bv"] = a0[:, 2].reshape(128, D).T, b0[:, 2].reshape(1, 128)
    rel = np.concatenate([I["L0_attn_Wr"], I["L0_attn_br"][:, None]], 1)
    far = np.zeros((128, 2), f)
    wrel = np.zeros((128, 4, 512), f)
    span = np.clip(np.arange(-255, 256), -128, 128) + 128
    for g in range(4):
        far[32 * g:32 * g + 9, 0], far[32 * g:32 * g + 9, 1] = rel[0], rel[256]
        wrel[32 * g:32 * g + 9, g, 0:511] = rel[span].T
    w["A0_far"], w["A0_wrel"] = far, wrel.reshape(128, 2048)
    a1 = I["L1_ffn_in_proj_w"].reshape(3, HEADS, HD, D)
    b1 = I["L1_ffn_in_proj_b"].reshape(3, HEADS, HD)
    w["A1_wq"], w["A1_wk"] = heads4(a1[0]), heads4(a1[1])
    w["A1_bq"], w["A1_bk"] = bias4(b1[0]), bias4(b1[1])
    w["A1_wv"], w["A1_bv"] = a1[2].reshape(128, D).T, b1[2].reshape(1, 128)
    w["A1_wo"], w["A1_bo"] = I["L1_ffn_out_w"].T, I["L1_ffn_out_b"].reshape(1, D)
    token = np.arange(128)
    apart = (token[:, None] % 16 != token[None] % 16)
    w["A1_mask"] = np.tile(np.where(apart, f(BIG), f(0)), (1, 4)).astype(f)
    w["A2_wq"] = heads4(I["L1_attn_Wq"].T.reshape(HEADS, HD, D))
    w["A2_wk"] = heads4(I["L1_attn_Wk"].T.reshape(HEADS, HD, D))
    w["A2_bq"] = w["A2_bk"] = bias4(zero)
    w["A2_wv"], w["A2_wo"] = I["L1_attn_Wv"], I["L1_attn_Wo"]
    w["A2_mask"] = np.concatenate([np.zeros((128, 384), f), np.where(token[None] > token[:, None], f(BIG), f(0))], 1)
    w["A3_wq"], w["A3_wk"] = heads4(I["L3_attn_Wq"]), heads4(I["L3_attn_Wk"])
    w["A3_bq"], w["A3_bk"] = bias4(I["L3_attn_bq"]), bias4(I["L3_attn_bk"])
    w["A3_wv"], w["A3_bv"] = I["L3_attn_Wv"].reshape(128, D).T, I["L3_attn_bv"].reshape(1, 128)
    for key in ("A2", "A3"):
        for part in ("wq", "wk", "bq", "bk"):
            w[f"{key}_{part}"] = slots4(w[f"{key}_{part}"])
    w["A3_wo"], w["A3_bo"] = I["L3_attn_Wo"].T, I["L3_attn_bo"].reshape(1, D)
    return {k: np.ascontiguousarray(v) for k, v in w.items()}


def kernel(**inputs):
    import concourse.bacc as _bacc
    from concourse.bass_utils import run_bass_kernel_spmd as _run

    nc = _bacc.Bacc("TRN2", target_bir_lowering=False, num_devices=1)
    arrays, W = {}, {}
    for name, a in layout(inputs).items():
        arrays[f"in_{name}_dram"] = a
        W[name] = nc.dram_tensor(f"in_{name}_dram", a.shape, mybir.dt.from_np(a.dtype), kind="ExternalInput").ap()
    out = nc.dram_tensor("out_0_dram", [N, D], F32, kind="ExternalOutput").ap()
    program(nc, W, out, STAGES)
    r = _run(nc, [arrays], core_ids=[0])
    return r.results[0]["out_0_dram"].reshape(NB, T, D)
```
